# Optimizing a Trainium2 kernel written in Bass

```python
import numpy as np
import jax
import jax.numpy as jnp

def _softmax(x, axis=-1):
    return jax.nn.softmax(x, axis=axis)

def _gelu(x):
    return jax.nn.gelu(x, approximate=True)

def _silu(x):
    return jax.nn.silu(x)

def _sigmoid(x):
    return jax.nn.sigmoid(x)

def _layernorm(x, axis=-1, eps=1e-05):
    m = jnp.mean(x, axis=axis, keepdims=True)
    v = jnp.var(x, axis=axis, keepdims=True)
    return (x - m) / jnp.sqrt(v + eps)

def _scatter_add(tgt, idx, src, axis=0):
    return tgt.at[idx].add(src)

def _segment_sum(src, seg, n):
    return jax.ops.segment_sum(src, seg, n)
kernel_name = 'mk_xattn_ffn_d1_seqx_r4_38bf6c'

def setup_inputs(seed: int=0):
    np.random.seed(seed)
    _w = jnp.asarray

    def _rec_inputs():
        import jax
        import jax.numpy as jnp
        _rk = jax.random.key(seed)
        x = -0.0002928 + 1 * jax.random.normal(jax.random.fold_in(_rk, 1), (4, 1024, 256), jnp.float32)
        _lenS = 1024 - jax.random.randint(jax.random.fold_in(_rk, 7), (4,), 0, max(1, 1024 // 4) + 1, jnp.int32)
        _lenS2 = 154 - jax.random.randint(jax.random.fold_in(_rk, 8), (4,), 0, max(1, 154 // 4) + 1, jnp.int32)
        _ctx_1024P = jax.random.normal(jax.random.fold_in(_rk, 11), (4, 16, 256), jnp.float32)
        _ctx_1024c = jax.random.dirichlet(jax.random.fold_in(_rk, 511), 0.3 * jnp.ones((16,), jnp.float32), (4, 154))
        _ctx_1024t = jnp.einsum('bsk,bkd->bsd', _ctx_1024c, _ctx_1024P)
        _ctx_1024t = _ctx_1024t * jax.lax.rsqrt(jnp.mean(jnp.square(_ctx_1024t)) + 1e-12) * 0.953939
        ctx_1024 = -1.39393e-06 + 0.999914 * (_ctx_1024t + 0.3 * jax.random.normal(jax.random.fold_in(_rk, 611), (4, 154, 256), jnp.float32))
        return (x, ctx_1024)
    x, ctx_1024 = _rec_inputs()

    def _L0_xattn_setup():
        import jax, jax.numpy as jnp
        import numpy as np
        NUM_HEADS = 16
        D_MODEL = 256
        HEAD_DIM = D_MODEL // NUM_HEADS
        SCALE = 8.0 / HEAD_DIM
        LN_EPS = 1e-05

        def _layernorm(x, g, b):
            mu = jnp.mean(x, axis=-1, keepdims=True)
            var = jnp.mean(jnp.square(x - mu), axis=-1, keepdims=True)
            return (x - mu) * jax.lax.rsqrt(var + LN_EPS) * g + b
        key = jax.random.key(seed)
        ks = jax.random.split(key, 8)
        B, N, M = (2, 512, 512)
        std = 1.0 / np.sqrt(D_MODEL)
        return {'x1': jax.random.normal(ks[0], (B, N, D_MODEL), jnp.float32), 'x2': jax.random.normal(ks[1], (B, M, D_MODEL), jnp.float32), 'Wq': jax.random.normal(ks[2], (D_MODEL, D_MODEL), jnp.float32) * std, 'Wk': jax.random.normal(ks[3], (D_MODEL, D_MODEL), jnp.float32) * std, 'Wv': jax.random.normal(ks[4], (D_MODEL, D_MODEL), jnp.float32) * std, 'Wp': jax.random.normal(ks[5], (D_MODEL, D_MODEL), jnp.float32) * std, 'bp': jnp.zeros((D_MODEL,), jnp.float32), 'ln_g': jnp.ones((HEAD_DIM,), jnp.float32), 'ln_b': jnp.zeros((HEAD_DIM,), jnp.float32)}
    _L0_xattn_all = _L0_xattn_setup()
    _L0_xattn_in = {k: v for k, v in _L0_xattn_all.items() if k in ('Wq', 'Wk', 'Wv', 'Wp', 'bp', 'ln_g', 'ln_b')}
    del _L0_xattn_all

    def _L0_ffn_setup():
        import jax, jax.numpy as jnp
        import numpy as np
        TOP_K = 2
        ROUTE_SCALE = 1.0
        EPS = 1e-20
        B, S, D = (2, 128, 256)
        E = 8
        F = 192
        FS = 192 * 1
        key = jax.random.key(seed)
        ks = jax.random.split(key, 9)
        s = 0.02
        return {'hidden_states': jax.random.normal(ks[0], (B, S, D), dtype=jnp.float32), 'W_gate_router': jax.random.normal(ks[1], (D, E), dtype=jnp.float32) * s, 'expert_bias': jnp.zeros((E,), dtype=jnp.float32), 'Wg': jax.random.normal(ks[2], (E, D, F), dtype=jnp.float32) * s, 'Wu': jax.random.normal(ks[3], (E, D, F), dtype=jnp.float32) * s, 'Wd': jax.random.normal(ks[4], (E, F, D), dtype=jnp.float32) * s, 'Wg_s': jax.random.normal(ks[5], (D, FS), dtype=jnp.float32) * s, 'Wu_s': jax.random.normal(ks[6], (D, FS), dtype=jnp.float32) * s, 'Wd_s': jax.random.normal(ks[7], (FS, D), dtype=jnp.float32) * s}
    _L0_ffn_all = _L0_ffn_setup()
    _L0_ffn_in = {k: v for k, v in _L0_ffn_all.items() if k in ('W_gate_router', 'expert_bias', 'Wg', 'Wu', 'Wd', 'Wg_s', 'Wu_s', 'Wd_s')}
    del _L0_ffn_all
    return {'x': x, 'ctx_1024': ctx_1024, 'L0_xattn_Wq': _L0_xattn_in['Wq'], 'L0_xattn_Wk': _L0_xattn_in['Wk'], 'L0_xattn_Wv': _L0_xattn_in['Wv'], 'L0_xattn_Wp': _L0_xattn_in['Wp'], 'L0_xattn_bp': _L0_xattn_in['bp'], 'L0_xattn_ln_g': _L0_xattn_in['ln_g'], 'L0_xattn_ln_b': _L0_xattn_in['ln_b'], 'L0_ffn_W_gate_router': _L0_ffn_in['W_gate_router'], 'L0_ffn_expert_bias': _L0_ffn_in['expert_bias'], 'L0_ffn_Wg': _L0_ffn_in['Wg'], 'L0_ffn_Wu': _L0_ffn_in['Wu'], 'L0_ffn_Wd': _L0_ffn_in['Wd'], 'L0_ffn_Wg_s': _L0_ffn_in['Wg_s'], 'L0_ffn_Wu_s': _L0_ffn_in['Wu_s'], 'L0_ffn_Wd_s': _L0_ffn_in['Wd_s']}

def reference(x, ctx_1024, L0_xattn_Wq, L0_xattn_Wk, L0_xattn_Wv, L0_xattn_Wp, L0_xattn_bp, L0_xattn_ln_g, L0_xattn_ln_b, L0_ffn_W_gate_router, L0_ffn_expert_bias, L0_ffn_Wg, L0_ffn_Wu, L0_ffn_Wd, L0_ffn_Wg_s, L0_ffn_Wu_s, L0_ffn_Wd_s):
    import jax
    import jax.numpy as jnp

    def _L0_xattn_ref(x1, x2, Wq, Wk, Wv, Wp, bp, ln_g, ln_b):
        import jax, jax.numpy as jnp
        import numpy as np
        NUM_HEADS = 16
        D_MODEL = 256
        HEAD_DIM = D_MODEL // NUM_HEADS
        SCALE = 8.0 / HEAD_DIM
        LN_EPS = 1e-05

        def _layernorm(x, g, b):
            mu = jnp.mean(x, axis=-1, keepdims=True)
            var = jnp.mean(jnp.square(x - mu), axis=-1, keepdims=True)
            return (x - mu) * jax.lax.rsqrt(var + LN_EPS) * g + b
        B, N, C = x1.shape
        M = x2.shape[1]
        H, D = (NUM_HEADS, HEAD_DIM)
        q = (x1 @ Wq.T).reshape(B, N, H, D).transpose(0, 2, 1, 3)
        k = (x2 @ Wk.T).reshape(B, M, H, D).transpose(0, 2, 1, 3)
        v = (x2 @ Wv.T).reshape(B, M, H, D).transpose(0, 2, 1, 3)
        q = _layernorm(q, ln_g, ln_b)
        k = _layernorm(k, ln_g, ln_b)
        q = q * SCALE
        attn = jnp.einsum('bhnd,bhmd->bhnm', q, k)
        attn = jax.nn.softmax(attn, axis=-1)
        out = jnp.einsum('bhnm,bhmd->bhnd', attn, v)
        out = out.transpose(0, 2, 1, 3).reshape(B, N, C)
        return out @ Wp.T + bp

    def _L0_ffn_ref(hidden_states, W_gate_router, expert_bias, Wg, Wu, Wd, Wg_s, Wu_s, Wd_s):
        import jax, jax.numpy as jnp
        import numpy as np
        TOP_K = 2
        ROUTE_SCALE = 1.0
        EPS = 1e-20
        B, S, D = (2, 128, 256)
        E = 8
        F = 192
        FS = 192 * 1
        b, s, d = hidden_states.shape
        x = hidden_states.reshape(-1, d)
        T = x.shape[0]
        logits = x @ W_gate_router
        scores = jax.nn.sigmoid(logits.astype(jnp.float32))
        _, sel = jax.lax.top_k(scores + expert_bias, TOP_K)
        top_scores = jnp.take_along_axis(scores, sel, axis=1)
        top_scores = top_scores / (top_scores.sum(-1, keepdims=True) + EPS)
        top_scores = top_scores * ROUTE_SCALE
        shared = jax.nn.silu(x @ Wg_s) * (x @ Wu_s) @ Wd_s
        tok = jnp.repeat(jnp.arange(T), TOP_K)
        exp = sel.reshape(-1)
        w = top_scores.reshape(-1)
        xr = x[tok]
        h = jax.nn.silu(jnp.einsum('nd,edf->enf', xr, Wg)) * jnp.einsum('nd,edf->enf', xr, Wu)
        out_all = jnp.einsum('enf,efd->end', h, Wd)
        routed = out_all[exp, jnp.arange(exp.shape[0])]
        routed = (routed.astype(jnp.float32) * w[:, None]).astype(hidden_states.dtype)
        out = shared.at[tok].add(routed)
        return out.reshape(b, s, d)
    x = x + _L0_xattn_ref(_layernorm(x, axis=-1), ctx_1024, L0_xattn_Wq, L0_xattn_Wk, L0_xattn_Wv, L0_xattn_Wp, L0_xattn_bp, L0_xattn_ln_g, L0_xattn_ln_b)
    x = x + _L0_ffn_ref(_layernorm(x, axis=-1), L0_ffn_W_gate_router, L0_ffn_expert_bias, L0_ffn_Wg, L0_ffn_Wu, L0_ffn_Wd, L0_ffn_Wg_s, L0_ffn_Wu_s, L0_ffn_Wd_s)
    return x

_drawn_inputs = setup_inputs


def setup_inputs(seed=0):
    import zlib

    import numpy as np

    out = dict(_drawn_inputs(seed))
    spreads = {'L0_xattn_bp': (0.0, 0.1),
     'L0_xattn_ln_g': (1.0, 0.2),
     'L0_xattn_ln_b': (0.0, 0.324),
     'L0_ffn_expert_bias': (0.0, 0.8)}
    factors = {'L0_ffn_W_gate_router': 8.0,
     'L0_ffn_Wg': 6.56,
     'L0_ffn_Wu': 6.471,
     'L0_ffn_Wd': 6.493,
     'L0_ffn_Wg_s': 4.669,
     'L0_ffn_Wu_s': 4.618,
     'L0_ffn_Wd_s': 4.617}
    for name, (base, spread) in spreads.items():
        noise = np.random.default_rng([zlib.crc32(name.encode()), seed]).standard_normal(out[name].shape)
        drawn = base * np.exp(spread * noise) if base else spread * noise
        out[name] = jnp.asarray(drawn.astype(out[name].dtype))
    for name, factor in factors.items():
        out[name] = (out[name] * factor).astype(out[name].dtype)
    return out
```

```python
from contextlib import ExitStack

import concourse.bass as bass
from concourse import mybir
from concourse.bass import ds
import numpy as np

F32 = mybir.dt.float32
F16 = mybir.dt.float16
I32 = mybir.dt.int32
ALU = mybir.AluOpType
ACT = mybir.ActivationFunctionType
AX = mybir.AxisListType.X

P = 128
B, N, D = 4, 1024, 256
M, H, HD = 154, 16, 16
KC = D // P
GH = 4
G = H // GH
GW = GH * HD
W = -(-GH * M // P)
VC = HD + 1
STEPS = B * G
TT = 2
TILES = B * N // P
E, F = 8, 192
FC = 2
FP = F // FC
SLOTS = 2 * TILES + E
ROW = D + 2
SCALE = 8.0 / HD
EPS = 1e-5
GUARD = 64.0
PV_LAG, O_LAG, Q_LEAD = 1, 6, 4
SEGMENTS = [(-4, 1, "q"), (-2, 1, "q"), (0, 1, "sqp"), (2, 2, "sqp"), (6, 1, "sqpo"), (8, 2, "sqpo"), (12, 2, "spo"), (16, 1, "po"),
            (18, 2, "o")]
G_LAG, H_LAG, D_LAG = 1, 2, 3
SORTED = SLOTS * P
NOWHERE = 1 << 15
BIG = 1e30
CT = 4


def segments(eng, body):
    for first, pairs, kinds in SEGMENTS:
        if pairs == 1:
            for p in range(2):
                body(first + p, p, kinds)
        else:
            with eng.Fori(0, pairs) as i:
                for p in range(2):
                    body(2 * i + (first + p), p, kinds)


def ffn_steps(eng, tiles, body):
    def peeled(j):
        body(j, j % 2, lambda lag: 0 <= j - lag < tiles)
    for j in range(4):
        peeled(j)
    with eng.Fori(2, tiles // 2) as i:
        for p in range(2):
            body(2 * i + p, p, lambda lag: True)
    for j in range(tiles, tiles + 4):
        peeled(j)


def works(kind, s, kinds):
    if kind not in kinds:
        return False
    return not (isinstance(s, int) and kind == "p" and not 0 <= s - PV_LAG < STEPS)


def build(nc, x, xT, ctx2T, wq, wkv, wp, bp, ln_g, ln_b, centre, ident, ident16, mask, maskT, wr, wgu, wd, wgu_s, wd_s, e_bias, tri_c, rev_c, tok_c, tst_c, fill_c,
          x2_rows, x2_cols, sorted_rows, y_rows, out):
    ctx = ExitStack()
    with ctx:
        def sb(name, shape, dt=F32):
            return ctx.enter_context(nc.sbuf_tensor(name, shape, dt))

        def ps(name, shape, dt=F32):
            return ctx.enter_context(nc.psum_tensor(name, shape, dt))

        def sem(name):
            return ctx.enter_context(nc.semaphore(name))

        id32 = sb("id32", [P, P])
        id16 = sb("id16", [P, P], F16)
        msk = sb("msk", [P, W, GH])
        mskT = sb("mskT", [P, W, P], F16)
        wq_sb = sb("wq_sb", [P, KC, D])
        wp_sb = sb("wp_sb", [P, KC, D])
        wr_sb = sb("wr_sb", [P, KC, E])
        bp_sb = sb("bp_sb", [P, D])
        gb = sb("gb", [P, 2, HD])
        hmean = sb("hmean", [P, KC, 2, H])
        kred = sb("kred", [P, 6, STEPS * W])
        kbias = sb("kbias", [P, STEPS * W])
        gcoef = sb("gcoef", [P, 4, HD])
        guard = sb("guard", [P, 4])
        KB = sb("KB", [P, STEPS, W, 2, P], F16)
        VB = sb("VB", [P, STEPS, W, GH * VC])
        x_in = sb("x_in", [P, 2, KC, TT * P])
        X1 = sb("X1", [P, TILES, D])
        xstat = sb("xstat", [P, TT, 6])
        xmv = sb("xmv", [P, TT, 2])
        qeps = sb("qeps", [P, TT])
        sq = sb("sq", [P, TT * D])
        qss = sb("qss", [P, TT * H])
        qln = sb("qln", [P, TT * H])
        qr = sb("qr", [P, TT * H])
        nq = sb("nq", [P, TT, G, GW])
        qs = sb("qs", [P, TT, G, 2, GW], F16)
        qT = sb("qT", [P, 2, G, N], F16)
        Pb = sb("Pb", [P, 2, W, N])
        scr = Pb[:, :, :, :].rearrange("p a c n -> p (a c n)")
        sizes = [STEPS * W * HD] * 4 + [2 * D, KC * D, KC * D, 2 * KC * D, 2 * G * P]
        part = [scr[:, sum(sizes[:i]):sum(sizes[:i + 1])] for i in range(len(sizes))]
        kown, ktmp, ktmp2 = (x_.rearrange("p (r d) -> p r d", d=HD) for x_ in part[:3])
        krep = part[8].bitcast(F16).rearrange("p (a l g k) -> p a l g k", a=2, l=2, g=G)
        khl = part[3].bitcast(F16).rearrange("p (l r d) -> p l r d", l=2, d=HD)
        kgrp = part[4].rearrange("p (a g d j) -> p a g d j", a=2, g=G, j=GH)
        cen, wq_raw, wkv_sb = (x_.rearrange("p (k n) -> p k n", k=KC) for x_ in part[5:8])
        rec = sb("rec", [P, 2, 4 * GH])
        Oat = sb("Oat", [P, 2 * N // P, D])
        c_x = Oat[:, :, :].rearrange("p t r -> p (t r)")[:, 0:KC * B * 2 * M].rearrange("p (k b m) -> p k b m", k=KC, b=B)
        OS = sb("OS", [P, 2, TT, D])
        OT = sb("OT", [P, TT * D])
        ostat = sb("ostat", [P, TT, 6])
        omv = sb("omv", [P, TT, 2])
        X2 = sb("X2", [P, 2, TT, D])
        X2T = sb("X2T", [P, 2, TT * D])
        LG = sb("LG", [P, TILES, E])
        oln = sb("oln", [P, TT])
        orr = sb("orr", [P, TT])

        def views(memory, *shapes):
            at, out_ = 0, []
            for shape in shapes:
                n_ = int(np.prod(shape))
                v_ = memory[:, at:at + n_]
                if len(shape) == 2:
                    v_ = v_.rearrange("p (a b) -> p a b", a=shape[0])
                if len(shape) == 3:
                    v_ = v_.rearrange("p (a b c) -> p a b c", a=shape[0], b=shape[1])
                out_.append(v_)
                at += n_
            return out_

        probs = Pb[:, :, :, :].rearrange("p a c n -> p (a c n)")
        wgu_sb, wd_sb = views(probs, (KC, E, 2 * F), (FC, E, D))
        ya, = views(probs, (2, 2 * CT, D))
        keys = KB[:, :, :, :, :].rearrange("p a b c d -> p (a b c d)").bitcast(F32)
        XR, wgus_sb = views(keys, (TILES, ROW), (KC, 2 * F))
        vals = VB[:, :, :, :].rearrange("p a b c -> p (a b c)")
        (tri, ones, ebias, rev, tokens, tstart, ex, sc, sbias, cand, oh1, oh2, cum_a, cum_b, slot, small, etf, wts, pos_f, etile, pos,
         wide) = views(vals, (P,), (P,), (E,), (E,), (TILES,), (SLOTS,), *[(TILES, E)] * 9, (16, TILES), (SLOTS,), (2, TILES),
                       (2, TILES), (SLOTS,), (2, TILES), (SLOTS, E))
        etile = etile.bitcast(I32)
        pos = pos.bitcast(I32)
        qmem = qT[:, :, :, :].rearrange("p a g n -> p (a g n)").bitcast(F32)
        wds_sb, x_row, x_col, act_g, h_in, h_col = views(qmem, (FC, D), (2, ROW), (2, D), (2, F), (2, F), (2, D))
        y_out = sq[:, :].rearrange("p (a d) -> p a d", a=2)
        dest_f = rec[:, 0, :]
        dest = rec[:, 1, :].bitcast(I32)
        empty = OS[:, 0, :, :].rearrange("p t d -> p (t d)")[:, 0:ROW]

        bankS = [ps(f"bankS{i}", [P, N]) for i in range(2)]
        bankO = [ps(f"bankO{i}", [P, 512]) for i in range(2)]
        bankQ = ps("bankQ", [P, 512])
        bankR = ps("bankR", [P, 512])

        c_in = sem("c_in")
        x_rows = sem("x_rows")
        x_ld = [sem("x_ld0"), sem("x_ld1")]
        wq_c = sem("wq_c")
        wq_h = sem("wq_h")
        dve_k = sem("dve_k")
        kv_rd = sem("kv_rd")
        kv_used = sem("kv_used")
        krep_rd = sem("krep_rd")
        kt_rd = sem("kt_rd")
        kb_done = sem("kb_done")
        k_ln = sem("k_ln")
        k_u = sem("k_u")
        u_all = sem("u_all")
        ctx_done = sem("ctx_done")
        pre = sem("pre")
        u_ready = sem("u_ready")
        sq_ready = sem("sq_ready")
        qv_ready = sem("qv_ready")
        qr_ready = sem("qr_ready")
        qs_ready = sem("qs_ready")
        qt_ready = sem("qt_ready")
        q_done = sem("q_done")
        act_q = sem("act_q")
        act_o = sem("act_o")
        dve_q = sem("dve_q")
        dve_p = sem("dve_p")
        dve_o = sem("dve_o")
        s_ready = sem("s_ready")
        exp_done = sem("exp_done")
        pv_ready = sem("pv_ready")
        pv_norm = sem("pv_norm")
        os_ld = [sem("os_ld0"), sem("os_ld1")]
        ot_ready = sem("ot_ready")
        ot_sb = sem("ot_sb")
        y_ready = sem("y_ready")
        ov_ready = sem("ov_ready")
        or_ready = sem("or_ready")
        o_done = sem("o_done")
        x2_ready = sem("x2_ready")
        x2t_ready = sem("x2t_ready")
        x2t_sb = sem("x2t_sb")
        lg_ready = sem("lg_ready")
        x2_st = [sem("x2_st0"), sem("x2_st1")]
        x2t_st = [sem("x2t_st0"), sem("x2t_st1")]
        s_out = sem("s_out")
        filled = sem("filled")
        fill_in = sem("fill_in")
        aside_n = {e_.engine: sem(f"aside{n_}") for n_, e_ in enumerate((nc.sync, nc.scalar, nc.vector))}
        r_in = sem("r_in")
        w_in = sem("w_in")
        xr_in = sem("xr_in")
        r_exp = sem("r_exp")
        r_tot = sem("r_tot")
        r_sum = sem("r_sum")
        r_ex0 = sem("r_ex0")
        routed = sem("routed")
        scat = [sem(f"scat{i}") for i in range(4)]
        kinds_ = ("s", "e")
        f_ld = {k: [sem(f"{k}_ld{i}") for i in range(2)] for k in kinds_}
        f_xt, f_xc, f_gu, f_si, f_h, f_ht, f_hc, f_y, f_yd = (
            {k: sem(f"{k}_{n_}") for k in kinds_} for n_ in ("xt", "xc", "gu", "si", "h", "ht", "hc", "y", "yd"))
        e_dst = sem("e_dst")
        e_chain = sem("e_chain")
        y_st = [sem("y_st0"), sem("y_st1")]
        c_ld = [sem("c_ld0"), sem("c_ld1")]
        c_half = sem("c_half")
        c_sum = sem("c_sum")
        o_st = [sem("o_st0"), sem("o_st1")]

        block = ctx.enter_context(nc.Block())
        N_CONST = 13
        def aside(eng):
            eng.sem_inc(aside_n[eng.engine], 1)

        starts = [(c * P) % M for c in range(W)]

        @block.sync
        def _(sp):
            for dst, src in (
                (cen[:], centre.rearrange("(k p) n -> p k n", p=P)),
                (wq_raw[:], wq.rearrange("(k p) n -> p k n", p=P)),
                (wkv_sb[:], wkv.rearrange("(k p) n -> p k n", p=P)),
                (c_x[:], ctx2T.rearrange("(k p) b m -> p k b m", p=P)),
                (gb[:, 0, :], ln_g.partition_broadcast(P)),
                (gb[:, 1, :], ln_b.partition_broadcast(P)),
                (bp_sb[:], bp.partition_broadcast(P)),
                (msk[:], mask), (mskT[:], maskT), (id16[:], ident16), (id32[:], ident),
                (wp_sb[:], wp.rearrange("(k p) n -> p k n", p=P)),
                (wr_sb[:], wr.rearrange("(k p) n -> p k n", p=P)),
            ):
                sp.dma_start(dst, src).then_inc(c_in, 16)
            for b in range(B):
                sp.dma_start(X1[:, b * 8:(b + 1) * 8, :],
                             x[b * N:(b + 1) * N, :].rearrange("(t p) d -> p t d", p=P)).then_inc(x_rows, 16)

            def outputs_in(n, p):
                sp.wait_ge(pv_norm, min(2 * n + 8, 2 * STEPS) if isinstance(n, int) else 2 * n + 8)
                aside(sp)
                if not isinstance(n, int) or n >= 2:
                    sp.wait_ge(ot_ready, n - 1)
                aside(sp)
                sp.dma_start(OS[:, p, :, :], Oat[:, ds((2 * n) % 16, TT), :]).then_inc(os_ld[p], 16)

            def store(m, p):
                sp.wait_ge(x2_ready, m + 1)
                aside(sp)
                sp.dma_start(x2_rows.rearrange("(t p) d -> p t d", p=P)[:, ds(2 * m, TT), :], X2[:, p, :, :]).then_inc(x2_st[p], 16)
                sp.wait_ge(x2t_sb, m + 1)
                aside(sp)
                sp.dma_start(x2_cols[ds(m, 1), :, :].rearrange("o p t -> p (o t)"), X2T[:, p, :]).then_inc(x2t_st[p], 16)

            outputs_in(0, 0)
            for m in range(2):
                outputs_in(m + 1, 1 - m)
                store(m, m)
            with sp.Fori(0, STEPS // 2 - 3) as i:
                for p in range(2):
                    m = 2 * i + (2 + p)
                    outputs_in(m + 1, 1 - p)
                    store(m, p)
            for m in range(STEPS - 4, STEPS):
                if m + 1 < STEPS:
                    outputs_in(m + 1, (m + 1) % 2)
                store(m, m % 2)
            sp.wait_ge(pv_ready, 2 * STEPS)
            sp.wait_ge(pv_norm, 2 * STEPS)
            for dst, src in ((tri, tri_c[0]), (ones, tri_c[1]), (ebias, e_bias.partition_broadcast(P)), (rev, rev_c), (tokens, tok_c),
                             (tstart, tst_c)):
                sp.dma_start(dst, src).then_inc(r_in, 16)
            for dst, src in ((wgus_sb, wgu_s.rearrange("(k p) f -> p k f", p=P)), (wds_sb[0:FP], wd_s.rearrange("(k p) d -> p k d", p=FP))):
                sp.dma_start(dst, src).then_inc(w_in, 16)
            for k in range(KC):
                sp.dma_start(wgu_sb[:, k], wgu[k * P:(k + 1) * P]).then_inc(w_in, 16)
            for k in range(FC):
                sp.dma_start(wd_sb[0:FP, k], wd[k * FP:(k + 1) * FP]).then_inc(w_in, 16)
            for p in range(2):
                sp.wait_ge(x2_st[p], 8 * STEPS)
                sp.wait_ge(x2t_st[p], 8 * STEPS)
            sp.dma_start(XR[:, :, 0:D], x2_rows.rearrange("(t p) d -> p t d", p=P)).then_inc(xr_in, 16)

            def load_shared(j, p, has):
                if has(0):
                    if not isinstance(j, int) or j >= 2:
                        sp.wait_ge(f_gu["s"], j - 1)
                    aside(sp)
                    src = x2_cols[ds(j // 2, 1), :, p * D:(p + 1) * D] if isinstance(j, int) else x2_cols[ds(j // 2, 1), :, p * D:(p + 1) * D]
                    sp.dma_start(x_col[:, p], src.rearrange("o p t -> p (o t)")).then_inc(f_ld["s"][p], 16)
            ffn_steps(sp, TILES, load_shared)

            for i in range(4):
                sp.wait_ge(scat[i], 16 * (2 * TILES // 4))

            def load_rows(j, p, has):
                if has(0):
                    if not isinstance(j, int) or j >= 2:
                        sp.wait_ge(f_xt["e"], j - 1)
                        sp.wait_ge(e_dst, j - 1)
                    aside(sp)
                    sp.dma_start(x_row[:, p], sorted_rows[ds(j, 1), :, :].rearrange("o p r -> p (o r)")).then_inc(f_ld["e"][p], 16)
            ffn_steps(sp, SLOTS, load_rows)

            for i in range(2):
                sp.wait_ge(y_st[i], 8 * SLOTS)
            y_t = y_rows.rearrange("(k t p) d -> p k t d", k=2, p=P)
            for c in range(TILES // CT):
                if c >= 2:
                    sp.wait_ge(c_sum, c - 1)
                for k in range(2):
                    sp.dma_start(ya[:, c % 2, k * CT:(k + 1) * CT], y_t[:, k, c * CT:(c + 1) * CT]) \
                        .then_inc(c_ld[c % 2], 16)
                if c >= 1:
                    sp.wait_ge(c_sum, c)
                    sp.dma_start(out.rearrange("(t p) d -> p t d", p=P)[:, (c - 1) * CT:c * CT], X1[:, (c - 1) * CT:c * CT]) \
                        .then_inc(s_out, 16)
            sp.wait_ge(c_sum, TILES // CT)
            sp.dma_start(out.rearrange("(t p) d -> p t d", p=P)[:, TILES - CT:], X1[:, TILES - CT:]).then_inc(s_out, 16)
            sp.wait_ge(s_out, 16 * (TILES // CT))

        @block.gpsimd
        def _(pool):
            def load(i, p):
                n = 2 * i + p
                if not (isinstance(n, int) and n < 2):
                    pool.wait_ge(u_ready, n - 1)
                pool.dma_start(x_in[:, p, :, :],
                               xT.rearrange("(k p) t -> p k t", p=P)[:, :, ds(256 * n, 256)]).then_inc(x_ld[p], 16)
            load(0, 0)
            load(0, 1)
            pool.dma_start(empty, fill_c).then_inc(fill_in, 16)
            pool.wait_ge(fill_in, 16)
            pool.dma_start(sorted_rows.rearrange("s p r -> p s r"), empty.unsqueeze(1).to_broadcast([P, SLOTS, ROW])).then_inc(filled, 16)
            pool.wait_ge(k_u, 1)
            pool.partition_all_reduce(guard[:, 1:2], guard[:, 0:1], P, bass.bass_isa.ReduceOp.max).then_inc(u_all, 1)
            with pool.Fori(1, STEPS // 2) as i:
                load(i, 0)
                load(i, 1)
            pool.wait_ge(xr_in, 16)
            pool.wait_ge(filled, 16)
            pool.wait_ge(routed, 1)
            for n in range(2 * TILES):
                t, k = divmod(n, 2)
                pool.indirect_dma_start(sorted_rows.rearrange("s p r -> (s p) r"), bass.IndirectOffsetOnAxis(ap=pos[:, k, t:t + 1], axis=0),
                                        XR[:, t, :], None, bounds_check=SORTED - 1, oob_is_err=False).then_inc(scat[n % 4], 16)
            for i in range(SLOTS):
                pool.wait_ge(f_yd["e"], i + 1)
                pool.indirect_dma_start(y_rows, bass.IndirectOffsetOnAxis(ap=dest[:, i % 4:i % 4 + 1], axis=0),
                                        y_out[:, i % 2], None, bounds_check=2 * B * N - 1, oob_is_err=False).then_inc(y_st[i % 2], 16)

        @block.scalar
        def _(act):
            act.preload_act_table_set("natural_log_exp_and_others")
            act.wait_ge(dve_k, 1)
            act.activation(kred[:, 1, :], kred[:, 0, :], ACT.Ln).then_inc(k_ln, 1)
            act.wait_ge(k_ln, 1)
            act.activation(kred[:, 2, :], kred[:, 1, :], ACT.Exp, scale=-0.5).then_inc(k_ln, 1)
            act.wait_ge(dve_k, 2)
            act.activation(kred[:, 4, :], kred[:, 3, :], ACT.Ln).then_inc(k_ln, 1)
            act.wait_ge(k_ln, 3)
            act.activation(kred[:, 5, :], kred[:, 4, :], ACT.Exp, scale=0.5).then_inc(k_ln, 1)

            act.wait_ge(dve_k, 3)
            for w in range(B * W):
                b, c = divmod(w, W)
                if w >= 2:
                    act.wait_ge(kt_rd, w - 1)
                for hl in range(2):
                    src = khl[:, hl, :, :].rearrange("p (s c) d -> p s c d", c=W)[:, b * G:(b + 1) * G, c, :]
                    act.activation(krep[:, w % 2, hl, :, :].rearrange("p g (r d) -> p g r d", d=HD),
                                   src.unsqueeze(2).to_broadcast([P, G, P // HD, HD]), ACT.Copy).then_inc(krep_rd, 1)

            def body(s, p, kinds):
                n, m = s + Q_LEAD, s - O_LAG

                def exp(c):
                    act.wait_ge(s_ready, 5 * s + (c + 1))
                    if not isinstance(s, int) or s >= 2:
                        act.wait_ge(pv_ready, 2 * s - 2)
                    act.wait_ge(ctx_done, 1)
                    act.activation(Pb[:, p, c, :], bankS[(p + c) % 2][:, :], ACT.Exp,
                                   bias=kbias[:, ds(5 * s + c, 1)]).then_inc(exp_done, 1)

                if works("s", s, kinds):
                    exp(0)
                if works("q", s, kinds):
                    act.wait_ge(u_ready, n + 1)
                    act.activation(sq[:, :], bankQ[:, :], ACT.Square).then_inc(sq_ready, 1)
                if works("o", s, kinds):
                    act.wait_ge(ot_ready, m + 1)
                    act.activation(OT[:, :], bankR[:, :], ACT.Copy).then_inc(ot_sb, 1)
                if works("s", s, kinds):
                    exp(1)
                if works("q", s, kinds):
                    act.wait_ge(qv_ready, n + 1)
                    act.activation(qln[:, :], qss[:, :], ACT.Ln).then_inc(act_q, 1)
                    act.wait_ge(act_q, n + 1)
                    act.activation(qr[:, :], qln[:, :], ACT.Exp, scale=-0.5).then_inc(qr_ready, 1)
                if works("s", s, kinds):
                    exp(2)
                if works("o", s, kinds):
                    act.wait_ge(ov_ready, m + 1)
                    act.activation(oln[:, :], omv[:, :, 1], ACT.Ln).then_inc(act_o, 1)
                    act.wait_ge(act_o, m + 1)
                    act.activation(orr[:, :], oln[:, :], ACT.Exp, scale=-0.5).then_inc(or_ready, 1)
                if works("s", s, kinds):
                    exp(3)
                if works("q", s, kinds):
                    act.wait_ge(qt_ready, n + 1)
                    if not (isinstance(n, int) and n < 8):
                        act.wait_ge(s_ready, 5 * (n - 4))
                    aside(act)
                    k = (n // 2) if isinstance(n, int) else (s + Q_LEAD) // 2
                    act.activation(qT[:, ds((n // 4) % 2, 1), :, ds(256 * (n % 4), 256)],
                                   bankQ[:, :].bitcast(F16).rearrange("p (o g t) -> p o g t", o=1, g=G), ACT.Copy).then_inc(q_done, 1)
                if works("s", s, kinds):
                    exp(4)
                if works("o", s, kinds):
                    act.wait_ge(x2t_ready, m + 1)
                    if not isinstance(m, int) or m >= 2:
                        act.wait_ge(lg_ready, m - 1)
                        act.wait_ge(x2t_st[p], 8 * (m - p))
                    act.activation(X2T[:, p, :], bankR[:, :], ACT.Copy).then_inc(x2t_sb, 1)
            segments(act, body)

            act.wait_ge(o_done, STEPS)
            act.wait_ge(r_in, 16 * 6)
            act.activation(ex[:], LG[:], ACT.Exp, scale=-1.0).then_inc(r_exp, 1)

            def ffn(kind, tiles):
                def step(j, p, has):
                    if kind == "e" and has(0):
                        act.wait_ge(f_xt["e"], j + 1)
                        if not isinstance(j, int) or j >= 2:
                            act.wait_ge(f_gu["e"], j - 1)
                        aside(act)
                        act.activation(x_col[:, p], bankO[p][:, 0:D], ACT.Copy).then_inc(f_xc["e"], 1)
                    i = j - G_LAG
                    if has(G_LAG):
                        act.wait_ge(f_gu[kind], i + 1)
                        if not isinstance(j, int) or i >= 2:
                            act.wait_ge(f_h[kind], i - 1)
                        aside(act)
                        act.activation(act_g[:, 1 - p], bankS[1 - p][:, 0:F], ACT.Silu).then_inc(f_si[kind], 1)
                ffn_steps(act, tiles, step)
            ffn("s", TILES)
            ffn("e", SLOTS)

        @block.tensor
        def _(pe):
            pe.wait_ge(c_in, 16 * N_CONST)
            for mt in range(KC):
                for k in range(KC):
                    last = pe.matmul(bankS[0][:, mt * D:(mt + 1) * D], cen[:, k, mt * P:(mt + 1) * P], wq_raw[:, k, :],
                                     start=(k == 0), stop=(k == KC - 1))
            last.then_inc(wq_c, 1)
            pe.wait_ge(wq_h, 2)
            kv = [bankO[0], bankO[1], bankR]
            for w in range(B * W):
                b, c = divmod(w, W)
                if w >= 3:
                    pe.wait_ge(kv_used, w - 2)
                for k in range(KC):
                    last = pe.matmul(kv[w % 3][:, :], c_x[:, k, b, starts[c]:starts[c] + P], wkv_sb[:, k, :],
                                     start=(k == 0), stop=(k == KC - 1))
                last.then_inc(kv_rd, 1)
            for w in range(B * W):
                pe.wait_ge(krep_rd, 2 * w + 2)
                if w >= 2:
                    pe.wait_ge(kb_done, w - 1)
                for hl in range(2):
                    for g in range(G):
                        o = bankO[w % 2][:, :].bitcast(F16)[:, (hl * G + g) * P:(hl * G + g + 1) * P]
                        last = pe.transpose(o, krep[:, w % 2, hl, g, :], id16[:, :])
                last.then_inc(kt_rd, 1)

            def body(s, p, kinds):
                n, m = s + Q_LEAD, s - O_LAG

                def scores(c):
                    if not works("s", s, kinds):
                        return
                    if c == 0:
                        pe.wait_ge(q_done, s + 4 if "q" in kinds else STEPS)
                        pe.wait_ge(ctx_done, 1)
                    if not isinstance(s, int) or 5 * s + c >= 2:
                        pe.wait_ge(exp_done, 5 * s + (c - 1))
                    for half in range(2):
                        for hl in range(2):
                            last = pe.matmul(bankS[(p + c) % 2][:, half * 512:half * 512 + 512],
                                             KB[:, ds(s, 1), c, hl, :].rearrange("p o k -> p (o k)"),
                                             qT[:, ds((s // 4) % 2, 1), ds(s % 4, 1), half * 512:half * 512 + 512].rearrange("p a b t -> p (a b t)"),
                                             start=(hl == 0), stop=(hl == 1))
                    last.then_inc(s_ready, 1)

                def pv(qts):
                    if not works("p", s, kinds):
                        return
                    v = s - PV_LAG
                    for qt in qts:
                        bank = qt // 4
                        if qt % 4 == 0:
                            pe.wait_ge(exp_done, 5 * v + 5)
                            if not isinstance(v, int) or v >= 1:
                                pe.wait_ge(pv_norm, 2 * v + (bank - 1))
                        for c in range(W):
                            last = pe.matmul(bankO[bank][:, (qt % 4) * GH * VC:(qt % 4 + 1) * GH * VC],
                                             Pb[:, 1 - p, c, qt * P:(qt + 1) * P],
                                             VB[:, ds(v, 1), c, :].rearrange("p o k -> p (o k)"), start=(c == 0), stop=(c == W - 1))
                        if qt % 4 == 3:
                            last.then_inc(pv_ready, 1)

                scores(0)
                if works("q", s, kinds):
                    pe.wait_ge(x_ld[p], 8 * (n - p) + 16)
                    pe.wait_ge(wq_h, 2)
                    if not (isinstance(n, int) and n < 1):
                        pe.wait_ge(q_done, n)
                    for t in range(TT):
                        for k in range(KC):
                            last = pe.matmul(bankQ[:, t * D:(t + 1) * D], x_in[:, p, k, t * P:(t + 1) * P], wq_sb[:, k, :],
                                             start=(k == 0), stop=(k == KC - 1))
                    last.then_inc(u_ready, 1)
                if works("o", s, kinds):
                    pe.wait_ge(os_ld[p], 8 * (m - p) + 16)
                    if not (isinstance(m, int) and m < 1):
                        pe.wait_ge(o_done, m)
                    for t in range(TT):
                        for k in range(KC):
                            last = pe.transpose(bankR[:, (t * KC + k) * P:(t * KC + k + 1) * P],
                                                OS[:, p, t, k * P:(k + 1) * P], id32[:, :])
                    last.then_inc(ot_ready, 1)
                pv((0, 1))
                scores(1)
                pv((2, 3))
                if works("o", s, kinds):
                    pe.wait_ge(ot_sb, m + 1)
                    for t in range(TT):
                        for k in range(KC):
                            last = pe.matmul(bankR[:, t * D:(t + 1) * D], OT[:, (t * KC + k) * P:(t * KC + k + 1) * P],
                                             wp_sb[:, k, :], start=(k == 0), stop=(k == KC - 1))
                    last.then_inc(y_ready, 1)
                scores(2)
                pv((4, 5))
                if works("q", s, kinds):
                    pe.wait_ge(qs_ready, n + 1)
                    for g in range(G):
                        for t in range(TT):
                            last = pe.transpose(bankQ[:, :].bitcast(F16)[:, g * 256 + t * P:g * 256 + (t + 1) * P],
                                                qs[:, t, g, :, :].rearrange("p a b -> p (a b)"), id16[:, :])
                    last.then_inc(qt_ready, 1)
                scores(3)
                pv((6, 7))
                if works("o", s, kinds):
                    pe.wait_ge(x2_ready, m + 1)
                    for t in range(TT):
                        for k in range(KC):
                            last = pe.transpose(bankR[:, (t * KC + k) * P:(t * KC + k + 1) * P],
                                                X2[:, p, t, k * P:(k + 1) * P], id32[:, :])
                    last.then_inc(x2t_ready, 1)
                scores(4)
                if works("o", s, kinds):
                    pe.wait_ge(x2t_sb, m + 1)
                    for t in range(TT):
                        for k in range(KC):
                            last = pe.matmul(bankR[:, t * E:(t + 1) * E], X2T[:, p, (t * KC + k) * P:(t * KC + k + 1) * P],
                                             wr_sb[:, k, :], start=(k == 0), stop=(k == KC - 1))
                    last.then_inc(lg_ready, 1)
            segments(pe, body)

            pe.wait_ge(r_in, 16 * 6)
            pe.wait_ge(r_tot, 1)
            pe.matmul(bankQ[:, 0:E], tri, small[:, 0, 0:E], start=True, stop=True)
            pe.matmul(bankQ[:, E:2 * E], ones, small[:, 0, 0:E], start=True, stop=True).then_inc(r_sum, 1)

            def ffn(kind, tiles):
                def expert(i):
                    return pe.value_load(etile[0:1, ds(i, 1)], min_val=0, max_val=E - 1)

                def step(j, p, has):
                    q = 1 - p
                    if kind == "e" and has(0):
                        pe.wait_ge(f_ld["e"][p], 8 * (j - p) + 16)
                        if not isinstance(j, int) or j >= 2:
                            pe.wait_ge(f_xc["e"], j - 1)
                        for k in range(KC):
                            last = pe.transpose(bankO[p][:, k * P:(k + 1) * P], x_row[:, p, k * P:(k + 1) * P], id32[:, :])
                        last.then_inc(f_xt["e"], 1)
                    i = j - G_LAG
                    if has(G_LAG):
                        if kind == "e":
                            e_ = expert(i)
                            pe.wait_ge(f_xc["e"], i + 1)
                        else:
                            pe.wait_ge(f_ld["s"][q], 8 * (i - q) + 16)
                        if not isinstance(j, int) or i >= 2:
                            pe.wait_ge(f_h[kind], i - 1)
                        for k in range(KC):
                            rhs = wgu_sb[:, k, ds(e_, 1), :].rearrange("p o f -> p (o f)") if kind == "e" else wgus_sb[:, k, :]
                            last = pe.matmul(bankS[q][:, 0:2 * F], x_col[:, q, k * P:(k + 1) * P], rhs, start=(k == 0), stop=(k == KC - 1))
                        last.then_inc(f_gu[kind], 1)
                    i = j - D_LAG
                    if has(D_LAG):
                        if kind == "e":
                            e_ = expert(i)
                        pe.wait_ge(f_hc[kind], i + 1)
                        if not isinstance(j, int) or i >= 2:
                            pe.wait_ge(f_yd[kind], i - 1)
                        for k in range(FC):
                            rhs = wd_sb[0:FP, k, ds(e_, 1), :].rearrange("p o d -> p (o d)") if kind == "e" else wds_sb[0:FP, k, :]
                            last = pe.matmul(bankS[q][:, 512:512 + D], h_col[0:FP, q, k * P:(k + 1) * P], rhs, start=(k == 0), stop=(k == FC - 1))
                        last.then_inc(f_y[kind], 1)
                    i = j - H_LAG
                    if has(H_LAG):
                        pe.wait_ge(f_h[kind], i + 1)
                        if not isinstance(j, int) or i >= 2:
                            pe.wait_ge(f_hc[kind], i - 1)
                        for k in range(FC):
                            last = pe.transpose((bankQ, bankR)[p][0:FP, k * P:(k + 1) * P], h_in[:, p, k * FP:(k + 1) * FP], id32[:, :])
                        last.then_inc(f_ht[kind], 1)
                ffn_steps(pe, tiles, step)
            pe.wait_ge(w_in, 16 * (2 + KC + FC))
            ffn("s", TILES)
            pe.wait_ge(routed, 1)
            ffn("e", SLOTS)

        @block.vector
        def _(dve):
            link_n = [0]

            def link(ins):
                link_n[0] += 1
                ins.then_inc(pre, 1)
                dve.wait_ge(pre, link_n[0])

            dve.wait_ge(c_in, 16 * N_CONST)
            v = wkv_sb[:, :, 0:D].rearrange("p k (h d) -> p k h d", d=HD)
            link(dve.tensor_reduce(hmean[:, :, 0, :], v, AX, ALU.add))
            link(dve.tensor_scalar(hmean[:, :, 0, :], hmean[:, :, 0, :], 1.0 / HD, None, ALU.mult))
            for k in range(KC):
                last = dve.tensor_tensor(v[:, k], v[:, k], hmean[:, k, 0, :].unsqueeze(2).to_broadcast([P, H, HD]), ALU.subtract)
            last.then_inc(wq_h, 1)
            dve.wait_ge(wq_c, 1)
            v = bankS[0][:, 0:KC * D].rearrange("p (k h d) -> p k h d", k=KC, d=HD)
            link(dve.tensor_reduce(hmean[:, :, 1, :], v, AX, ALU.add))
            link(dve.tensor_scalar(hmean[:, :, 1, :], hmean[:, :, 1, :], 1.0 / HD, None, ALU.mult))
            for k in range(KC):
                last = dve.tensor_tensor(wq_sb[:, k, :].rearrange("p (h d) -> p h d", d=HD), v[:, k],
                                         hmean[:, k, 1, :].unsqueeze(2).to_broadcast([P, H, HD]), ALU.subtract)
            last.then_inc(wq_h, 1)
            link(dve.tensor_tensor(gcoef[:, 0, :], gb[:, 0, :], gb[:, 0, :], ALU.mult))
            link(dve.tensor_scalar(gcoef[:, 0, :], gcoef[:, 0, :], SCALE, None, ALU.mult))
            link(dve.tensor_tensor(gcoef[:, 1, :], gb[:, 0, :], gb[:, 1, :], ALU.mult))
            link(dve.tensor_scalar(gcoef[:, 1, :], gcoef[:, 1, :], SCALE, None, ALU.mult))
            link(dve.tensor_tensor(gcoef[:, 2, :], gb[:, 1, :], gb[:, 1, :], ALU.mult))
            link(dve.tensor_reduce(guard[:, 2:3], gcoef[:, 2, :], AX, ALU.add))
            link(dve.tensor_scalar(guard[:, 2:3], guard[:, 2:3], SCALE, None, ALU.mult))
            kv = [bankO[0], bankO[1], bankR]
            for w in range(B * W):
                b, c = divmod(w, W)
                dve.wait_ge(kv_rd, w + 1)
                src = kv[w % 3]
                m_ = msk[:, c, :].unsqueeze(1).unsqueeze(3).to_broadcast([P, G, GH, HD])
                if w >= 2:
                    dve.wait_ge(dve_k if False else kv_used, w - 1)
                dve.tensor_tensor(kgrp[:, w % 2, :, :, :].rearrange("p g d j -> p g j d"),
                                  src[:, 0:D].rearrange("p (g j d) -> p g j d", g=G, j=GH), m_, ALU.mult).then_inc(pre, 1)
                link_n[0] += 1
                dve.tensor_tensor(VB[:, b * G:(b + 1) * G, c, :].rearrange("p g (j d) -> p g j d", d=VC)[:, :, :, 0:HD],
                                  src[:, D:2 * D].rearrange("p (g j d) -> p g j d", g=G, j=GH), m_, ALU.mult)
                dve.wait_ge(pre, link_n[0])
                dve.tensor_reduce(kown[:, :, :].rearrange("p (s c) d -> p s c d", c=W)[:, b * G:(b + 1) * G, c, :],
                                  kgrp[:, w % 2, :, :, :], AX, ALU.add).then_inc(kv_used, 1)
            for b in range(B):
                for g in range(G):
                    last = dve.tensor_copy(VB[:, b * G + g, :, :].rearrange("p c (j d) -> p c j d", d=VC)[:, :, :, HD], msk[:, :, :])
            link(last)
            R = STEPS * W
            full = lambda a: a.unsqueeze(1).to_broadcast([P, R, HD])
            rows = lambda a: a.unsqueeze(2).to_broadcast([P, R, HD])
            dve.wait_ge(kv_used, B * W)
            link(dve.tensor_tensor(ktmp[:], kown[:], kown[:], ALU.mult))
            link(dve.tensor_reduce(kred[:, 3, :], ktmp[:], AX, ALU.add))
            dve.tensor_scalar(kred[:, 0, :], kred[:, 3, :], 1.0 / HD, EPS, ALU.mult, ALU.add).then_inc(dve_k, 1)
            dve.wait_ge(k_ln, 2)
            link(dve.tensor_tensor(kown[:], kown[:], rows(kred[:, 2, :]), ALU.mult))
            link(dve.tensor_tensor(ktmp[:], kown[:], full(gcoef[:, 1, :]), ALU.mult))
            link(dve.tensor_reduce(kbias[:], ktmp[:], AX, ALU.add))
            link(dve.tensor_scalar(kbias[:], kbias[:], guard[:, 2:3], None, ALU.add))
            link(dve.tensor_tensor(ktmp2[:], kown[:], full(gcoef[:, 0, :]), ALU.mult))
            link(dve.tensor_tensor(ktmp2[:], ktmp2[:], full(gcoef[:, 1, :]), ALU.add))
            link(dve.tensor_copy(khl[:, 0], ktmp2[:]))
            dve.tensor_tensor(khl[:, 1], ktmp2[:], khl[:, 0], ALU.subtract).then_inc(pre, 1)
            link_n[0] += 1
            link(dve.tensor_tensor(ktmp[:], ktmp2[:], ktmp2[:], ALU.mult))
            link(dve.tensor_reduce(kred[:, 3, :], ktmp[:], AX, ALU.add))
            dve.tensor_scalar(kred[:, 3, :], kred[:, 3, :], 1e-30, None, ALU.add).then_inc(dve_k, 1)
            dve.wait_ge(k_ln, 4)
            link(dve.scalar_tensor_tensor(out=kred[:, 0, :], in0=kred[:, 5, :], scalar=float(HD) ** 0.5, in1=kbias[:],
                                          op0=ALU.mult, op1=ALU.add))
            dve.tensor_reduce(guard[:, 0:1], kred[:, 0, :], AX, ALU.max).then_inc(k_u, 1)
            dve.wait_ge(u_all, 1)
            link(dve.tensor_scalar(guard[:, 3:4], guard[:, 1:2], -GUARD, 0.0, ALU.add, ALU.max))
            dve.tensor_scalar(kbias[:], kbias[:], guard[:, 3:4], None, ALU.subtract).then_inc(dve_k, 1)
            for w in range(B * W):
                b, c = divmod(w, W)
                dve.wait_ge(kt_rd, w + 1)
                dst = KB[:, b * G:(b + 1) * G, c, :, :].rearrange("p g l k -> p l g k")
                dve.tensor_tensor(dst, bankO[w % 2][:, :].bitcast(F16).rearrange("p (l g k) -> p l g k", l=2, g=G),
                                  mskT[:, c, :].unsqueeze(1).unsqueeze(1).to_broadcast([P, 2, G, P]), ALU.mult).then_inc(kb_done, 1)
            dve.wait_ge(kb_done, B * W)
            dve.tensor_copy(guard[:, 0:1], guard[:, 3:4]).then_inc(ctx_done, 1)

            dve.wait_ge(x_rows, 16 * B)

            def body(s, p, kinds):
                n, m = s + Q_LEAD, s - O_LAG
                QL, OL = 5, 4

                def q(k, ins):
                    ins.then_inc(dve_q, 1)
                    dve.wait_ge(dve_q, QL * n + k)

                def o(k, ins):
                    ins.then_inc(dve_o, 1)
                    dve.wait_ge(dve_o, OL * m + k)

                def norm(bank):
                    if not works("p", s, kinds):
                        return
                    v = s - PV_LAG
                    if "o" in kinds and bank == 0:
                        dve.wait_ge(os_ld[p], 8 * (m - p) + 16)
                    dve.wait_ge(pv_ready, 2 * v + (bank + 1))
                    src = bankO[bank][:, 0:4 * GH * VC].rearrange("p (t j d) -> p t j d", t=4, d=VC)
                    r = rec[:, bank, :].rearrange("p (t j) -> p t j", t=4)
                    dve.reciprocal(r, src[:, :, :, HD]).then_inc(dve_p, 1)
                    dve.wait_ge(dve_p, 2 * v + (bank + 1))
                    aside(dve)
                    dst = Oat[:, ds(8 * ((v // 4) % 2) + 4 * bank, 4), ds(GW * (v % 4), GW)].rearrange("p t (j d) -> p t j d", d=HD)
                    dve.tensor_tensor(dst, src[:, :, :, 0:HD], r.unsqueeze(3).to_broadcast([P, 4, GH, HD]), ALU.mult).then_inc(pv_norm, 1)

                if works("q", s, kinds):
                    aside(dve)
                    for t in range(TT):
                        last = dve.bn_stats(xstat[:, t, :], X1[:, ds(2 * n + t, 1), :].rearrange("p o d -> p (o d)"))
                    q(1, last)
                    aside(dve)
                    for t in range(TT):
                        last = dve.bn_aggr(xmv[:, t, :], xstat[:, t, :])
                    q(2, last)
                    q(3, dve.tensor_scalar(qeps[:, :], xmv[:, :, 1], EPS, EPS, ALU.add, ALU.mult))
                    dve.wait_ge(sq_ready, n + 1)
                    q(4, dve.tensor_reduce(qss[:, :], sq[:, :].rearrange("p (h d) -> p h d", d=HD), AX, ALU.add))
                    for t in range(TT):
                        last = dve.tensor_scalar(qss[:, t * H:(t + 1) * H], qss[:, t * H:(t + 1) * H], 1.0 / HD,
                                                 qeps[:, t:t + 1], ALU.mult, ALU.add)
                    last.then_inc(qv_ready, 1)
                norm(0)
                if works("o", s, kinds):
                    dve.wait_ge(y_ready, m + 1)
                    aside(dve)
                    xr = X1[:, ds(2 * m, TT), :].rearrange("p t d -> p (t d)")
                    o(1, dve.tensor_tensor(xr, xr, bankR[:, :], ALU.add))
                    for t in range(TT):
                        xt = X1[:, ds(2 * m + t, 1), :].rearrange("p o d -> p (o d)")
                        last = dve.tensor_tensor(xt, xt, bp_sb[:, :], ALU.add)
                    o(2, last)
                    aside(dve)
                    for t in range(TT):
                        last = dve.bn_stats(ostat[:, t, :], X1[:, ds(2 * m + t, 1), :].rearrange("p o d -> p (o d)"))
                    o(3, last)
                    aside(dve)
                    for t in range(TT):
                        last = dve.bn_aggr(omv[:, t, :], ostat[:, t, :])
                    o(4, last)
                    dve.tensor_scalar(omv[:, :, 1], omv[:, :, 1], EPS, None, ALU.add).then_inc(ov_ready, 1)
                if works("q", s, kinds):
                    dve.wait_ge(qr_ready, n + 1)
                    nqv = nq[:, :, :, :].rearrange("p t g (j d) -> p (t g j) d", d=HD)
                    q(5, dve.tensor_tensor(nqv, bankQ[:, :].rearrange("p (h d) -> p h d", d=HD),
                                           qr[:, :].unsqueeze(2).to_broadcast([P, TT * H, HD]), ALU.mult))
                    if not (isinstance(n, int) and n < 1):
                        dve.wait_ge(qt_ready, n)
                    hi = qs[:, :, :, 0, :].rearrange("p t g k -> p (t g) k")
                    lo = qs[:, :, :, 1, :].rearrange("p t g k -> p (t g) k")
                    full_ = nq[:, :, :, :].rearrange("p t g k -> p (t g) k")
                    dve.tensor_copy(hi, full_).then_inc(u_all, 1)
                    dve.wait_ge(u_all, n + 2)
                    dve.tensor_tensor(lo, full_, hi, ALU.subtract).then_inc(qs_ready, 1)
                if works("o", s, kinds):
                    dve.wait_ge(or_ready, m + 1)
                    if not isinstance(m, int) or m >= 2:
                        dve.wait_ge(x2t_ready, m - 1)
                        dve.wait_ge(x2_st[p], 8 * (m - p))
                    for t in range(TT):
                        last = dve.tensor_scalar(X2[:, p, t, :], X1[:, ds(2 * m + t, 1), :].rearrange("p o d -> p (o d)"),
                                                 omv[:, t, 0:1], orr[:, t:t + 1], ALU.subtract, ALU.mult)
                    last.then_inc(x2_ready, 1)
                norm(1)
                if works("o", s, kinds):
                    dve.wait_ge(lg_ready, m + 1)
                    dve.tensor_copy(LG[:, ds(2 * m, TT), :], bankR[:, 0:TT * E].rearrange("p (t e) -> p t e", e=E)).then_inc(o_done, 1)
            segments(dve, body)

            dve.wait_ge(r_exp, 1)
            dve.wait_ge(xr_in, 16)
            tile_of = lambda a: a.unsqueeze(2).to_broadcast([P, TILES, E])
            of_e = lambda a: a.unsqueeze(1).to_broadcast([P, TILES, E])
            link(dve.tensor_scalar(ex, ex, 1.0, None, ALU.add))
            link(dve.reciprocal(sc, ex))
            link(dve.tensor_tensor(sbias, sc, of_e(ebias), ALU.add))
            for k, oh in enumerate((oh1, oh2)):
                link(dve.tensor_reduce(small[:, 1], sbias, AX, ALU.max))
                link(dve.tensor_tensor(cand, sbias, tile_of(small[:, 1]), ALU.is_equal))
                link(dve.tensor_tensor(cand, cand, of_e(rev), ALU.mult))
                link(dve.tensor_reduce(small[:, 2 + k], cand, AX, ALU.max))
                link(dve.tensor_tensor(oh, cand, tile_of(small[:, 2 + k]), ALU.is_equal))
                link(dve.tensor_tensor(cand, oh, sc, ALU.mult))
                link(dve.tensor_reduce(small[:, 4 + k], cand, AX, ALU.add))
                if k == 0:
                    link(dve.scalar_tensor_tensor(out=sbias, in0=oh, scalar=-BIG, in1=sbias, op0=ALU.mult, op1=ALU.add))
            link(dve.tensor_tensor(cum_a, oh1, oh2, ALU.add))
            a_, b_ = cum_a, cum_b
            step_ = 1
            while step_ < TILES:
                dve.tensor_copy(b_[:, 0:step_], a_[:, 0:step_])
                link(dve.tensor_tensor(b_[:, step_:], a_[:, step_:], a_[:, 0:TILES - step_], ALU.add))
                a_, b_ = b_, a_
                step_ *= 2
            dve.tensor_copy(small[:, 0, 0:E], a_[:, TILES - 1, :]).then_inc(r_tot, 1)
            link(dve.tensor_tensor(slot, a_, oh1, ALU.subtract))
            link(dve.tensor_tensor(slot, slot, oh2, ALU.subtract))
            link(dve.tensor_tensor(small[:, 6], small[:, 4], small[:, 5], ALU.add))
            link(dve.tensor_scalar(small[:, 6], small[:, 6], 1e-20, None, ALU.add))
            link(dve.reciprocal(small[:, 7], small[:, 6]))
            for k in range(2):
                last = dve.tensor_tensor(wts[:, k], small[:, 4 + k], small[:, 7], ALU.mult)
            link(last)
            dve.wait_ge(r_sum, 1)
            n_i = small[:, 9, 0:E].bitcast(I32)
            link(dve.tensor_scalar(n_i, bankQ[:, E:2 * E], float(P - 1), None, ALU.add))
            link(dve.tensor_scalar(n_i, n_i, 7, 7, ALU.arith_shift_right, ALU.logical_shift_left))
            link(dve.tensor_copy(small[:, 10, 0:E], n_i))
            a_, b_ = small[:, 10, 0:E], small[:, 11, 0:E]
            link(dve.tensor_copy(small[:, 12, 0:E], a_))
            for step_ in (1, 2, 4):
                dve.tensor_copy(b_[:, 0:step_], a_[:, 0:step_])
                link(dve.tensor_tensor(b_[:, step_:], a_[:, step_:], a_[:, 0:E - step_], ALU.add))
                a_, b_ = b_, a_
            ends = a_
            link(dve.tensor_tensor(small[:, 12, 0:E], ends, small[:, 12, 0:E], ALU.subtract))
            link(dve.tensor_tensor(small[:, 12, 0:E], small[:, 12, 0:E], bankQ[:, 0:E], ALU.add))
            link(dve.tensor_tensor(slot, slot, of_e(small[:, 12, 0:E]), ALU.add))
            for k, oh in enumerate((oh1, oh2)):
                link(dve.tensor_tensor(cand, slot, oh, ALU.mult))
                link(dve.tensor_reduce(pos_f[:, k], cand, AX, ALU.add))
            link(dve.tensor_copy(pos, pos_f))
            link(dve.tensor_tensor(wide, tstart.unsqueeze(2).to_broadcast([P, SLOTS, E]), ends.unsqueeze(1).to_broadcast([P, SLOTS, E]), ALU.is_ge))
            link(dve.tensor_reduce(etf, wide, AX, ALU.add))
            link(dve.tensor_scalar(etf, etf, float(E - 1), None, ALU.min))
            link(dve.tensor_copy(etile, etf))
            link(dve.tensor_copy(XR[:, :, D], tokens))
            dve.tensor_scalar(XR[:, :, D + 1], small[:, 2], -1.0, float(E), ALU.mult, ALU.add).then_inc(routed, 1)

            def ffn(kind, tiles):
                def step(j, p, has):
                    q = 1 - p
                    if kind == "e" and has(0):
                        dve.wait_ge(f_ld["e"][p], 8 * (j - p) + 16)
                        if not isinstance(j, int) or j >= 4:
                            dve.wait_ge(y_st[p], 8 * (j - p) - 16)
                        aside(dve)
                        dve.tensor_scalar(dest_f[:, p:p + 1], x_row[:, p, D + 1:D + 2], etf[:, ds(j, 1)], float(B * N),
                                          ALU.not_equal, ALU.mult).then_inc(e_chain, 1)
                        dve.wait_ge(e_chain, j + 1)
                        aside(dve)
                        dve.tensor_tensor(dest[:, ds(j % 4, 1)], dest_f[:, p:p + 1], x_row[:, p, D:D + 1], ALU.add).then_inc(e_dst, 1)
                    i = j - D_LAG
                    if has(D_LAG):
                        dve.wait_ge(f_y[kind], i + 1)
                        if kind == "s":
                            xt = X1[:, ds(i, 1), :].rearrange("p o d -> p (o d)")
                            dve.tensor_tensor(xt, xt, bankS[q][:, 512:512 + D], ALU.add).then_inc(f_yd["s"], 1)
                        else:
                            if not isinstance(j, int) or i >= 2:
                                dve.wait_ge(y_st[q], 8 * (i - q))
                            aside(dve)
                            dve.tensor_copy(y_out[:, q], bankS[q][:, 512:512 + D]).then_inc(f_yd["e"], 1)
                    i = j - G_LAG
                    if has(G_LAG):
                        dve.wait_ge(f_si[kind], i + 1)
                        if not isinstance(j, int) or i >= 2:
                            dve.wait_ge(f_ht[kind], i - 1)
                        dve.tensor_tensor(h_in[:, q], act_g[:, q], bankS[q][:, F:2 * F], ALU.mult).then_inc(f_h[kind], 1)
                    i = j - H_LAG
                    if has(H_LAG):
                        dve.wait_ge(f_ht[kind], i + 1)
                        if not isinstance(j, int) or i >= 2:
                            dve.wait_ge(f_y[kind], i - 1)
                        aside(dve)
                        dve.tensor_copy(h_col[0:FP, p], (bankQ, bankR)[p][0:FP, 0:D]).then_inc(f_hc[kind], 1)
                ffn_steps(dve, tiles, step)
            ffn("s", TILES)
            ffn("e", SLOTS)

            for c in range(TILES // CT):
                dve.wait_ge(c_ld[c % 2], 32 * (c // 2 + 1))
                for k in range(2):
                    for t in range(CT):
                        tile = c * CT + t
                        last = dve.scalar_tensor_tensor(out=X1[:, tile, :], in0=ya[:, c % 2, k * CT + t], scalar=wts[:, k, tile:tile + 1],
                                                        in1=X1[:, tile, :], op0=ALU.mult, op1=ALU.add)
                    if k == 0:
                        last.then_inc(c_half, 1)
                        dve.wait_ge(c_half, c + 1)
                last.then_inc(c_sum, 1)


_OUT = (B, N, D)


def kernel(**inputs):
    import concourse.bacc as _bacc
    from concourse.bass_utils import run_bass_kernel_spmd as _run

    g = {k: np.asarray(v) for k, v in inputs.items()}
    a = {}
    a["x"] = g["x"].reshape(B * N, D)
    a["xT"] = np.ascontiguousarray(a["x"].T)
    c = g["ctx_1024"].transpose(2, 0, 1)
    a["ctx2T"] = np.ascontiguousarray(np.concatenate([c, c], axis=2))
    a["wq"] = np.ascontiguousarray(g["L0_xattn_Wq"].T)
    a["wkv"] = np.ascontiguousarray(np.concatenate([g["L0_xattn_Wk"].T, g["L0_xattn_Wv"].T], axis=1))
    a["wp"] = np.ascontiguousarray(g["L0_xattn_Wp"].T)
    a["bp"] = g["L0_xattn_bp"]
    a["wr"] = g["L0_ffn_W_gate_router"]
    a["ln_g"] = g["L0_xattn_ln_g"]
    a["ln_b"] = g["L0_xattn_ln_b"]
    a["centre"] = (np.eye(D) - 1.0 / D).astype(np.float32)
    a["ident"] = np.eye(P, dtype=np.float32)
    a["ident16"] = np.eye(P, dtype=np.float16)
    head = (np.arange(W)[None, :] * P + np.arange(P)[:, None]) // M
    a["mask"] = (head[:, :, None] == np.arange(GH)).astype(np.float32)
    own = (np.arange(P) // HD) % GH
    a["maskT"] = (own[:, None, None] == head.T[None]).astype(np.float16)
    cat = np.concatenate([g["L0_ffn_Wg"], g["L0_ffn_Wu"]], axis=2)
    a["wgu"] = np.ascontiguousarray(cat.transpose(1, 0, 2))
    a["wd"] = np.ascontiguousarray(g["L0_ffn_Wd"].transpose(1, 0, 2))
    a["wgu_s"] = np.concatenate([g["L0_ffn_Wg_s"], g["L0_ffn_Wu_s"]], axis=1)
    a["wd_s"] = g["L0_ffn_Wd_s"]
    a["e_bias"] = g["L0_ffn_expert_bias"]
    row = np.arange(P)
    a["tri_c"] = np.stack([row[:, None] < row[None, :], np.ones((P, P), bool)]).astype(np.float32)
    a["rev_c"] = np.tile(np.arange(E, 0, -1, dtype=np.float32), (P, 1))
    a["tok_c"] = (np.arange(TILES)[None, :] * P + row[:, None]).astype(np.float32)
    a["tst_c"] = np.tile(np.arange(SLOTS, dtype=np.float32) * P, (P, 1))
    a["fill_c"] = np.zeros((P, ROW), np.float32)
    a["fill_c"][:, D] = NOWHERE
    nc = _bacc.Bacc("TRN2", target_bir_lowering=False, num_devices=1)
    args = {n: nc.dram_tensor(f"in_{n}", v.shape, mybir.dt.from_np(v.dtype), kind="ExternalInput").ap() for n, v in a.items()}
    out = nc.dram_tensor("out", (B * N, D), F32, kind="ExternalOutput").ap()
    scratch = {n: nc.dram_tensor(n, shape, F32, kind="Internal").ap() for n, shape in (
        ("x2_rows", (B * N, D)), ("x2_cols", (STEPS, P, TT * D)), ("sorted_rows", (SLOTS, P, ROW)), ("y_rows", (2 * B * N, D)))}
    build(nc, **args, **scratch, out=out)
    r = _run(nc, [{f"in_{n}": v for n, v in a.items()}], core_ids=[0])
    return r.results[0]["out"].reshape(_OUT)
```

```python
from contextlib import ExitStack

import concourse.bass as bass
from concourse import mybir
from concourse.bass import ds
import numpy as np

F32 = mybir.dt.float32
F16 = mybir.dt.float16
I32 = mybir.dt.int32
ALU = mybir.AluOpType
ACT = mybir.ActivationFunctionType
AX = mybir.AxisListType.X

P = 128
B, N, D = 4, 1024, 256
M, H, HD = 154, 16, 16
KC = D // P
GH = 4
G = H // GH
GW = GH * HD
W = -(-GH * M // P)
VC = HD + 1
STEPS = B * G
TT = 2
TILES = B * N // P
E, F = 8, 192
FC = 2
FP = F // FC
SLOTS = 2 * TILES + E
ROW = D + 2
SCALE = 8.0 / HD
EPS = 1e-5
GUARD = 64.0
PV_LAG, O_LAG, U_LEAD, T_LEAD = 1, 6, 5, 4
SEGMENTS = [(-5, 0, "u"), (-4, 2, "ut"), (0, 0, "uts"), (1, 0, "utsp"), (2, 2, "utsp"), (6, 2, "utspo"), (10, 0, "utspo"), (11, 0, "tspo"),
            (12, 2, "spo"), (16, 0, "po")]
LATE = 11
SORTED = SLOTS * P
NOWHERE = 1 << 15
BIG = 1e30
CT = 4


def segments(eng, body):
    for first, pairs, kinds in SEGMENTS:
        if pairs == 0:
            body(first, first % 2, kinds)
        else:
            with eng.Fori(0, pairs) as i:
                for p in range(2):
                    body(2 * i + (first + p), p, kinds)


def quads(eng, tiles, body):
    body(0)
    with eng.Fori(1, tiles // 4 - 1) as a:
        body(a)
    body(tiles // 4 - 1)


def more(a, tiles):
    return not (isinstance(a, int) and a == tiles // 4 - 1)


def build(nc, x, xT, ctx2T, wq, wkv, wp, bp, ln_g, ln_b, centre, ident, ident16, mask, maskT, wr, wgu, wd, wgu_s, wd_s, e_bias, tri_c, rev_c, tok_c, tst_c, fill_c,
          x2_rows, x2_cols, sorted_rows, y_rows, out):
    ctx = ExitStack()
    with ctx:
        def sb(name, shape, dt=F32):
            return ctx.enter_context(nc.sbuf_tensor(name, shape, dt))

        def ps(name, shape, dt=F32):
            return ctx.enter_context(nc.psum_tensor(name, shape, dt))

        def sem(name):
            return ctx.enter_context(nc.semaphore(name))

        id32 = sb("id32", [P, P])
        id16 = sb("id16", [P, P], F16)
        msk = sb("msk", [P, W, GH])
        mskT = sb("mskT", [P, W, P], F16)
        wq_sb = sb("wq_sb", [P, KC, D])
        wp_sb = sb("wp_sb", [P, KC, D])
        wr_sb = sb("wr_sb", [P, KC, E])
        bp_sb = sb("bp_sb", [P, D])
        gb = sb("gb", [P, 2, HD])
        hmean = sb("hmean", [P, KC, 2, H])
        kred = sb("kred", [P, 6, STEPS * W])
        kbias = sb("kbias", [P, STEPS * W])
        gcoef = sb("gcoef", [P, 4, HD])
        guard = sb("guard", [P, 4])
        KB = sb("KB", [P, STEPS, W, 2, P], F16)
        VB = sb("VB", [P, STEPS, W, GH * VC])
        x_in = sb("x_in", [P, 2, KC, TT * P])
        X1 = sb("X1", [P, TILES, D])
        xstat = sb("xstat", [P, TT, 6])
        xmv = sb("xmv", [P, TT, 2])
        qeps = sb("qeps", [P, TT])
        sq = sb("sq", [P, TT * D])
        qss = sb("qss", [P, TT * H])
        qln = sb("qln", [P, TT * H])
        qr = sb("qr", [P, TT * H])
        nq = sb("nq", [P, TT, G, GW])
        qs = sb("qs", [P, TT, G, 2, GW], F16)
        qT = sb("qT", [P, 2, G, N], F16)
        Pb = sb("Pb", [P, 2, W, N])
        scr = Pb[:, :, :, :].rearrange("p a c n -> p (a c n)")
        sizes = [STEPS * W * HD] * 4 + [2 * D, KC * D, KC * D, 2 * KC * D, 2 * G * P]
        part = [scr[:, sum(sizes[:i]):sum(sizes[:i + 1])] for i in range(len(sizes))]
        kown, ktmp, ktmp2 = (x_.rearrange("p (r d) -> p r d", d=HD) for x_ in part[:3])
        krep = part[8].bitcast(F16).rearrange("p (a l g k) -> p a l g k", a=2, l=2, g=G)
        khl = part[3].bitcast(F16).rearrange("p (l r d) -> p l r d", l=2, d=HD)
        kgrp = part[4].rearrange("p (a g d j) -> p a g d j", a=2, g=G, j=GH)
        cen, wq_raw, wkv_sb = (x_.rearrange("p (k n) -> p k n", k=KC) for x_ in part[5:8])
        rec = sb("rec", [P, 2, 4 * GH])
        Oat = sb("Oat", [P, 2 * N // P, D])
        c_x = Oat[:, :, :].rearrange("p t r -> p (t r)")[:, 0:KC * B * 2 * M].rearrange("p (k b m) -> p k b m", k=KC, b=B)
        OS = sb("OS", [P, 2, TT, D])
        OT = sb("OT", [P, TT * D])
        ostat = sb("ostat", [P, TT, 6])
        omv = sb("omv", [P, TT, 2])
        X2 = sb("X2", [P, 2, TT, D])
        X2T = sb("X2T", [P, 2, TT * D])
        LG = sb("LG", [P, TILES, E])
        oln = sb("oln", [P, TT])
        late_mv = sb("late_mv", [P, STEPS - LATE, TT, 2])
        late_r = sb("late_r", [P, STEPS - LATE, TT])
        orr = sb("orr", [P, TT])

        def views(memory, *shapes):
            at, out_ = 0, []
            for shape in shapes:
                n_ = int(np.prod(shape))
                v_ = memory[:, at:at + n_]
                if len(shape) == 2:
                    v_ = v_.rearrange("p (a b) -> p a b", a=shape[0])
                if len(shape) == 3:
                    v_ = v_.rearrange("p (a b c) -> p a b c", a=shape[0], b=shape[1])
                out_.append(v_)
                at += n_
            return out_

        probs = Pb[:, :, :, :].rearrange("p a c n -> p (a c n)")
        wgu_sb, wd_sb = views(probs, (KC, E, 2 * F), (FC, E, D))
        ya, = views(probs, (2, 2 * CT, D))
        keys = KB[:, :, :, :, :].rearrange("p a b c d -> p (a b c d)").bitcast(F32)
        XR, wgus_sb = views(keys, (TILES, ROW), (KC, 2 * F))
        vals = VB[:, :, :, :].rearrange("p a b c -> p (a b c)")
        (tri, ones, ebias, rev, tokens, tstart, ex, sc, sbias, cand, oh1, oh2, cum_a, cum_b, slot, small, etf, wts, pos_f, etile, pos,
         wide) = views(vals, (P,), (P,), (E,), (E,), (TILES,), (SLOTS,), *[(TILES, E)] * 9, (16, TILES), (SLOTS,), (2, TILES),
                       (2, TILES), (SLOTS,), (2, TILES), (SLOTS, E))
        etile = etile.bitcast(I32)
        pos = pos.bitcast(I32)
        qmem = qT[:, :, :, :].rearrange("p a g n -> p (a g n)").bitcast(F32)
        wds_sb, x_col, act_g, h_in, h_col = views(qmem, (FC, D), (4, D), (4, F), (2, F), (4, D))
        x_row, y_out, dest_f, dest = views(Oat[:, :, :].rearrange("p t r -> p (t r)"), (4, ROW), (4, D), (2, 2), (SLOTS,))
        dest = dest.bitcast(I32)
        empty = OS[:, 0, :, :].rearrange("p t d -> p (t d)")[:, 0:ROW]

        bankS = [ps(f"bankS{i}", [P, N]) for i in range(2)]
        bankO = [ps(f"bankO{i}", [P, 512]) for i in range(2)]
        bankQ = ps("bankQ", [P, 512])
        bankR = ps("bankR", [P, 512])

        c_in = sem("c_in")
        x_rows = sem("x_rows")
        x_ld = [sem("x_ld0"), sem("x_ld1")]
        wq_c = sem("wq_c")
        wq_h = sem("wq_h")
        dve_k = sem("dve_k")
        kv_rd = sem("kv_rd")
        kv_used = sem("kv_used")
        krep_rd = sem("krep_rd")
        kt_rd = sem("kt_rd")
        kb_done = sem("kb_done")
        k_ln = sem("k_ln")
        k_u = sem("k_u")
        u_all = sem("u_all")
        ctx_done = sem("ctx_done")
        pre = sem("pre")
        u_ready = sem("u_ready")
        sq_ready = sem("sq_ready")
        qv_ready = sem("qv_ready")
        qr_ready = sem("qr_ready")
        qs_ready = sem("qs_ready")
        qt_ready = sem("qt_ready")
        q_done = sem("q_done")
        act_q = sem("act_q")
        act_o = sem("act_o")
        dve_q = sem("dve_q")
        dve_p = sem("dve_p")
        dve_o = sem("dve_o")
        s_ready = sem("s_ready")
        exp_done = sem("exp_done")
        pv_ready = sem("pv_ready")
        pv_norm = sem("pv_norm")
        os_ld = [sem("os_ld0"), sem("os_ld1")]
        ot_ready = sem("ot_ready")
        ot_sb = sem("ot_sb")
        y_ready = sem("y_ready")
        ov_ready = sem("ov_ready")
        or_ready = sem("or_ready")
        o_done = sem("o_done")
        x2_ready = sem("x2_ready")
        x2t_ready = sem("x2t_ready")
        x2t_sb = sem("x2t_sb")
        lg_ready = sem("lg_ready")
        x2_st = [sem("x2_st0"), sem("x2_st1")]
        x2t_st = [sem("x2t_st0"), sem("x2t_st1")]
        s_out = sem("s_out")
        filled = sem("filled")
        fill_in = sem("fill_in")
        aside_n = {e_.engine: sem(f"aside{n_}") for n_, e_ in enumerate((nc.sync, nc.scalar, nc.vector))}
        r_in = sem("r_in")
        ws_in = sem("ws_in")
        w_in = sem("w_in")
        lx_st = sem("lx_st")
        xr_in = sem("xr_in")
        r_exp = sem("r_exp")
        r_tot = sem("r_tot")
        r_sum = sem("r_sum")
        r_ex0 = sem("r_ex0")
        routed = sem("routed")
        scat = [sem(f"scat{i}") for i in range(4)]
        kinds_ = ("s", "e")
        l_ot, l_os, l_y, l_ov, l_ln, l_or, l_x2, l_xt, l_xs, l_lg, l_done = (
            sem("l_" + n_) for n_ in ("ot", "os", "y", "ov", "ln", "or", "x2", "xt", "xs", "lg", "done"))
        q_hi = sem("q_hi")
        f_ld = {k: [sem(f"{k}_ld{i}") for i in range(2)] for k in kinds_}
        f_xt, f_xc, f_gu, f_si, f_h, f_ht, f_hc, f_y, f_yd = (
            {k: sem(f"{k}_{n_}") for k in kinds_} for n_ in ("xt", "xc", "gu", "si", "h", "ht", "hc", "y", "yd"))
        e_dst = sem("e_dst")
        e_chain = sem("e_chain")
        y_st = [sem(f"y_st{i}") for i in range(4)]
        c_ld = [sem("c_ld0"), sem("c_ld1")]
        c_half = sem("c_half")
        c_sum = sem("c_sum")
        o_st = [sem("o_st0"), sem("o_st1")]

        def gate_bank(k):
            return bankS[0][:, (k % 2) * 512:(k % 2) * 512 + 512]

        def down_bank(k):
            return bankS[1][:, (k % 2) * 512:(k % 2) * 512 + D]

        late = range(LATE, STEPS)
        late_bank = [bankS[0][:, 0:512], bankS[0][:, 512:], bankS[1][:, 0:512], bankS[1][:, 512:], bankQ[:, :]]
        slot_of = lambda a, k: a[:, k].rearrange("p t d -> p (t d)")
        late_ot = [slot_of(OS, 0), slot_of(OS, 1), OT[:, :], slot_of(X2, 0), slot_of(X2, 1)]
        late_x2t = [x_in[:, 0].rearrange("p k t -> p (k t)"), x_in[:, 1].rearrange("p k t -> p (k t)"), sq[:, :],
                    nq[:, :, :, :].rearrange("p t g k -> p (t g k)"), X2T[:, 1, :]]

        block = ctx.enter_context(nc.Block())
        N_CONST = 13
        def aside(eng):
            eng.sem_inc(aside_n[eng.engine], 1)

        starts = [(c * P) % M for c in range(W)]

        @block.sync
        def _(sp):
            for dst, src in (
                (cen[:], centre.rearrange("(k p) n -> p k n", p=P)),
                (wq_raw[:], wq.rearrange("(k p) n -> p k n", p=P)),
                (wkv_sb[:], wkv.rearrange("(k p) n -> p k n", p=P)),
                (c_x[:], ctx2T.rearrange("(k p) b m -> p k b m", p=P)),
                (gb[:, 0, :], ln_g.partition_broadcast(P)),
                (gb[:, 1, :], ln_b.partition_broadcast(P)),
                (bp_sb[:], bp.partition_broadcast(P)),
                (msk[:], mask), (mskT[:], maskT), (id16[:], ident16), (id32[:], ident),
                (wp_sb[:], wp.rearrange("(k p) n -> p k n", p=P)),
                (wr_sb[:], wr.rearrange("(k p) n -> p k n", p=P)),
            ):
                sp.dma_start(dst, src).then_inc(c_in, 16)
            for b in range(B):
                sp.dma_start(X1[:, b * 8:(b + 1) * 8, :],
                             x[b * N:(b + 1) * N, :].rearrange("(t p) d -> p t d", p=P)).then_inc(x_rows, 16)

            def outputs_in(n, p):
                sp.wait_ge(pv_norm, 2 * n + 8)
                aside(sp)
                if not isinstance(n, int) or n >= 2:
                    sp.wait_ge(ot_ready, n - 1)
                    aside(sp)
                    sp.wait_ge(x2_st[p], 8 * (n - p))
                    aside(sp)
                    sp.wait_ge(x2t_st[p], 8 * (n - p))
                aside(sp)
                sp.dma_start(OS[:, p, :, :], Oat[:, ds((2 * n) % 16, TT), :]).then_inc(os_ld[p], 16)

            def store(m, p):
                sp.wait_ge(x2_ready, m + 1)
                aside(sp)
                sp.dma_start(x2_rows.rearrange("(t p) d -> p t d", p=P)[:, ds(2 * m, TT), :], X2[:, p, :, :]).then_inc(x2_st[p], 16)
                sp.wait_ge(x2t_sb, m + 1)
                aside(sp)
                sp.dma_start(x2_cols[ds(m, 1), :, :].rearrange("o p t -> p (o t)"), X2T[:, p, :]).then_inc(x2t_st[p], 16)

            outputs_in(0, 0)
            outputs_in(1, 1)
            store(0, 0)
            with sp.Fori(1, LATE // 2) as i:
                for p in range(2):
                    outputs_in(2 * i + p, p)
                    store(2 * i + (p - 1), 1 - p)
            outputs_in(LATE - 1, (LATE - 1) % 2)
            store(LATE - 2, LATE % 2)
            store(LATE - 1, 1 - LATE % 2)
            sp.wait_ge(s_ready, W * STEPS)
            for p in range(2):
                sp.wait_ge(x2_st[p], 16 * ((LATE + 1 - p) // 2))
            sp.dma_start(XR[:, 0:TT * LATE, 0:D], x2_rows.rearrange("(t p) d -> p t d", p=P)[:, 0:TT * LATE]).then_inc(xr_in, 16)
            sp.wait_ge(pv_ready, 2 * STEPS)
            for dst, src in ((tri, tri_c[0]), (ones, tri_c[1]), (ebias, e_bias.partition_broadcast(P)), (rev, rev_c), (tokens, tok_c),
                             (tstart, tst_c)):
                sp.dma_start(dst, src).then_inc(r_in, 16)
            for dst, src in ((wgus_sb, wgu_s.rearrange("(k p) f -> p k f", p=P)), (wds_sb[0:FP], wd_s.rearrange("(k p) d -> p k d", p=FP))):
                sp.dma_start(dst, src).then_inc(ws_in, 16)
            for k, m in enumerate(late):
                sp.wait_ge(l_xs, k + 1)
                sp.dma_start(x2_cols[m], late_x2t[k]).then_inc(lx_st, 16)
            for k in range(KC):
                sp.dma_start(wgu_sb[:, k], wgu[k * P:(k + 1) * P]).then_inc(w_in, 16)
            for k in range(FC):
                sp.dma_start(wd_sb[0:FP, k], wd[k * FP:(k + 1) * FP]).then_inc(w_in, 16)
            for p in range(2):
                sp.wait_ge(x2t_st[p], 16 * ((LATE + 1 - p) // 2))
            sp.wait_ge(lx_st, 16 * len(late))

            def load_shared(a):
                for h in range(2):
                    if not isinstance(a, int) or a >= 1:
                        sp.wait_ge(f_gu["s"], 4 * a + (2 * h - 2))
                    aside(sp)
                    sp.dma_start(x_col[:, 2 * h:2 * h + 2], x2_cols[ds(2 * a + h, 1), :, :].rearrange("o p (t c) -> p (o t) c", t=2)) \
                        .then_inc(f_ld["s"][h], 16)
            quads(sp, TILES, load_shared)

            for i in range(4):
                sp.wait_ge(scat[i], 16 * (2 * TILES // 4))

            def load_rows(a):
                for h in range(2):
                    if not isinstance(a, int) or a >= 1:
                        sp.wait_ge(f_xt["e"], 2 * a + (h - 1))
                        sp.wait_ge(e_dst, 2 * a + (h - 1))
                    aside(sp)
                    sp.dma_start(x_row[:, 2 * h:2 * h + 2], sorted_rows[ds(4 * a + 2 * h, 2), :, :].rearrange("t p r -> p t r")) \
                        .then_inc(f_ld["e"][h], 16)
            quads(sp, SLOTS, load_rows)

            for i in range(4):
                sp.wait_ge(y_st[i], 4 * SLOTS)
            y_t = y_rows.rearrange("(k t p) d -> p k t d", k=2, p=P)
            for c in range(TILES // CT):
                if c >= 2:
                    sp.wait_ge(c_sum, c - 1)
                for k in range(2):
                    sp.dma_start(ya[:, c % 2, k * CT:(k + 1) * CT], y_t[:, k, c * CT:(c + 1) * CT]) \
                        .then_inc(c_ld[c % 2], 16)
                if c >= 1:
                    sp.wait_ge(c_sum, c)
                    sp.dma_start(out.rearrange("(t p) d -> p t d", p=P)[:, (c - 1) * CT:c * CT], X1[:, (c - 1) * CT:c * CT]) \
                        .then_inc(s_out, 16)
            sp.wait_ge(c_sum, TILES // CT)
            sp.dma_start(out.rearrange("(t p) d -> p t d", p=P)[:, TILES - CT:], X1[:, TILES - CT:]).then_inc(s_out, 16)
            sp.wait_ge(s_out, 16 * (TILES // CT))

        @block.gpsimd
        def _(pool):
            def load(i, p):
                n = 2 * i + p
                if not (isinstance(n, int) and n < 2):
                    pool.wait_ge(u_ready, n - 1)
                pool.dma_start(x_in[:, p, :, :],
                               xT.rearrange("(k p) t -> p k t", p=P)[:, :, ds(256 * n, 256)]).then_inc(x_ld[p], 16)
            load(0, 0)
            load(0, 1)
            pool.dma_start(empty, fill_c).then_inc(fill_in, 16)
            pool.wait_ge(fill_in, 16)
            pool.dma_start(sorted_rows.rearrange("s p r -> p s r"), empty.unsqueeze(1).to_broadcast([P, SLOTS, ROW])).then_inc(filled, 16)
            pool.wait_ge(k_u, 1)
            pool.partition_all_reduce(guard[:, 1:2], guard[:, 0:1], P, bass.bass_isa.ReduceOp.max).then_inc(u_all, 1)
            with pool.Fori(1, STEPS // 2) as i:
                load(i, 0)
                load(i, 1)
            pool.wait_ge(xr_in, 16)
            pool.wait_ge(l_x2, len(late))
            pool.wait_ge(filled, 16)
            pool.wait_ge(routed, 1)
            for n in range(2 * TILES):
                t, k = divmod(n, 2)
                pool.indirect_dma_start(sorted_rows.rearrange("s p r -> (s p) r"), bass.IndirectOffsetOnAxis(ap=pos[:, k, t:t + 1], axis=0),
                                        XR[:, t, :], None, bounds_check=SORTED - 1, oob_is_err=False).then_inc(scat[n % 4], 16)
            for i in range(SLOTS):
                pool.wait_ge(f_yd["e"], i + 1)
                pool.indirect_dma_start(y_rows, bass.IndirectOffsetOnAxis(ap=dest[:, i:i + 1], axis=0),
                                        y_out[:, i % 4], None, bounds_check=2 * B * N - 1, oob_is_err=False).then_inc(y_st[i % 4], 16)

        @block.scalar
        def _(act):
            act.preload_act_table_set("natural_log_exp_and_others")
            act.wait_ge(dve_k, 1)
            act.activation(kred[:, 1, :], kred[:, 0, :], ACT.Ln).then_inc(k_ln, 1)
            act.wait_ge(k_ln, 1)
            act.activation(kred[:, 2, :], kred[:, 1, :], ACT.Exp, scale=-0.5).then_inc(k_ln, 1)
            act.wait_ge(dve_k, 2)
            act.activation(kred[:, 4, :], kred[:, 3, :], ACT.Ln).then_inc(k_ln, 1)
            act.wait_ge(k_ln, 3)
            act.activation(kred[:, 5, :], kred[:, 4, :], ACT.Exp, scale=0.5).then_inc(k_ln, 1)

            act.wait_ge(dve_k, 3)
            for w in range(B * W):
                b, c = divmod(w, W)
                if w >= 2:
                    act.wait_ge(kt_rd, w - 1)
                for hl in range(2):
                    src = khl[:, hl, :, :].rearrange("p (s c) d -> p s c d", c=W)[:, b * G:(b + 1) * G, c, :]
                    act.activation(krep[:, w % 2, hl, :, :].rearrange("p g (r d) -> p g r d", d=HD),
                                   src.unsqueeze(2).to_broadcast([P, G, P // HD, HD]), ACT.Copy).then_inc(krep_rd, 1)

            def body(s, p, kinds):
                n, tn, m = s + U_LEAD, s + T_LEAD, s - O_LAG

                def exp(s, p, c):
                    act.wait_ge(s_ready, 5 * s + (c + 1))
                    act.activation(Pb[:, p, c, :], bankS[(p + c) % 2][:, :], ACT.Exp,
                                   bias=kbias[:, ds(5 * s + c, 1)]).then_inc(exp_done, 1)

                if "o" in kinds:
                    act.wait_ge(ot_ready, m + 1)
                    act.activation(OT[:, :], bankR[:, :], ACT.Copy).then_inc(ot_sb, 1)
                if "p" in kinds:
                    exp(s - 1, 1 - p, W - 1)
                if "s" in kinds:
                    if isinstance(s, int) and s == 0:
                        act.wait_ge(ctx_done, 1)
                    exp(s, p, 0)
                if "t" in kinds:
                    act.wait_ge(qt_ready, tn + 1)
                    aside(act)
                    act.activation(qT[:, ds((tn // 4) % 2, 1), :, ds(256 * (tn % 4), 256)],
                                   bankQ[:, :].bitcast(F16).rearrange("p (o g t) -> p o g t", o=1, g=G), ACT.Copy).then_inc(q_done, 1)
                if "s" in kinds:
                    exp(s, p, 1)
                if "o" in kinds:
                    act.wait_ge(ov_ready, m + 1)
                    act.activation(oln[:, :], omv[:, :, 1], ACT.Ln).then_inc(act_o, 1)
                    act.wait_ge(act_o, m + 1)
                    act.activation(orr[:, :], oln[:, :], ACT.Exp, scale=-0.5).then_inc(or_ready, 1)
                if "u" in kinds:
                    act.wait_ge(u_ready, n + 1)
                    act.activation(sq[:, :], bankQ[:, :], ACT.Square).then_inc(sq_ready, 1)
                    act.wait_ge(qv_ready, n + 1)
                    act.activation(qln[:, :], qss[:, :], ACT.Ln).then_inc(act_q, 1)
                    act.wait_ge(act_q, n + 1)
                    act.activation(qr[:, :], qln[:, :], ACT.Exp, scale=-0.5).then_inc(qr_ready, 1)
                if "s" in kinds:
                    exp(s, p, 2)
                if "o" in kinds:
                    act.wait_ge(x2t_ready, m + 1)
                    act.activation(X2T[:, p, :], bankR[:, :], ACT.Copy).then_inc(x2t_sb, 1)
                if "s" in kinds:
                    exp(s, p, 3)
            segments(act, body)

            for k, m in enumerate(late):
                act.wait_ge(l_ot, k + 1)
                if k == 2:
                    act.wait_ge(y_ready, LATE)
                if k == 3:
                    for p in range(2):
                        act.wait_ge(x2_st[p], 16 * ((LATE + 1 - p) // 2))
                act.activation(late_ot[k], late_bank[k], ACT.Copy).then_inc(l_os, 1)
            for k, m in enumerate(late):
                act.wait_ge(l_ov, k + 1)
                act.activation(late_r[:, k], late_mv[:, k, :, 1], ACT.Ln).then_inc(l_ln, 1)
                act.wait_ge(l_ln, k + 1)
                act.activation(late_r[:, k], late_r[:, k], ACT.Exp, scale=-0.5).then_inc(l_or, 1)
                if k >= 1:
                    act.wait_ge(l_xt, k)
                    act.activation(late_x2t[k - 1], late_bank[k - 1], ACT.Copy).then_inc(l_xs, 1)
            act.wait_ge(x2t_st[1], 16 * (LATE // 2))
            act.wait_ge(l_xt, len(late))
            act.activation(late_x2t[-1], late_bank[-1], ACT.Copy).then_inc(l_xs, 1)
            act.wait_ge(o_done, LATE)
            act.wait_ge(l_done, len(late))
            act.wait_ge(r_in, 16 * 6)
            act.activation(ex[:], LG[:], ACT.Exp, scale=-1.0).then_inc(r_exp, 1)

            def columns(a):
                for h in range(2):
                    act.wait_ge(f_xt["e"], 2 * a + (h + 1))
                    act.activation(x_col[:, 2 * h:2 * h + 2], bankO[h][:, :].rearrange("p (t c) -> p t c", t=2), ACT.Copy) \
                        .then_inc(f_xc["e"], 1)

            def ffn(kind, tiles):
                def gates(a):
                    for k in range(4):
                        act.wait_ge(f_gu[kind], 4 * a + (k + 1))
                        if not isinstance(a, int) or a >= 1:
                            act.wait_ge(f_h[kind], 4 * a + (k - 3))
                        act.activation(act_g[:, k], gate_bank(k)[:, 0:F], ACT.Silu).then_inc(f_si[kind], 1)
                    if kind == "e" and more(a, tiles):
                        columns(a + 1)
                if kind == "e":
                    columns(0)
                quads(act, tiles, gates)
            ffn("s", TILES)
            ffn("e", SLOTS)

        @block.tensor
        def _(pe):
            pe.wait_ge(c_in, 16 * N_CONST)
            for mt in range(KC):
                for k in range(KC):
                    last = pe.matmul(bankS[0][:, mt * D:(mt + 1) * D], cen[:, k, mt * P:(mt + 1) * P], wq_raw[:, k, :],
                                     start=(k == 0), stop=(k == KC - 1))
            last.then_inc(wq_c, 1)
            pe.wait_ge(wq_h, 2)
            kv = [bankO[0], bankO[1], bankR]
            for w in range(B * W):
                b, c = divmod(w, W)
                if w >= 3:
                    pe.wait_ge(kv_used, w - 2)
                for k in range(KC):
                    last = pe.matmul(kv[w % 3][:, :], c_x[:, k, b, starts[c]:starts[c] + P], wkv_sb[:, k, :],
                                     start=(k == 0), stop=(k == KC - 1))
                last.then_inc(kv_rd, 1)
            for w in range(B * W):
                pe.wait_ge(krep_rd, 2 * w + 2)
                if w >= 2:
                    pe.wait_ge(kb_done, w - 1)
                for hl in range(2):
                    for g in range(G):
                        o = bankO[w % 2][:, :].bitcast(F16)[:, (hl * G + g) * P:(hl * G + g + 1) * P]
                        last = pe.transpose(o, krep[:, w % 2, hl, g, :], id16[:, :])
                last.then_inc(kt_rd, 1)

            def turn_two(bank, rows):
                for t in range(TT):
                    for k in range(KC):
                        last = pe.transpose(bank[:, (t * KC + k) * P:(t * KC + k + 1) * P], rows[:, t, k * P:(k + 1) * P], id32[:, :])
                return last

            def times_two(bank, width, columns, weights):
                for t in range(TT):
                    for k in range(KC):
                        last = pe.matmul(bank[:, t * width:(t + 1) * width], columns[:, (t * KC + k) * P:(t * KC + k + 1) * P],
                                         weights[:, k, :], start=(k == 0), stop=(k == KC - 1))
                return last

            def body(s, p, kinds):
                n, tn, v, m = s + U_LEAD, s + T_LEAD, s - PV_LAG, s - O_LAG

                def scores(s, p, c):
                    if not isinstance(s, int) or 5 * s + c >= 2:
                        pe.wait_ge(exp_done, 5 * s + (c - 1))
                    for half in range(2):
                        for hl in range(2):
                            last = pe.matmul(bankS[(p + c) % 2][:, half * 512:half * 512 + 512],
                                             KB[:, ds(s, 1), c, hl, :].rearrange("p o k -> p (o k)"),
                                             qT[:, ds((s // 4) % 2, 1), ds(s % 4, 1), half * 512:half * 512 + 512].rearrange("p a b t -> p (a b t)"),
                                             start=(hl == 0), stop=(hl == 1))
                    last.then_inc(s_ready, 1)

                def pv(qts):
                    for qt in qts:
                        bank = qt // 4
                        if qt == 0:
                            pe.wait_ge(exp_done, 5 * v + 5)
                        if qt % 4 == 0 and (not isinstance(v, int) or v >= 1):
                            pe.wait_ge(pv_norm, 2 * v + (bank - 1))
                        for c in range(W):
                            last = pe.matmul(bankO[bank][:, (qt % 4) * GH * VC:(qt % 4 + 1) * GH * VC],
                                             Pb[:, 1 - p, c, qt * P:(qt + 1) * P],
                                             VB[:, ds(v, 1), c, :].rearrange("p o k -> p (o k)"), start=(c == 0), stop=(c == W - 1))
                        if qt % 4 == 3:
                            last.then_inc(pv_ready, 1)

                if "o" in kinds:
                    pe.wait_ge(os_ld[p], 8 * (m - p) + 16)
                    if not (isinstance(m, int) and m < 1):
                        pe.wait_ge(o_done, m)
                    turn_two(bankR, OS[:, p]).then_inc(ot_ready, 1)
                if "p" in kinds:
                    scores(s - 1, 1 - p, W - 1)
                if "s" in kinds:
                    pe.wait_ge(q_done, s + T_LEAD if "t" in kinds else STEPS)
                    if isinstance(s, int) and s == 0:
                        pe.wait_ge(ctx_done, 1)
                    scores(s, p, 0)
                if "t" in kinds:
                    pe.wait_ge(qs_ready, tn + 1)
                    for g in range(G):
                        for t in range(TT):
                            last = pe.transpose(bankQ[:, :].bitcast(F16)[:, g * 256 + t * P:g * 256 + (t + 1) * P],
                                                qs[:, t, g, :, :].rearrange("p a b -> p (a b)"), id16[:, :])
                    last.then_inc(qt_ready, 1)
                if "o" in kinds:
                    pe.wait_ge(ot_sb, m + 1)
                    times_two(bankR, D, OT, wp_sb).then_inc(y_ready, 1)
                if "p" in kinds:
                    pv((0, 1))
                if "s" in kinds:
                    scores(s, p, 1)
                if "u" in kinds:
                    pe.wait_ge(x_ld[1 - p], 8 * (n + p) + 8)
                    if isinstance(n, int) and n == 0:
                        pe.wait_ge(wq_h, 2)
                    else:
                        pe.wait_ge(q_done, n)
                    for t in range(TT):
                        for k in range(KC):
                            last = pe.matmul(bankQ[:, t * D:(t + 1) * D], x_in[:, 1 - p, k, t * P:(t + 1) * P], wq_sb[:, k, :],
                                             start=(k == 0), stop=(k == KC - 1))
                    last.then_inc(u_ready, 1)
                if "p" in kinds:
                    pv((2, 3))
                if "s" in kinds:
                    scores(s, p, 2)
                if "o" in kinds:
                    pe.wait_ge(x2_ready, m + 1)
                    turn_two(bankR, X2[:, p]).then_inc(x2t_ready, 1)
                if "p" in kinds:
                    pv((4, 5))
                if "s" in kinds:
                    scores(s, p, 3)
                if "o" in kinds:
                    pe.wait_ge(x2t_sb, m + 1)
                    times_two(bankR, E, X2T[:, p], wr_sb).then_inc(lg_ready, 1)
                if "p" in kinds:
                    pv((6, 7))
            segments(pe, body)

            pe.wait_ge(exp_done, W * STEPS)
            pe.wait_ge(q_done, STEPS)
            pe.wait_ge(pv_norm, 2 * STEPS)
            for k, m in enumerate(late):
                turn_two(late_bank[k], Oat[:, (2 * m) % 16:(2 * m) % 16 + TT]).then_inc(l_ot, 1)
            for k, m in enumerate(late):
                pe.wait_ge(l_os, k + 1)
                times_two(late_bank[k], D, late_ot[k], wp_sb).then_inc(l_y, 1)
            for k, m in enumerate(late):
                pe.wait_ge(l_x2, k + 1)
                turn_two(late_bank[k], XR[:, 2 * m:2 * m + TT]).then_inc(l_xt, 1)
                if k >= 1:
                    pe.wait_ge(l_xs, k)
                    times_two(late_bank[k - 1], E, late_x2t[k - 1], wr_sb).then_inc(l_lg, 1)
            pe.wait_ge(l_xs, len(late))
            times_two(late_bank[-1], E, late_x2t[-1], wr_sb).then_inc(l_lg, 1)

            pe.wait_ge(r_in, 16 * 6)
            pe.wait_ge(r_tot, 1)
            pe.matmul(bankQ[:, 0:E], tri, small[:, 0, 0:E], start=True, stop=True)
            pe.matmul(bankQ[:, E:2 * E], ones, small[:, 0, 0:E], start=True, stop=True).then_inc(r_sum, 1)

            def expert(tile):
                return pe.value_load(etile[0:1, ds(tile, 1)], min_val=0, max_val=E - 1)

            def transposes(a, h):
                pe.wait_ge(f_ld["e"][h], 16 * a + 16)
                for t in range(2):
                    for k in range(KC):
                        last = pe.transpose(bankO[h][:, (t * KC + k) * P:(t * KC + k + 1) * P], x_row[:, 2 * h + t, k * P:(k + 1) * P], id32[:, :])
                last.then_inc(f_xt["e"], 1)

            def ffn(kind, tiles):
                def four(a):
                    def up(k, e_):
                        if k % 2 == 0:
                            if kind == "e":
                                pe.wait_ge(f_xc["e"], 2 * a + (k // 2 + 1))
                            else:
                                pe.wait_ge(f_ld["s"][k // 2], 16 * a + 16)
                        for c in range(KC):
                            rhs = wgu_sb[:, c, ds(e_, 1), :].rearrange("p o f -> p (o f)") if kind == "e" else wgus_sb[:, c, :]
                            last = pe.matmul(gate_bank(k)[:, 0:2 * F], x_col[:, k, c * P:(c + 1) * P], rhs, start=(c == 0), stop=(c == KC - 1))
                        last.then_inc(f_gu[kind], 1)

                    def turn(k):
                        pe.wait_ge(f_h[kind], 4 * a + (k + 1))
                        for c in range(FC):
                            last = pe.transpose((bankQ, bankR)[k % 2][0:FP, c * P:(c + 1) * P], h_in[:, k % 2, c * FP:(c + 1) * FP], id32[:, :])
                        last.then_inc(f_ht[kind], 1)

                    def down(k, e_):
                        pe.wait_ge(f_hc[kind], 4 * a + (k + 1))
                        if k >= 2 or not isinstance(a, int) or a >= 1:
                            pe.wait_ge(f_yd[kind], 4 * a + (k - 1))
                        for c in range(FC):
                            rhs = wd_sb[0:FP, c, ds(e_, 1), :].rearrange("p o d -> p (o d)") if kind == "e" else wds_sb[0:FP, c, :]
                            last = pe.matmul(down_bank(k), h_col[0:FP, k, c * P:(c + 1) * P], rhs,
                                             start=(c == 0), stop=(c == FC - 1))
                        last.then_inc(f_y[kind], 1)

                    e_ = [None] * 4
                    if kind == "e":
                        e_[0] = expert(4 * a)
                    for k in range(4):
                        up(k, e_[k])
                        if kind == "e" and k < 3:
                            e_[k + 1] = expert(4 * a + (k + 1))
                        if k >= 1:
                            turn(k - 1)
                        if k >= 2:
                            down(k - 2, e_[k - 2])
                    if kind == "e" and more(a, tiles):
                        transposes(a + 1, 0)
                    turn(3)
                    down(2, e_[2])
                    if kind == "e" and more(a, tiles):
                        transposes(a + 1, 1)
                    down(3, e_[3])
                if kind == "e":
                    transposes(0, 0)
                    transposes(0, 1)
                quads(pe, tiles, four)
            pe.wait_ge(ws_in, 16 * 2)
            ffn("s", TILES)
            pe.wait_ge(w_in, 16 * (KC + FC))
            pe.wait_ge(routed, 1)
            ffn("e", SLOTS)

        @block.vector
        def _(dve):
            link_n = [0]

            def link(ins):
                link_n[0] += 1
                ins.then_inc(pre, 1)
                dve.wait_ge(pre, link_n[0])

            dve.wait_ge(c_in, 16 * N_CONST)
            v = wkv_sb[:, :, 0:D].rearrange("p k (h d) -> p k h d", d=HD)
            link(dve.tensor_reduce(hmean[:, :, 0, :], v, AX, ALU.add))
            link(dve.tensor_scalar(hmean[:, :, 0, :], hmean[:, :, 0, :], 1.0 / HD, None, ALU.mult))
            for k in range(KC):
                last = dve.tensor_tensor(v[:, k], v[:, k], hmean[:, k, 0, :].unsqueeze(2).to_broadcast([P, H, HD]), ALU.subtract)
            last.then_inc(wq_h, 1)
            dve.wait_ge(wq_c, 1)
            v = bankS[0][:, 0:KC * D].rearrange("p (k h d) -> p k h d", k=KC, d=HD)
            link(dve.tensor_reduce(hmean[:, :, 1, :], v, AX, ALU.add))
            link(dve.tensor_scalar(hmean[:, :, 1, :], hmean[:, :, 1, :], 1.0 / HD, None, ALU.mult))
            for k in range(KC):
                last = dve.tensor_tensor(wq_sb[:, k, :].rearrange("p (h d) -> p h d", d=HD), v[:, k],
                                         hmean[:, k, 1, :].unsqueeze(2).to_broadcast([P, H, HD]), ALU.subtract)
            last.then_inc(wq_h, 1)
            link(dve.tensor_tensor(gcoef[:, 0, :], gb[:, 0, :], gb[:, 0, :], ALU.mult))
            link(dve.tensor_scalar(gcoef[:, 0, :], gcoef[:, 0, :], SCALE, None, ALU.mult))
            link(dve.tensor_tensor(gcoef[:, 1, :], gb[:, 0, :], gb[:, 1, :], ALU.mult))
            link(dve.tensor_scalar(gcoef[:, 1, :], gcoef[:, 1, :], SCALE, None, ALU.mult))
            link(dve.tensor_tensor(gcoef[:, 2, :], gb[:, 1, :], gb[:, 1, :], ALU.mult))
            link(dve.tensor_reduce(guard[:, 2:3], gcoef[:, 2, :], AX, ALU.add))
            link(dve.tensor_scalar(guard[:, 2:3], guard[:, 2:3], SCALE, None, ALU.mult))
            kv = [bankO[0], bankO[1], bankR]
            for w in range(B * W):
                b, c = divmod(w, W)
                dve.wait_ge(kv_rd, w + 1)
                src = kv[w % 3]
                m_ = msk[:, c, :].unsqueeze(1).unsqueeze(3).to_broadcast([P, G, GH, HD])
                if w >= 2:
                    dve.wait_ge(kv_used, w - 1)
                dve.tensor_tensor(kgrp[:, w % 2, :, :, :].rearrange("p g d j -> p g j d"),
                                  src[:, 0:D].rearrange("p (g j d) -> p g j d", g=G, j=GH), m_, ALU.mult).then_inc(pre, 1)
                link_n[0] += 1
                dve.tensor_tensor(VB[:, b * G:(b + 1) * G, c, :].rearrange("p g (j d) -> p g j d", d=VC)[:, :, :, 0:HD],
                                  src[:, D:2 * D].rearrange("p (g j d) -> p g j d", g=G, j=GH), m_, ALU.mult)
                dve.wait_ge(pre, link_n[0])
                dve.tensor_reduce(kown[:, :, :].rearrange("p (s c) d -> p s c d", c=W)[:, b * G:(b + 1) * G, c, :],
                                  kgrp[:, w % 2, :, :, :], AX, ALU.add).then_inc(kv_used, 1)
            for b in range(B):
                for g in range(G):
                    last = dve.tensor_copy(VB[:, b * G + g, :, :].rearrange("p c (j d) -> p c j d", d=VC)[:, :, :, HD], msk[:, :, :])
            link(last)
            R = STEPS * W
            full = lambda a: a.unsqueeze(1).to_broadcast([P, R, HD])
            rows = lambda a: a.unsqueeze(2).to_broadcast([P, R, HD])
            dve.wait_ge(kv_used, B * W)
            link(dve.tensor_tensor(ktmp[:], kown[:], kown[:], ALU.mult))
            link(dve.tensor_reduce(kred[:, 3, :], ktmp[:], AX, ALU.add))
            dve.tensor_scalar(kred[:, 0, :], kred[:, 3, :], 1.0 / HD, EPS, ALU.mult, ALU.add).then_inc(dve_k, 1)
            dve.wait_ge(k_ln, 2)
            link(dve.tensor_tensor(kown[:], kown[:], rows(kred[:, 2, :]), ALU.mult))
            link(dve.tensor_tensor(ktmp[:], kown[:], full(gcoef[:, 1, :]), ALU.mult))
            link(dve.tensor_reduce(kbias[:], ktmp[:], AX, ALU.add))
            link(dve.tensor_scalar(kbias[:], kbias[:], guard[:, 2:3], None, ALU.add))
            link(dve.tensor_tensor(ktmp2[:], kown[:], full(gcoef[:, 0, :]), ALU.mult))
            link(dve.tensor_tensor(ktmp2[:], ktmp2[:], full(gcoef[:, 1, :]), ALU.add))
            link(dve.tensor_copy(khl[:, 0], ktmp2[:]))
            dve.tensor_tensor(khl[:, 1], ktmp2[:], khl[:, 0], ALU.subtract).then_inc(pre, 1)
            link_n[0] += 1
            link(dve.tensor_tensor(ktmp[:], ktmp2[:], ktmp2[:], ALU.mult))
            link(dve.tensor_reduce(kred[:, 3, :], ktmp[:], AX, ALU.add))
            dve.tensor_scalar(kred[:, 3, :], kred[:, 3, :], 1e-30, None, ALU.add).then_inc(dve_k, 1)
            dve.wait_ge(k_ln, 4)
            link(dve.scalar_tensor_tensor(out=kred[:, 0, :], in0=kred[:, 5, :], scalar=float(HD) ** 0.5, in1=kbias[:],
                                          op0=ALU.mult, op1=ALU.add))
            dve.tensor_reduce(guard[:, 0:1], kred[:, 0, :], AX, ALU.max).then_inc(k_u, 1)
            dve.wait_ge(u_all, 1)
            link(dve.tensor_scalar(guard[:, 3:4], guard[:, 1:2], -GUARD, 0.0, ALU.add, ALU.max))
            dve.tensor_scalar(kbias[:], kbias[:], guard[:, 3:4], None, ALU.subtract).then_inc(dve_k, 1)
            for w in range(B * W):
                b, c = divmod(w, W)
                dve.wait_ge(kt_rd, w + 1)
                dst = KB[:, b * G:(b + 1) * G, c, :, :].rearrange("p g l k -> p l g k")
                dve.tensor_tensor(dst, bankO[w % 2][:, :].bitcast(F16).rearrange("p (l g k) -> p l g k", l=2, g=G),
                                  mskT[:, c, :].unsqueeze(1).unsqueeze(1).to_broadcast([P, 2, G, P]), ALU.mult).then_inc(kb_done, 1)
            dve.wait_ge(kb_done, B * W)
            dve.tensor_copy(guard[:, 0:1], guard[:, 3:4]).then_inc(ctx_done, 1)

            dve.wait_ge(x_rows, 16 * B)

            def body(s, p, kinds):
                n, v, m = s + U_LEAD, s - PV_LAG, s - O_LAG
                QL, OL = 5, 4

                def q(k, ins):
                    ins.then_inc(dve_q, 1)
                    dve.wait_ge(dve_q, QL * n + k)

                def o(k, ins):
                    ins.then_inc(dve_o, 1)
                    dve.wait_ge(dve_o, OL * m + k)

                def norm(bank):
                    if "o" in kinds and bank == 0:
                        dve.wait_ge(os_ld[p], 8 * (m - p) + 16)
                    dve.wait_ge(pv_ready, 2 * v + (bank + 1))
                    src = bankO[bank][:, 0:4 * GH * VC].rearrange("p (t j d) -> p t j d", t=4, d=VC)
                    r = rec[:, bank, :].rearrange("p (t j) -> p t j", t=4)
                    dve.reciprocal(r, src[:, :, :, HD]).then_inc(dve_p, 1)
                    dve.wait_ge(dve_p, 2 * v + (bank + 1))
                    aside(dve)
                    dst = Oat[:, ds(8 * ((v // 4) % 2) + 4 * bank, 4), ds(GW * (v % 4), GW)].rearrange("p t (j d) -> p t j d", d=HD)
                    dve.tensor_tensor(dst, src[:, :, :, 0:HD], r.unsqueeze(3).to_broadcast([P, 4, GH, HD]), ALU.mult).then_inc(pv_norm, 1)

                if "u" in kinds:
                    aside(dve)
                    for t in range(TT):
                        last = dve.bn_stats(xstat[:, t, :], X1[:, ds(2 * n + t, 1), :].rearrange("p o d -> p (o d)"))
                    q(1, last)
                    aside(dve)
                    for t in range(TT):
                        last = dve.bn_aggr(xmv[:, t, :], xstat[:, t, :])
                    q(2, last)
                    q(3, dve.tensor_scalar(qeps[:, :], xmv[:, :, 1], EPS, EPS, ALU.add, ALU.mult))
                if "o" in kinds:
                    dve.wait_ge(y_ready, m + 1)
                    aside(dve)
                    xr = X1[:, ds(2 * m, TT), :]
                    o(1, dve.tensor_tensor(xr, xr, bankR[:, :].rearrange("p (t d) -> p t d", t=TT), ALU.add))
                    o(2, dve.tensor_tensor(xr, xr, bp_sb[:, :].unsqueeze(1).to_broadcast([P, TT, D]), ALU.add))
                    aside(dve)
                    for t in range(TT):
                        last = dve.bn_stats(ostat[:, t, :], X1[:, ds(2 * m + t, 1), :].rearrange("p o d -> p (o d)"))
                    o(3, last)
                    aside(dve)
                    for t in range(TT):
                        last = dve.bn_aggr(omv[:, t, :], ostat[:, t, :])
                    o(4, last)
                    dve.tensor_scalar(omv[:, :, 1], omv[:, :, 1], EPS, None, ALU.add).then_inc(ov_ready, 1)
                    dve.wait_ge(or_ready, m + 1)
                    for t in range(TT):
                        last = dve.tensor_scalar(X2[:, p, t, :], X1[:, ds(2 * m + t, 1), :].rearrange("p o d -> p (o d)"),
                                                 omv[:, t, 0:1], orr[:, t:t + 1], ALU.subtract, ALU.mult)
                    last.then_inc(x2_ready, 1)
                if "u" in kinds:
                    dve.wait_ge(sq_ready, n + 1)
                    q(4, dve.tensor_reduce(qss[:, :], sq[:, :].rearrange("p (h d) -> p h d", d=HD), AX, ALU.add))
                    for t in range(TT):
                        last = dve.tensor_scalar(qss[:, t * H:(t + 1) * H], qss[:, t * H:(t + 1) * H], 1.0 / HD,
                                                 qeps[:, t:t + 1], ALU.mult, ALU.add)
                    last.then_inc(qv_ready, 1)
                if "p" in kinds:
                    norm(0)
                if "u" in kinds:
                    dve.wait_ge(qr_ready, n + 1)
                    nqv = nq[:, :, :, :].rearrange("p t g (j d) -> p (t g j) d", d=HD)
                    q(5, dve.tensor_tensor(nqv, bankQ[:, :].rearrange("p (h d) -> p h d", d=HD),
                                           qr[:, :].unsqueeze(2).to_broadcast([P, TT * H, HD]), ALU.mult))
                    hi = qs[:, :, :, 0, :].rearrange("p t g k -> p (t g) k")
                    lo = qs[:, :, :, 1, :].rearrange("p t g k -> p (t g) k")
                    full_ = nq[:, :, :, :].rearrange("p t g k -> p (t g) k")
                    dve.tensor_copy(hi, full_).then_inc(q_hi, 1)
                    dve.wait_ge(q_hi, n + 1)
                    dve.tensor_tensor(lo, full_, hi, ALU.subtract).then_inc(qs_ready, 1)
                if "o" in kinds:
                    dve.wait_ge(lg_ready, m + 1)
                    dve.tensor_copy(LG[:, ds(2 * m, TT), :], bankR[:, 0:TT * E].rearrange("p (t e) -> p t e", e=E)).then_inc(o_done, 1)
                if "p" in kinds:
                    norm(1)
            segments(dve, body)

            def moments(k, m):
                dve.wait_ge(l_y, k + 1)
                xr = X1[:, 2 * m:2 * m + TT]
                link(dve.tensor_tensor(xr, xr, late_bank[k].rearrange("p (t d) -> p t d", t=TT), ALU.add))
                link(dve.tensor_tensor(xr, xr, bp_sb[:, :].unsqueeze(1).to_broadcast([P, TT, D]), ALU.add))
                for t in range(TT):
                    last = dve.bn_stats(ostat[:, t, :], X1[:, 2 * m + t])
                link(last)
                for t in range(TT):
                    last = dve.bn_aggr(late_mv[:, k, t, :], ostat[:, t, :])
                link(last)
                dve.tensor_scalar(late_mv[:, k, :, 1], late_mv[:, k, :, 1], EPS, None, ALU.add).then_inc(l_ov, 1)

            def rows_of(k, m):
                dve.wait_ge(l_or, k + 1)
                for t in range(TT):
                    last = dve.tensor_scalar(XR[:, 2 * m + t, 0:D], X1[:, 2 * m + t], late_mv[:, k, t, 0:1], late_r[:, k, t:t + 1],
                                             ALU.subtract, ALU.mult)
                last.then_inc(l_x2, 1)
            for k, m in enumerate(late):
                moments(k, m)
                if k >= 1:
                    rows_of(k - 1, m - 1)
            rows_of(len(late) - 1, STEPS - 1)
            for k, m in enumerate(late):
                dve.wait_ge(l_lg, k + 1)
                dve.tensor_copy(LG[:, 2 * m:2 * m + TT, :], late_bank[k][:, 0:TT * E].rearrange("p (t e) -> p t e", e=E)).then_inc(l_done, 1)

            dve.wait_ge(r_exp, 1)
            tile_of = lambda a: a.unsqueeze(2).to_broadcast([P, TILES, E])
            of_e = lambda a: a.unsqueeze(1).to_broadcast([P, TILES, E])
            link(dve.tensor_scalar(ex, ex, 1.0, None, ALU.add))
            link(dve.reciprocal(sc, ex))
            link(dve.tensor_tensor(sbias, sc, of_e(ebias), ALU.add))
            for k, oh in enumerate((oh1, oh2)):
                link(dve.tensor_reduce(small[:, 1], sbias, AX, ALU.max))
                link(dve.tensor_tensor(cand, sbias, tile_of(small[:, 1]), ALU.is_equal))
                link(dve.tensor_tensor(cand, cand, of_e(rev), ALU.mult))
                link(dve.tensor_reduce(small[:, 2 + k], cand, AX, ALU.max))
                link(dve.tensor_tensor(oh, cand, tile_of(small[:, 2 + k]), ALU.is_equal))
                link(dve.tensor_tensor(cand, oh, sc, ALU.mult))
                link(dve.tensor_reduce(small[:, 4 + k], cand, AX, ALU.add))
                if k == 0:
                    link(dve.scalar_tensor_tensor(out=sbias, in0=oh, scalar=-BIG, in1=sbias, op0=ALU.mult, op1=ALU.add))
            link(dve.tensor_tensor(cum_a, oh1, oh2, ALU.add))
            a_, b_ = cum_a, cum_b
            step_ = 1
            while step_ < TILES:
                dve.tensor_copy(b_[:, 0:step_], a_[:, 0:step_])
                link(dve.tensor_tensor(b_[:, step_:], a_[:, step_:], a_[:, 0:TILES - step_], ALU.add))
                a_, b_ = b_, a_
                step_ *= 2
            dve.tensor_copy(small[:, 0, 0:E], a_[:, TILES - 1, :]).then_inc(r_tot, 1)
            link(dve.tensor_tensor(slot, a_, oh1, ALU.subtract))
            link(dve.tensor_tensor(slot, slot, oh2, ALU.subtract))
            link(dve.tensor_tensor(small[:, 6], small[:, 4], small[:, 5], ALU.add))
            link(dve.tensor_scalar(small[:, 6], small[:, 6], 1e-20, None, ALU.add))
            link(dve.reciprocal(small[:, 7], small[:, 6]))
            for k in range(2):
                last = dve.tensor_tensor(wts[:, k], small[:, 4 + k], small[:, 7], ALU.mult)
            link(last)
            dve.wait_ge(r_sum, 1)
            n_i = small[:, 9, 0:E].bitcast(I32)
            link(dve.tensor_scalar(n_i, bankQ[:, E:2 * E], float(P - 1), None, ALU.add))
            link(dve.tensor_scalar(n_i, n_i, 7, 7, ALU.arith_shift_right, ALU.logical_shift_left))
            link(dve.tensor_copy(small[:, 10, 0:E], n_i))
            a_, b_ = small[:, 10, 0:E], small[:, 11, 0:E]
            link(dve.tensor_copy(small[:, 12, 0:E], a_))
            for step_ in (1, 2, 4):
                dve.tensor_copy(b_[:, 0:step_], a_[:, 0:step_])
                link(dve.tensor_tensor(b_[:, step_:], a_[:, step_:], a_[:, 0:E - step_], ALU.add))
                a_, b_ = b_, a_
            ends = a_
            link(dve.tensor_tensor(small[:, 12, 0:E], ends, small[:, 12, 0:E], ALU.subtract))
            link(dve.tensor_tensor(small[:, 12, 0:E], small[:, 12, 0:E], bankQ[:, 0:E], ALU.add))
            link(dve.tensor_tensor(slot, slot, of_e(small[:, 12, 0:E]), ALU.add))
            for k, oh in enumerate((oh1, oh2)):
                link(dve.tensor_tensor(cand, slot, oh, ALU.mult))
                link(dve.tensor_reduce(pos_f[:, k], cand, AX, ALU.add))
            link(dve.tensor_copy(pos, pos_f))
            link(dve.tensor_tensor(wide, tstart.unsqueeze(2).to_broadcast([P, SLOTS, E]), ends.unsqueeze(1).to_broadcast([P, SLOTS, E]), ALU.is_ge))
            link(dve.tensor_reduce(etf, wide, AX, ALU.add))
            link(dve.tensor_scalar(etf, etf, float(E - 1), None, ALU.min))
            link(dve.tensor_copy(etile, etf))
            link(dve.tensor_copy(XR[:, :, D], tokens))
            dve.tensor_scalar(XR[:, :, D + 1], small[:, 2], -1.0, float(E), ALU.mult, ALU.add).then_inc(routed, 1)

            def places(a):
                for h in range(2):
                    dve.wait_ge(f_ld["e"][h], 16 * a + 16)
                    aside(dve)
                    dve.tensor_tensor(dest_f[:, h], x_row[:, 2 * h:2 * h + 2, D + 1], etf[:, ds(4 * a + 2 * h, 2)], ALU.not_equal).then_inc(e_chain, 1)
                    dve.wait_ge(e_chain, 2 * a + (h + 1))
                    aside(dve)
                    dve.scalar_tensor_tensor(out=dest[:, ds(4 * a + 2 * h, 2)], in0=dest_f[:, h], scalar=float(B * N),
                                             in1=x_row[:, 2 * h:2 * h + 2, D], op0=ALU.mult, op1=ALU.add).then_inc(e_dst, 1)

            def ffn(kind, tiles):
                def four(a):
                    def inner(k):
                        dve.wait_ge(f_si[kind], 4 * a + (k + 1))
                        if k >= 2 or not isinstance(a, int) or a >= 1:
                            dve.wait_ge(f_ht[kind], 4 * a + (k - 1))
                        dve.tensor_tensor(h_in[:, k % 2], act_g[:, k], gate_bank(k)[:, F:2 * F], ALU.mult).then_inc(f_h[kind], 1)

                    def columns(k):
                        dve.wait_ge(f_ht[kind], 4 * a + (k + 1))
                        aside(dve)
                        dve.tensor_copy(h_col[0:FP, k], (bankQ, bankR)[k % 2][0:FP, 0:D]).then_inc(f_hc[kind], 1)

                    def result(k):
                        dve.wait_ge(f_y[kind], 4 * a + (k + 1))
                        if kind == "s":
                            aside(dve)
                            xt = X1[:, ds(4 * a + k, 1), :].rearrange("p o d -> p (o d)")
                            dve.tensor_tensor(xt, xt, down_bank(k), ALU.add).then_inc(f_yd["s"], 1)
                        else:
                            if not isinstance(a, int) or a >= 1:
                                dve.wait_ge(y_st[k], 16 * a)
                            aside(dve)
                            dve.tensor_copy(y_out[:, k], down_bank(k)).then_inc(f_yd["e"], 1)

                    inner(0)
                    inner(1)
                    columns(0)
                    inner(2)
                    columns(1)
                    result(0)
                    inner(3)
                    columns(2)
                    result(1)
                    columns(3)
                    result(2)
                    if kind == "e" and more(a, tiles):
                        places(a + 1)
                    result(3)
                if kind == "e":
                    places(0)
                quads(dve, tiles, four)
            ffn("s", TILES)
            ffn("e", SLOTS)

            for c in range(TILES // CT):
                dve.wait_ge(c_ld[c % 2], 32 * (c // 2 + 1))
                for k in range(2):
                    for t in range(CT):
                        tile = c * CT + t
                        last = dve.scalar_tensor_tensor(out=X1[:, tile, :], in0=ya[:, c % 2, k * CT + t], scalar=wts[:, k, tile:tile + 1],
                                                        in1=X1[:, tile, :], op0=ALU.mult, op1=ALU.add)
                    if k == 0:
                        last.then_inc(c_half, 1)
                        dve.wait_ge(c_half, c + 1)
                last.then_inc(c_sum, 1)


_OUT = (B, N, D)


def kernel(**inputs):
    import concourse.bacc as _bacc
    from concourse.bass_utils import run_bass_kernel_spmd as _run

    g = {k: np.asarray(v) for k, v in inputs.items()}
    a = {}
    a["x"] = g["x"].reshape(B * N, D)
    a["xT"] = np.ascontiguousarray(a["x"].T)
    c = g["ctx_1024"].transpose(2, 0, 1)
    a["ctx2T"] = np.ascontiguousarray(np.concatenate([c, c], axis=2))
    a["wq"] = np.ascontiguousarray(g["L0_xattn_Wq"].T)
    a["wkv"] = np.ascontiguousarray(np.concatenate([g["L0_xattn_Wk"].T, g["L0_xattn_Wv"].T], axis=1))
    a["wp"] = np.ascontiguousarray(g["L0_xattn_Wp"].T)
    a["bp"] = g["L0_xattn_bp"]
    a["wr"] = g["L0_ffn_W_gate_router"]
    a["ln_g"] = g["L0_xattn_ln_g"]
    a["ln_b"] = g["L0_xattn_ln_b"]
    a["centre"] = (np.eye(D) - 1.0 / D).astype(np.float32)
    a["ident"] = np.eye(P, dtype=np.float32)
    a["ident16"] = np.eye(P, dtype=np.float16)
    head = (np.arange(W)[None, :] * P + np.arange(P)[:, None]) // M
    a["mask"] = (head[:, :, None] == np.arange(GH)).astype(np.float32)
    own = (np.arange(P) // HD) % GH
    a["maskT"] = (own[:, None, None] == head.T[None]).astype(np.float16)
    cat = np.concatenate([g["L0_ffn_Wg"], g["L0_ffn_Wu"]], axis=2)
    a["wgu"] = np.ascontiguousarray(cat.transpose(1, 0, 2))
    a["wd"] = np.ascontiguousarray(g["L0_ffn_Wd"].transpose(1, 0, 2))
    a["wgu_s"] = np.concatenate([g["L0_ffn_Wg_s"], g["L0_ffn_Wu_s"]], axis=1)
    a["wd_s"] = g["L0_ffn_Wd_s"]
    a["e_bias"] = g["L0_ffn_expert_bias"]
    row = np.arange(P)
    a["tri_c"] = np.stack([row[:, None] < row[None, :], np.ones((P, P), bool)]).astype(np.float32)
    a["rev_c"] = np.tile(np.arange(E, 0, -1, dtype=np.float32), (P, 1))
    a["tok_c"] = (np.arange(TILES)[None, :] * P + row[:, None]).astype(np.float32)
    a["tst_c"] = np.tile(np.arange(SLOTS, dtype=np.float32) * P, (P, 1))
    a["fill_c"] = np.zeros((P, ROW), np.float32)
    a["fill_c"][:, D] = NOWHERE
    nc = _bacc.Bacc("TRN2", target_bir_lowering=False, num_devices=1)
    args = {n: nc.dram_tensor(f"in_{n}", v.shape, mybir.dt.from_np(v.dtype), kind="ExternalInput").ap() for n, v in a.items()}
    out = nc.dram_tensor("out", (B * N, D), F32, kind="ExternalOutput").ap()
    scratch = {n: nc.dram_tensor(n, shape, F32, kind="Internal").ap() for n, shape in (
        ("x2_rows", (B * N, D)), ("x2_cols", (STEPS, P, TT * D)), ("sorted_rows", (SLOTS, P, ROW)), ("y_rows", (2 * B * N, D)))}
    build(nc, **args, **scratch, out=out)
    r = _run(nc, [{f"in_{n}": v for n, v in a.items()}], core_ids=[0])
    return r.results[0]["out"].reshape(_OUT)
```

```python
from contextlib import ExitStack

import concourse.bass as bass
from concourse import mybir
from concourse.bass import ds
import numpy as np

F32 = mybir.dt.float32
F16 = mybir.dt.float16
I32 = mybir.dt.int32
ALU = mybir.AluOpType
ACT = mybir.ActivationFunctionType
AX = mybir.AxisListType.X

P = 128
B, N, D = 4, 1024, 256
M, H, HD = 154, 16, 16
KC = D // P
GH = 4
G = H // GH
GW = GH * HD
KT = -(-B * M // P)
W = -(-GH * M // P)
VC = HD + 1
STEPS = B * G
TT = 2
TILES = B * N // P
E, F = 8, 192
FC = 2
FP = F // FC
SLOTS = 2 * TILES + E
ROW = D + 2
SCALE = 8.0 / HD
EPS = 1e-5
GUARD = 64.0
PV_LAG, O_LAG, U_LEAD, T_LEAD = 1, 6, 5, 4
SEGMENTS = [(0, 0, "uts"), (1, 0, "utsp"), (2, 2, "utsp"), (6, 2, "utspo"), (10, 0, "utspo"), (11, 0, "tspo"),
            (12, 2, "spo"), (16, 0, "po")]
EARLY = U_LEAD
LATE = 11
SORTED = SLOTS * P
NOWHERE = 1 << 15
BIG = 1e30
CT = 4
CS = 4


def segments(eng, body):
    for first, pairs, kinds in SEGMENTS:
        if pairs == 0:
            body(first, first % 2, kinds)
        else:
            with eng.Fori(0, pairs) as i:
                for p in range(2):
                    body(2 * i + (first + p), p, kinds)


def quads(eng, tiles, body):
    body(0)
    with eng.Fori(1, tiles // 4 - 1) as a:
        body(a)
    body(tiles // 4 - 1)


def more(a, tiles):
    return not (isinstance(a, int) and a == tiles // 4 - 1)


def build(nc, x, xT, ctx2T, wq, wkv, keysT, wp, bp, ln_g, ln_b, centre, ident, ident16, mask, own, wr, wgu, wd, wgu_s, wd_s, e_bias,
          tri_c, rev_c, tok_c, tst_c, fill_c,
          x2_rows, x2_cols, sorted_rows, y_rows, out):
    ctx = ExitStack()
    with ctx:
        def sb(name, shape, dt=F32):
            return ctx.enter_context(nc.sbuf_tensor(name, shape, dt))

        def ps(name, shape, dt=F32):
            return ctx.enter_context(nc.psum_tensor(name, shape, dt))

        def sem(name):
            return ctx.enter_context(nc.semaphore(name))

        id32 = sb("id32", [P, P])
        id16 = sb("id16", [P, P], F16)
        msk = sb("msk", [P, W, GH])
        own_sb = sb("own_sb", [P, GH])
        wq_sb = sb("wq_sb", [P, KC, D])
        wp_sb = sb("wp_sb", [P, KC, D])
        wr_sb = sb("wr_sb", [P, KC, E])
        bp_sb = sb("bp_sb", [P, D])
        gb = sb("gb", [P, 2, HD])
        hmean = sb("hmean", [P, KC, 2, H])
        guard = sb("guard", [P, 10])
        KB = sb("KB", [P, STEPS, 2, W * P], F16)
        VB = sb("VB", [P, STEPS, W, GH * VC])
        x_in = sb("x_in", [P, 2, KC, TT * P])
        X1 = sb("X1", [P, TILES, D])
        xstat = sb("xstat", [P, TT, 6])
        xmv = sb("xmv", [P, TT, 2])
        qeps = sb("qeps", [P, TT])
        sq = sb("sq", [P, TT * D])
        qss = sb("qss", [P, TT * H])
        qln = sb("qln", [P, TT * H])
        qr = sb("qr", [P, TT * H])
        nq = sb("nq", [P, TT, G, GW])
        qs = sb("qs", [P, TT, G, 2, GW], F16)
        qT = sb("qT", [P, 2, G, N], F16)
        Pb = sb("Pb", [P, 2, W, N])
        scr = Pb[:, :, :, :].rearrange("p a c n -> p (a c n)")
        sizes = [KT * D, KT * D, 2 * KT * D, KC * D, KC * D, 2 * KC * D, KC * KT * P, KT * H, KT * H, KT * H, 2 * HD, 2 * TT * D, 2 * TT * H,
                 2 * TT * H, 2 * TT * H, EARLY * TT * 6, EARLY * TT * 2, EARLY * TT]
        part = [scr[:, sum(sizes[:i]):sum(sizes[:i + 1])] for i in range(len(sizes))]
        khat, ktmp = (x_.rearrange("p (r d) -> p r d", d=HD) for x_ in part[:2])
        khl = part[2].bitcast(F16).rearrange("p (l t g a e) -> p l t g a e", l=2, t=KT, g=G, a=2)
        cen, wq_raw, wkv_sb, k_x = (x_.rearrange("p (k n) -> p k n", k=KC) for x_ in part[3:7])
        kss, kln, kr = part[7:10]
        gcoef = part[10].rearrange("p (a d) -> p a d", a=2)
        e_sq, e_ss, e_ln, e_r = (x_.rearrange("p (a n) -> p a n", a=2) for x_ in part[11:15])
        e_stat, e_mv = (x_.rearrange("p (t n) -> p t n", t=EARLY * TT) for x_ in part[15:17])
        e_eps = part[17]
        shift = guard[:, 9:10]
        rec = sb("rec", [P, 2, 4 * GH])
        Oat = sb("Oat", [P, 2 * N // P, D])
        c_x = Oat[:, :, :].rearrange("p t r -> p (t r)")[:, 0:KC * B * 2 * M].rearrange("p (k b m) -> p k b m", k=KC, b=B)
        OS = sb("OS", [P, 2, TT, D])
        OT = sb("OT", [P, TT * D])
        ostat = sb("ostat", [P, TT, 6])
        omv = sb("omv", [P, TT, 2])
        X2 = sb("X2", [P, 2, TT, D])
        X2T = sb("X2T", [P, 2, TT * D])
        LG = sb("LG", [P, TILES, E])
        oln = sb("oln", [P, TT])
        late_mv = sb("late_mv", [P, STEPS - LATE, TT, 2])
        late_r = sb("late_r", [P, STEPS - LATE, TT])
        orr = sb("orr", [P, TT])

        def views(memory, *shapes):
            at, out_ = 0, []
            for shape in shapes:
                n_ = int(np.prod(shape))
                v_ = memory[:, at:at + n_]
                if len(shape) == 2:
                    v_ = v_.rearrange("p (a b) -> p a b", a=shape[0])
                if len(shape) == 3:
                    v_ = v_.rearrange("p (a b c) -> p a b c", a=shape[0], b=shape[1])
                out_.append(v_)
                at += n_
            return out_

        probs = Pb[:, :, :, :].rearrange("p a c n -> p (a c n)")
        wgu_sb, wd_sb = views(probs, (KC, E, 2 * F), (FC, E, D))
        ya, = views(probs, (CS, 2 * CT, D))
        keys = KB[:, :, :, :].rearrange("p a b c -> p (a b c)").bitcast(F32)
        XR, wgus_sb = views(keys, (TILES, ROW), (KC, 2 * F))
        vals = VB[:, :, :, :].rearrange("p a b c -> p (a b c)")
        (tri, ones, ebias, rev, tokens, tstart, ex, sc, sbias, cand, oh1, oh2, cum_a, cum_b, slot, small, etf, wts, pos_f, etile, pos,
         wide) = views(vals, (P,), (P,), (E,), (E,), (TILES,), (SLOTS,), *[(TILES, E)] * 9, (16, TILES), (SLOTS,), (2, TILES),
                       (2, TILES), (SLOTS,), (2, TILES), (SLOTS, E))
        etile = etile.bitcast(I32)
        pos = pos.bitcast(I32)
        qmem = qT[:, :, :, :].rearrange("p a g n -> p (a g n)").bitcast(F32)
        wds_sb, x_col, act_g, h_in, h_col = views(qmem, (FC, D), (4, D), (4, F), (2, F), (4, D))
        x_row, y_out, dest_f, dest = views(Oat[:, :, :].rearrange("p t r -> p (t r)"), (4, ROW), (4, D), (2, 2), (SLOTS,))
        dest = dest.bitcast(I32)
        empty = X2[:, 0, :, :].rearrange("p t d -> p (t d)")[:, 0:ROW]

        bankS = [ps(f"bankS{i}", [P, N]) for i in range(2)]
        bankO = [ps(f"bankO{i}", [P, 512]) for i in range(2)]
        bankQ = ps("bankQ", [P, 512])
        bankR = ps("bankR", [P, 512])

        kv_in = sem("kv_in")
        kx_in = sem("kx_in")
        v_in = sem("v_in")
        x_early = [sem(f"x_early{n}") for n in range(EARLY)]
        wq_in = sem("wq_in")
        g_in = sem("g_in")
        c_in = sem("c_in")
        x_rows = [sem(f"x_rows{b}") for b in range(B)]
        x_ld = [sem("x_ld0"), sem("x_ld1")]
        wq_c = sem("wq_c")
        w_h = sem("w_h")
        v_rd = sem("v_rd")
        v_used = sem("v_used")
        v_ones = sem("v_ones")
        k_rd = sem("k_rd")
        k_sq = sem("k_sq")
        k_ss = sem("k_ss")
        k_ln = sem("k_ln")
        k_r = sem("k_r")
        k_norm = sem("k_norm")
        k_fin = sem("k_fin")
        k_hl = sem("k_hl")
        kt_rd = sem("kt_rd")
        kb_dve = sem("kb_dve")
        kb_act = sem("kb_act")
        kb_pad = sem("kb_pad")
        gu_in = sem("gu_in")
        gu_ln = sem("gu_ln")
        gu_rt = sem("gu_rt")
        k_u = sem("k_u")
        u_all = sem("u_all")
        guarded = sem("guarded")
        pre = sem("pre")
        u_ready = sem("u_ready")
        sq_ready = sem("sq_ready")
        qv_ready = sem("qv_ready")
        qr_ready = sem("qr_ready")
        qs_ready = sem("qs_ready")
        qt_ready = sem("qt_ready")
        q_done = sem("q_done")
        act_q = sem("act_q")
        act_o = sem("act_o")
        dve_q = sem("dve_q")
        dve_p = sem("dve_p")
        dve_o = sem("dve_o")
        s_ready = sem("s_ready")
        exp_done = sem("exp_done")
        pv_ready = sem("pv_ready")
        pv_norm = sem("pv_norm")
        os_ld = [sem("os_ld0"), sem("os_ld1")]
        ot_ready = sem("ot_ready")
        ot_sb = sem("ot_sb")
        y_ready = sem("y_ready")
        ov_ready = sem("ov_ready")
        or_ready = sem("or_ready")
        o_done = sem("o_done")
        x2_ready = sem("x2_ready")
        x2t_ready = sem("x2t_ready")
        x2t_sb = sem("x2t_sb")
        lg_ready = sem("lg_ready")
        x2_st = [sem("x2_st0"), sem("x2_st1")]
        x2t_st = [sem("x2t_st0"), sem("x2t_st1")]
        s_out = sem("s_out")
        filled = sem("filled")
        fill_in = sem("fill_in")
        aside_n = {e_.engine: sem(f"aside{n_}") for n_, e_ in enumerate((nc.sync, nc.scalar, nc.vector))}
        r_in = sem("r_in")
        ws_in = sem("ws_in")
        w_in = sem("w_in")
        lx_st = sem("lx_st")
        xr_in = sem("xr_in")
        r_exp = sem("r_exp")
        r_tot = sem("r_tot")
        r_sum = sem("r_sum")
        routed = sem("routed")
        scat = [sem(f"scat{i}") for i in range(4)]
        kinds_ = ("s", "e")
        l_ot, l_os, l_y, l_ov, l_ln, l_or, l_x2, l_xt, l_xs, l_lg, l_done = (
            sem("l_" + n_) for n_ in ("ot", "os", "y", "ov", "ln", "or", "x2", "xt", "xs", "lg", "done"))
        l_bias = sem("l_bias")
        q_hi = sem("q_hi")
        f_ld = {k: [sem(f"{k}_ld{i}") for i in range(2)] for k in kinds_}
        f_xt, f_xc, f_gu, f_si, f_h, f_ht, f_hc, f_y, f_yd = (
            {k: sem(f"{k}_{n_}") for k in kinds_} for n_ in ("xt", "xc", "gu", "si", "h", "ht", "hc", "y", "yd"))
        e_dst = sem("e_dst")
        e_chain = sem("e_chain")
        y_st = [sem(f"y_st{i}") for i in range(4)]
        c_ld = [sem(f"c_ld{i}") for i in range(CS)]
        c_half = sem("c_half")
        c_sum = sem("c_sum")

        def gate_bank(k):
            return bankS[0][:, (k % 2) * 512:(k % 2) * 512 + 512]

        def down_bank(k):
            return bankS[1][:, (k % 2) * 512:(k % 2) * 512 + D]

        late = range(LATE, STEPS)
        late_bank = [bankS[0][:, 0:512], bankS[0][:, 512:], bankS[1][:, 0:512], bankS[1][:, 512:], bankQ[:, :]]
        slot_of = lambda a, k: a[:, k].rearrange("p t d -> p (t d)")
        late_ot = [slot_of(OS, 0), slot_of(OS, 1), OT[:, :], slot_of(X2, 0), slot_of(X2, 1)]
        late_x2t = [x_in[:, 0].rearrange("p k t -> p (k t)"), x_in[:, 1].rearrange("p k t -> p (k t)"), sq[:, :],
                    nq[:, :, :, :].rearrange("p t g k -> p (t g k)"), X2T[:, 1, :]]

        block = ctx.enter_context(nc.Block())

        def aside(eng):
            eng.sem_inc(aside_n[eng.engine], 1)

        starts = [(c * P) % M for c in range(W)]
        v_pairs = [(b, c) for c in range(W) for b in (0, 2)]
        turn_bank = [bankO[0], bankO[1], bankS[1][:, 0:512]]
        value_bank = [bankR, bankS[0][:, 0:512], bankS[0][:, 512:]]
        flat = lambda a: a.rearrange("p t d -> p (t d)")
        early_x = [a.rearrange("p (k t) -> p k t", k=KC) for a in (
            flat(x_in[:, 0]), flat(x_in[:, 1]), flat(OS[:, 0]), flat(OS[:, 1]), OT[:, :])]
        early_bank = [bankQ[:, :], bankS[1][:, 512:]]
        halves = [(hl, g) for hl in range(2) for g in range(G)]
        key_bank = [bankS[0][:, :], bankS[1][:, 0:D]]

        @block.sync
        def _(sp):
            for k in range(KC):
                sp.dma_start(wkv_sb[:, k], wkv[k * P:(k + 1) * P]).then_inc(kv_in, 16)
            for dst, src in ((cen[:], centre), (wq_raw[:], wq)):
                sp.dma_start(dst, src.rearrange("(k p) n -> p k n", p=P)).then_inc(wq_in, 16)
            for k in range(KC):
                sp.dma_start(k_x[:, k], keysT[k * P:(k + 1) * P]).then_inc(kx_in, 16)
            for dst, src in ((gb[:, 0, :], ln_g.partition_broadcast(P)), (gb[:, 1, :], ln_b.partition_broadcast(P)),
                             (msk[:], mask), (own_sb[:], own), (id16[:], ident16)):
                sp.dma_start(dst, src).then_inc(g_in, 16)
            sp.dma_start(X1[:, 0:8, :], x[0:N, :].rearrange("(t p) d -> p t d", p=P)).then_inc(x_rows[0], 16)
            sp.dma_start(c_x[:], ctx2T.rearrange("(k p) b m -> p k b m", p=P)).then_inc(v_in, 16)
            for b in range(1, B):
                sp.dma_start(X1[:, b * 8:(b + 1) * 8, :],
                             x[b * N:(b + 1) * N, :].rearrange("(t p) d -> p t d", p=P)).then_inc(x_rows[b], 16)
            for dst, src in ((bp_sb[:], bp.partition_broadcast(P)), (id32[:], ident), (wp_sb[:], wp.rearrange("(k p) n -> p k n", p=P)),
                             (wr_sb[:], wr.rearrange("(k p) n -> p k n", p=P))):
                sp.dma_start(dst, src).then_inc(c_in, 16)

            def outputs_in(n, p):
                sp.wait_ge(pv_norm, 2 * n + 8)
                aside(sp)
                if not isinstance(n, int) or n >= 2:
                    sp.wait_ge(ot_ready, n - 1)
                    aside(sp)
                    sp.wait_ge(x2_st[p], 8 * (n - p))
                    aside(sp)
                    sp.wait_ge(x2t_st[p], 8 * (n - p))
                aside(sp)
                sp.dma_start(OS[:, p, :, :], Oat[:, ds((2 * n) % 16, TT), :]).then_inc(os_ld[p], 16)

            def store(m, p):
                sp.wait_ge(x2_ready, m + 1)
                aside(sp)
                sp.dma_start(x2_rows.rearrange("(t p) d -> p t d", p=P)[:, ds(2 * m, TT), :], X2[:, p, :, :]).then_inc(x2_st[p], 16)
                sp.wait_ge(x2t_sb, m + 1)
                aside(sp)
                sp.dma_start(x2_cols[ds(m, 1), :, :].rearrange("o p t -> p (o t)"), X2T[:, p, :]).then_inc(x2t_st[p], 16)

            sp.wait_ge(filled, 16)
            outputs_in(0, 0)
            outputs_in(1, 1)
            store(0, 0)
            with sp.Fori(1, LATE // 2) as i:
                for p in range(2):
                    outputs_in(2 * i + p, p)
                    store(2 * i + (p - 1), 1 - p)
            outputs_in(LATE - 1, (LATE - 1) % 2)
            store(LATE - 2, LATE % 2)
            store(LATE - 1, 1 - LATE % 2)
            sp.wait_ge(s_ready, W * STEPS)
            for p in range(2):
                sp.wait_ge(x2_st[p], 16 * ((LATE + 1 - p) // 2))
            sp.dma_start(XR[:, 0:TT * LATE, 0:D], x2_rows.rearrange("(t p) d -> p t d", p=P)[:, 0:TT * LATE]).then_inc(xr_in, 16)
            sp.wait_ge(pv_ready, 2 * STEPS)
            for dst, src in ((tri, tri_c[0]), (ones, tri_c[1]), (ebias, e_bias.partition_broadcast(P)), (rev, rev_c), (tokens, tok_c),
                             (tstart, tst_c)):
                sp.dma_start(dst, src).then_inc(r_in, 16)
            for dst, src in ((wgus_sb, wgu_s.rearrange("(k p) f -> p k f", p=P)), (wds_sb[0:FP], wd_s.rearrange("(k p) d -> p k d", p=FP))):
                sp.dma_start(dst, src).then_inc(ws_in, 16)
            for k, m in enumerate(late):
                sp.wait_ge(l_xs, k + 1)
                sp.dma_start(x2_cols[m], late_x2t[k]).then_inc(lx_st, 16)
            for k in range(KC):
                sp.dma_start(wgu_sb[:, k], wgu[k * P:(k + 1) * P]).then_inc(w_in, 16)
            for k in range(FC):
                sp.dma_start(wd_sb[0:FP, k], wd[k * FP:(k + 1) * FP]).then_inc(w_in, 16)
            for p in range(2):
                sp.wait_ge(x2t_st[p], 16 * ((LATE + 1 - p) // 2))
            sp.wait_ge(lx_st, 16 * len(late))

            def load_shared(a):
                for h in range(2):
                    if not isinstance(a, int) or a >= 1:
                        sp.wait_ge(f_gu["s"], 4 * a + (2 * h - 2))
                    aside(sp)
                    sp.dma_start(x_col[:, 2 * h:2 * h + 2], x2_cols[ds(2 * a + h, 1), :, :].rearrange("o p (t c) -> p (o t) c", t=2)) \
                        .then_inc(f_ld["s"][h], 16)
            quads(sp, TILES, load_shared)

            for i in range(4):
                sp.wait_ge(scat[i], 16 * (2 * TILES // 4))

            def load_rows(a):
                for h in range(2):
                    if not isinstance(a, int) or a >= 1:
                        sp.wait_ge(f_xt["e"], 2 * a + (h - 1))
                        sp.wait_ge(e_dst, 2 * a + (h - 1))
                    aside(sp)
                    sp.dma_start(x_row[:, 2 * h:2 * h + 2], sorted_rows[ds(4 * a + 2 * h, 2), :, :].rearrange("t p r -> p t r")) \
                        .then_inc(f_ld["e"][h], 16)
            quads(sp, SLOTS, load_rows)

            for i in range(4):
                sp.wait_ge(y_st[i], 4 * SLOTS)
            y_t = y_rows.rearrange("(k t p) d -> p k t d", k=2, p=P)
            for c in range(TILES // CT):
                if c >= CS:
                    sp.wait_ge(c_sum, c - CS + 1)
                for k in range(2):
                    sp.dma_start(ya[:, c % CS, k * CT:(k + 1) * CT], y_t[:, k, c * CT:(c + 1) * CT]).then_inc(c_ld[c % CS], 16)
            sp.wait_ge(s_out, 16 * (TILES // CT))

        @block.gpsimd
        def _(pool):
            for n in range(EARLY):
                pool.dma_start(early_x[n], xT.rearrange("(k p) t -> p k t", p=P)[:, :, 256 * n:256 * (n + 1)]).then_inc(x_early[n], 16)
            pool.memset(KB[:, :, :, GH * M:], 0.0).then_inc(kb_pad, 1)
            pool.dma_start(empty, fill_c).then_inc(fill_in, 16)
            pool.wait_ge(fill_in, 16)
            pool.dma_start(sorted_rows.rearrange("s p r -> p s r"), empty.unsqueeze(1).to_broadcast([P, SLOTS, ROW])).then_inc(filled, 16)

            def load(n, p):
                pool.dma_start(x_in[:, p, :, :], xT.rearrange("(k p) t -> p k t", p=P)[:, :, ds(256 * n, 256)]).then_inc(x_ld[p], 16)
            pool.wait_ge(u_ready, 2)
            load(EARLY, 1)
            load(EARLY + 1, 0)
            pool.wait_ge(k_fin, 1)
            keys4 = khat.rearrange("p (t g j) d -> p t g (j d)", t=KT, g=G)
            for a_ in range(2):
                pool.wait_ge(k_hl, a_ + 1)
                last = pool.tensor_tensor(khl[:, 1, :, :, a_, :], keys4, khl[:, 0, :, :, a_, :], ALU.subtract)
            last.then_inc(k_hl, 2)
            pool.wait_ge(k_u, 1)
            pool.partition_all_reduce(guard[:, 3:4], guard[:, 1:2], P, bass.bass_isa.ReduceOp.max).then_inc(u_all, 1)
            with pool.Fori(0, (STEPS - EARLY - 2) // 2) as i:
                for k in range(2):
                    pool.wait_ge(u_ready, 2 * i + (EARLY + 1 + k))
                    load(2 * i + (EARLY + 2 + k), 1 - k)
            pool.wait_ge(u_ready, STEPS - 2)
            load(STEPS - 1, (STEPS - 1) % 2)
            pool.wait_ge(qv_ready, STEPS)
            pool.wait_ge(c_in, 16 * 4)
            pool.tensor_tensor(X1[:, TT * LATE:], X1[:, TT * LATE:], bp_sb[:, :].unsqueeze(1).to_broadcast([P, TILES - TT * LATE, D]), ALU.add) \
                .then_inc(l_bias, 1)
            pool.wait_ge(xr_in, 16)
            pool.wait_ge(l_x2, len(late))
            pool.wait_ge(filled, 16)
            pool.wait_ge(routed, 1)
            for n in range(2 * TILES):
                t, k = divmod(n, 2)
                pool.indirect_dma_start(sorted_rows.rearrange("s p r -> (s p) r"), bass.IndirectOffsetOnAxis(ap=pos[:, k, t:t + 1], axis=0),
                                        XR[:, t, :], None, bounds_check=SORTED - 1, oob_is_err=False).then_inc(scat[n % 4], 16)
            for i in range(SLOTS):
                pool.wait_ge(f_yd["e"], i + 1)
                pool.indirect_dma_start(y_rows, bass.IndirectOffsetOnAxis(ap=dest[:, i:i + 1], axis=0),
                                        y_out[:, i % 4], None, bounds_check=2 * B * N - 1, oob_is_err=False).then_inc(y_st[i % 4], 16)

        @block.scalar
        def _(act):
            act.preload_act_table_set("natural_log_exp_and_others")
            act.wait_ge(k_rd, 1)
            for bank, rows in zip(key_bank, (ktmp[:, 0:4 * H, :], ktmp[:, 4 * H:, :])):
                act.activation(rows.rearrange("p r d -> p (r d)"), bank, ACT.Square).then_inc(k_sq, 1)
            act.wait_ge(k_ss, 1)
            act.activation(kln, kss, ACT.Ln).then_inc(k_ln, 1)
            act.wait_ge(k_ln, 1)
            act.activation(kr, kln, ACT.Exp, scale=-0.5).then_inc(k_r, 1)
            act.wait_ge(k_fin, 1)
            keys4 = khat.rearrange("p (t g j) d -> p t g (j d)", t=KT, g=G)
            for a_ in range(2):
                act.activation(khl[:, 0, :, :, a_, :], keys4, ACT.Copy).then_inc(k_hl, 1)
            act.activation(ktmp.rearrange("p r d -> p (r d)"), khat.rearrange("p r d -> p (r d)"), ACT.Square).then_inc(k_sq, 1)

            def squares(n):
                act.wait_ge(u_ready, n + 1)
                act.activation(e_sq[:, n % 2], early_bank[n % 2], ACT.Square).then_inc(sq_ready, 1)

            def roots(n):
                act.wait_ge(qv_ready, n + 1)
                act.activation(e_ln[:, n % 2], e_ss[:, n % 2], ACT.Ln).then_inc(act_q, 1)
                act.wait_ge(act_q, n + 1)
                act.activation(e_r[:, n % 2], e_ln[:, n % 2], ACT.Exp, scale=-0.5).then_inc(qr_ready, 1)

            def columns_out(n):
                act.wait_ge(qt_ready, n + 1)
                act.activation(qT[:, 0, :, 256 * n:256 * (n + 1)], early_bank[n % 2].bitcast(F16).rearrange("p (g t) -> p g t", g=G),
                               ACT.Copy).then_inc(q_done, 1)

            def spread(i):
                hl, g = halves[i]
                act.wait_ge(kt_rd, i + 1)
                for j in range(GH):
                    last = act.activation(KB[:, :, hl, j * M:(j + 1) * M].rearrange("p (b g) m -> p b g m", g=G)[:, :, g, :],
                                          turn_bank[i % 3].bitcast(F16)[:, 0:B * M].rearrange("p (b m) -> p b m", b=B),
                                          ACT.Copy, scale=own_sb[:, j:j + 1])
                last.then_inc(kb_act, 1)

            squares(0)
            squares(1)
            roots(0)
            roots(1)
            act.wait_ge(g_in, 16 * 5)
            spread(1)
            spread(3)
            columns_out(0)
            squares(2)
            columns_out(1)
            squares(3)
            roots(2)
            act.wait_ge(gu_in, 1)
            act.activation(guard[:, 3:6], guard[:, 0:3], ACT.Ln).then_inc(gu_ln, 1)
            act.wait_ge(gu_ln, 1)
            act.activation(guard[:, 6:9], guard[:, 3:6], ACT.Exp, scale=0.5).then_inc(gu_rt, 1)
            spread(5)
            spread(7)
            roots(3)
            columns_out(2)
            squares(4)
            roots(4)
            columns_out(3)

            def body(s, p, kinds):
                n, tn, m = s + U_LEAD, s + T_LEAD, s - O_LAG

                def exp(s, p, c):
                    act.wait_ge(s_ready, 5 * s + (c + 1))
                    act.activation(Pb[:, p, c, :], bankS[(p + c) % 2][:, :], ACT.Exp, bias=shift).then_inc(exp_done, 1)

                if "o" in kinds:
                    act.wait_ge(ot_ready, m + 1)
                    act.activation(OT[:, :], bankR[:, :], ACT.Copy).then_inc(ot_sb, 1)
                if "p" in kinds:
                    exp(s - 1, 1 - p, W - 1)
                if "s" in kinds:
                    if isinstance(s, int) and s == 0:
                        act.wait_ge(guarded, 1)
                    exp(s, p, 0)
                if "t" in kinds:
                    act.wait_ge(qt_ready, tn + 1)
                    aside(act)
                    act.activation(qT[:, ds((tn // 4) % 2, 1), :, ds(256 * (tn % 4), 256)],
                                   bankQ[:, :].bitcast(F16).rearrange("p (o g t) -> p o g t", o=1, g=G), ACT.Copy).then_inc(q_done, 1)
                if "s" in kinds:
                    exp(s, p, 1)
                if "o" in kinds:
                    act.wait_ge(ov_ready, m + 1)
                    act.activation(oln[:, :], omv[:, :, 1], ACT.Ln).then_inc(act_o, 1)
                    act.wait_ge(act_o, m + 1)
                    act.activation(orr[:, :], oln[:, :], ACT.Exp, scale=-0.5).then_inc(or_ready, 1)
                if "u" in kinds:
                    act.wait_ge(u_ready, n + 1)
                    act.activation(sq[:, :], bankQ[:, :], ACT.Square).then_inc(sq_ready, 1)
                    act.wait_ge(qv_ready, n + 1)
                    act.activation(qln[:, :], qss[:, :], ACT.Ln).then_inc(act_q, 1)
                    act.wait_ge(act_q, n + 1)
                    act.activation(qr[:, :], qln[:, :], ACT.Exp, scale=-0.5).then_inc(qr_ready, 1)
                if "s" in kinds:
                    exp(s, p, 2)
                if "o" in kinds:
                    act.wait_ge(x2t_ready, m + 1)
                    act.activation(X2T[:, p, :], bankR[:, :], ACT.Copy).then_inc(x2t_sb, 1)
                if "s" in kinds:
                    exp(s, p, 3)
            segments(act, body)

            for k, m in enumerate(late):
                act.wait_ge(l_ot, k + 1)
                if k == 2:
                    act.wait_ge(y_ready, LATE)
                if k == 3:
                    for p in range(2):
                        act.wait_ge(x2_st[p], 16 * ((LATE + 1 - p) // 2))
                act.activation(late_ot[k], late_bank[k], ACT.Copy).then_inc(l_os, 1)
            for k, m in enumerate(late):
                act.wait_ge(l_ov, k + 1)
                act.activation(late_r[:, k], late_mv[:, k, :, 1], ACT.Ln).then_inc(l_ln, 1)
                act.wait_ge(l_ln, k + 1)
                act.activation(late_r[:, k], late_r[:, k], ACT.Exp, scale=-0.5).then_inc(l_or, 1)
                if k >= 1:
                    act.wait_ge(l_xt, k)
                    act.activation(late_x2t[k - 1], late_bank[k - 1], ACT.Copy).then_inc(l_xs, 1)
            act.wait_ge(x2t_st[1], 16 * (LATE // 2))
            act.wait_ge(l_xt, len(late))
            act.activation(late_x2t[-1], late_bank[-1], ACT.Copy).then_inc(l_xs, 1)
            act.wait_ge(o_done, LATE)
            act.wait_ge(l_done, len(late))
            act.wait_ge(r_in, 16 * 6)
            act.activation(ex[:], LG[:], ACT.Exp, scale=-1.0).then_inc(r_exp, 1)

            def columns(a):
                for h in range(2):
                    act.wait_ge(f_xt["e"], 2 * a + (h + 1))
                    act.activation(x_col[:, 2 * h:2 * h + 2], bankO[h][:, :].rearrange("p (t c) -> p t c", t=2), ACT.Copy) \
                        .then_inc(f_xc["e"], 1)

            def ffn(kind, tiles):
                def gates(a):
                    for k in range(4):
                        act.wait_ge(f_gu[kind], 4 * a + (k + 1))
                        if not isinstance(a, int) or a >= 1:
                            act.wait_ge(f_h[kind], 4 * a + (k - 3))
                        act.activation(act_g[:, k], gate_bank(k)[:, 0:F], ACT.Silu).then_inc(f_si[kind], 1)
                    if kind == "e" and more(a, tiles):
                        columns(a + 1)
                if kind == "e":
                    columns(0)
                quads(act, tiles, gates)
            ffn("s", TILES)
            ffn("e", SLOTS)

            for c in range(TILES // CT):
                act.wait_ge(c_sum, c + 1)
                act.dma_start(out.rearrange("(t p) d -> p t d", p=P)[:, c * CT:(c + 1) * CT], X1[:, c * CT:(c + 1) * CT]).then_inc(s_out, 16)

        @block.tensor
        def _(pe):
            def values(i):
                b, c = v_pairs[i]
                if i >= 3:
                    pe.wait_ge(v_used, i - 2)
                elif i >= 1:
                    pe.wait_ge(k_norm, 1)
                for t in range(2):
                    for k in range(KC):
                        last = pe.matmul(value_bank[i % 3][:, t * D:(t + 1) * D], c_x[:, k, b + t, starts[c]:starts[c] + P],
                                         wkv_sb[:, k, D:2 * D], start=(k == 0), stop=(k == KC - 1))
                last.then_inc(v_rd, 1)

            def turned_keys(i):
                hl, g = halves[i]
                pe.wait_ge(k_hl, 2 * hl + 2)
                if i >= 3:
                    pe.wait_ge((kb_dve, kb_act)[(i - 3) % 2], (i - 3) // 2 + 1)
                for t in range(KT):
                    last = pe.transpose(turn_bank[i % 3].bitcast(F16)[:, t * P:(t + 1) * P],
                                        khl[:, hl, t, g].rearrange("p a e -> p (a e)"), id16[:, :])
                last.then_inc(kt_rd, 1)

            def project(n):
                pe.wait_ge(x_early[n], 16)
                if n >= 2:
                    pe.wait_ge(q_done, n - 1)
                for t in range(TT):
                    for k in range(KC):
                        last = pe.matmul(early_bank[n % 2][:, t * D:(t + 1) * D], early_x[n][:, k, t * P:(t + 1) * P], wq_sb[:, k, :],
                                         start=(k == 0), stop=(k == KC - 1))
                last.then_inc(u_ready, 1)

            def turned_queries(bank, n):
                pe.wait_ge(qs_ready, n + 1)
                for g in range(G):
                    for t in range(TT):
                        last = pe.transpose(bank.bitcast(F16)[:, g * 256 + t * P:g * 256 + (t + 1) * P],
                                            qs[:, t, g, :, :].rearrange("p a b -> p (a b)"), id16[:, :])
                last.then_inc(qt_ready, 1)

            pe.wait_ge(wq_in, 16 * 2)
            for mt in range(KC):
                for k in range(KC):
                    last = pe.matmul(bankQ[:, mt * D:(mt + 1) * D], cen[:, k, mt * P:(mt + 1) * P], wq_raw[:, k, :],
                                     start=(k == 0), stop=(k == KC - 1))
            last.then_inc(wq_c, 1)
            pe.wait_ge(kx_in, 16 * 2)
            pe.wait_ge(w_h, 1)
            for t in range(KT):
                for k in range(KC):
                    last = pe.matmul(bankS[t // 4][:, (t % 4) * D:(t % 4 + 1) * D], k_x[:, k, t * P:(t + 1) * P], wkv_sb[:, k, 0:D],
                                     start=(k == 0), stop=(k == KC - 1))
            last.then_inc(k_rd, 1)
            pe.wait_ge(w_h, 2)
            project(0)
            project(1)
            pe.wait_ge(v_in, 16)
            values(0)
            values(1)
            values(2)
            pe.wait_ge(g_in, 16 * 5)
            for i in range(4):
                turned_keys(i)
            values(3)
            values(4)
            turned_queries(early_bank[0], 0)
            project(2)
            values(5)
            turned_queries(early_bank[1], 1)
            project(3)
            values(6)
            for i in range(4, 8):
                turned_keys(i)
            values(7)
            turned_queries(early_bank[0], 2)
            project(4)
            values(8)
            turned_queries(early_bank[1], 3)
            values(9)
            pe.wait_ge(v_used, len(v_pairs))
            pe.wait_ge(c_in, 16 * 4)

            def turn_two(bank, rows):
                for t in range(TT):
                    for k in range(KC):
                        last = pe.transpose(bank[:, (t * KC + k) * P:(t * KC + k + 1) * P], rows[:, t, k * P:(k + 1) * P], id32[:, :])
                return last

            def times_two(bank, width, columns, weights):
                for t in range(TT):
                    for k in range(KC):
                        last = pe.matmul(bank[:, t * width:(t + 1) * width], columns[:, (t * KC + k) * P:(t * KC + k + 1) * P],
                                         weights[:, k, :], start=(k == 0), stop=(k == KC - 1))
                return last

            def body(s, p, kinds):
                n, tn, v, m = s + U_LEAD, s + T_LEAD, s - PV_LAG, s - O_LAG

                def scores(s, p, c):
                    if not isinstance(s, int) or 5 * s + c >= 2:
                        pe.wait_ge(exp_done, 5 * s + (c - 1))
                    for half in range(2):
                        for hl in range(2):
                            last = pe.matmul(bankS[(p + c) % 2][:, half * 512:half * 512 + 512],
                                             KB[:, ds(s, 1), hl, c * P:(c + 1) * P].rearrange("p o k -> p (o k)"),
                                             qT[:, ds((s // 4) % 2, 1), ds(s % 4, 1), half * 512:half * 512 + 512].rearrange("p a b t -> p (a b t)"),
                                             start=(hl == 0), stop=(hl == 1))
                    last.then_inc(s_ready, 1)

                def pv(qts):
                    for qt in qts:
                        bank = qt // 4
                        if qt == 0 and isinstance(v, int) and v == 0:
                            pe.wait_ge(v_used, len(v_pairs))
                            pe.wait_ge(v_ones, 1)
                        if qt == 0:
                            pe.wait_ge(exp_done, 5 * v + 5)
                        if qt % 4 == 0 and (not isinstance(v, int) or v >= 1):
                            pe.wait_ge(pv_norm, 2 * v + (bank - 1))
                        for c in range(W):
                            last = pe.matmul(bankO[bank][:, (qt % 4) * GH * VC:(qt % 4 + 1) * GH * VC],
                                             Pb[:, 1 - p, c, qt * P:(qt + 1) * P],
                                             VB[:, ds(v, 1), c, :].rearrange("p o k -> p (o k)"), start=(c == 0), stop=(c == W - 1))
                        if qt % 4 == 3:
                            last.then_inc(pv_ready, 1)

                if "o" in kinds:
                    pe.wait_ge(os_ld[p], 8 * (m - p) + 16)
                    if not isinstance(m, int) or m >= 1:
                        pe.wait_ge(o_done, m)
                    turn_two(bankR, OS[:, p]).then_inc(ot_ready, 1)
                if "p" in kinds:
                    scores(s - 1, 1 - p, W - 1)
                if "s" in kinds:
                    pe.wait_ge(q_done, s + T_LEAD if "t" in kinds else STEPS)
                    if isinstance(s, int) and s == 0:
                        pe.wait_ge(kb_dve, 4)
                        pe.wait_ge(kb_act, 4)
                        pe.wait_ge(kb_pad, 1)
                    scores(s, p, 0)
                if "t" in kinds:
                    turned_queries(bankQ[:, :], tn)
                if "o" in kinds:
                    pe.wait_ge(ot_sb, m + 1)
                    times_two(bankR, D, OT, wp_sb).then_inc(y_ready, 1)
                if "p" in kinds:
                    pv((0, 1))
                if "s" in kinds:
                    scores(s, p, 1)
                if "u" in kinds:
                    pe.wait_ge(x_ld[1 - p], 8 * (n - EARLY - p) + 16)
                    pe.wait_ge(q_done, n)
                    for t in range(TT):
                        for k in range(KC):
                            last = pe.matmul(bankQ[:, t * D:(t + 1) * D], x_in[:, 1 - p, k, t * P:(t + 1) * P], wq_sb[:, k, :],
                                             start=(k == 0), stop=(k == KC - 1))
                    last.then_inc(u_ready, 1)
                if "p" in kinds:
                    pv((2, 3))
                if "s" in kinds:
                    scores(s, p, 2)
                if "o" in kinds:
                    pe.wait_ge(x2_ready, m + 1)
                    turn_two(bankR, X2[:, p]).then_inc(x2t_ready, 1)
                if "p" in kinds:
                    pv((4, 5))
                if "s" in kinds:
                    scores(s, p, 3)
                if "o" in kinds:
                    pe.wait_ge(x2t_sb, m + 1)
                    times_two(bankR, E, X2T[:, p], wr_sb).then_inc(lg_ready, 1)
                if "p" in kinds:
                    pv((6, 7))
            segments(pe, body)

            pe.wait_ge(exp_done, W * STEPS)
            pe.wait_ge(q_done, STEPS)
            pe.wait_ge(pv_norm, 2 * STEPS)
            for k, m in enumerate(late):
                turn_two(late_bank[k], Oat[:, (2 * m) % 16:(2 * m) % 16 + TT]).then_inc(l_ot, 1)
            for k, m in enumerate(late):
                pe.wait_ge(l_os, k + 1)
                times_two(late_bank[k], D, late_ot[k], wp_sb).then_inc(l_y, 1)
            for k, m in enumerate(late):
                pe.wait_ge(l_x2, k + 1)
                turn_two(late_bank[k], XR[:, 2 * m:2 * m + TT]).then_inc(l_xt, 1)
                if k >= 1:
                    pe.wait_ge(l_xs, k)
                    times_two(late_bank[k - 1], E, late_x2t[k - 1], wr_sb).then_inc(l_lg, 1)
            pe.wait_ge(l_xs, len(late))
            times_two(late_bank[-1], E, late_x2t[-1], wr_sb).then_inc(l_lg, 1)

            pe.wait_ge(r_in, 16 * 6)
            pe.wait_ge(r_tot, 1)
            pe.matmul(bankQ[:, 0:E], tri, small[:, 0, 0:E], start=True, stop=True)
            pe.matmul(bankQ[:, E:2 * E], ones, small[:, 0, 0:E], start=True, stop=True).then_inc(r_sum, 1)

            def expert(tile):
                return pe.value_load(etile[0:1, ds(tile, 1)], min_val=0, max_val=E - 1)

            def transposes(a, h):
                pe.wait_ge(f_ld["e"][h], 16 * a + 16)
                for t in range(2):
                    for k in range(KC):
                        last = pe.transpose(bankO[h][:, (t * KC + k) * P:(t * KC + k + 1) * P], x_row[:, 2 * h + t, k * P:(k + 1) * P], id32[:, :])
                last.then_inc(f_xt["e"], 1)

            def ffn(kind, tiles):
                def four(a):
                    def up(k, e_):
                        if k % 2 == 0:
                            if kind == "e":
                                pe.wait_ge(f_xc["e"], 2 * a + (k // 2 + 1))
                            else:
                                pe.wait_ge(f_ld["s"][k // 2], 16 * a + 16)
                        for c in range(KC):
                            rhs = wgu_sb[:, c, ds(e_, 1), :].rearrange("p o f -> p (o f)") if kind == "e" else wgus_sb[:, c, :]
                            last = pe.matmul(gate_bank(k)[:, 0:2 * F], x_col[:, k, c * P:(c + 1) * P], rhs, start=(c == 0), stop=(c == KC - 1))
                        last.then_inc(f_gu[kind], 1)

                    def turn(k):
                        pe.wait_ge(f_h[kind], 4 * a + (k + 1))
                        for c in range(FC):
                            last = pe.transpose((bankQ, bankR)[k % 2][0:FP, c * P:(c + 1) * P], h_in[:, k % 2, c * FP:(c + 1) * FP], id32[:, :])
                        last.then_inc(f_ht[kind], 1)

                    def down(k, e_):
                        pe.wait_ge(f_hc[kind], 4 * a + (k + 1))
                        if k >= 2 or not isinstance(a, int) or a >= 1:
                            pe.wait_ge(f_yd[kind], 4 * a + (k - 1))
                        for c in range(FC):
                            rhs = wd_sb[0:FP, c, ds(e_, 1), :].rearrange("p o d -> p (o d)") if kind == "e" else wds_sb[0:FP, c, :]
                            last = pe.matmul(down_bank(k), h_col[0:FP, k, c * P:(c + 1) * P], rhs,
                                             start=(c == 0), stop=(c == FC - 1))
                        last.then_inc(f_y[kind], 1)

                    e_ = [None] * 4
                    if kind == "e":
                        e_[0] = expert(4 * a)
                    for k in range(4):
                        up(k, e_[k])
                        if kind == "e" and k < 3:
                            e_[k + 1] = expert(4 * a + (k + 1))
                        if k >= 1:
                            turn(k - 1)
                        if k >= 2:
                            down(k - 2, e_[k - 2])
                    if kind == "e" and more(a, tiles):
                        transposes(a + 1, 0)
                    turn(3)
                    down(2, e_[2])
                    if kind == "e" and more(a, tiles):
                        transposes(a + 1, 1)
                    down(3, e_[3])
                if kind == "e":
                    transposes(0, 0)
                    transposes(0, 1)
                quads(pe, tiles, four)
            pe.wait_ge(ws_in, 16 * 2)
            ffn("s", TILES)
            pe.wait_ge(w_in, 16 * (KC + FC))
            pe.wait_ge(routed, 1)
            ffn("e", SLOTS)

        @block.vector
        def _(dve):
            link_n = [0]

            def link(ins):
                link_n[0] += 1
                ins.then_inc(pre, 1)
                dve.wait_ge(pre, link_n[0])

            dve.wait_ge(kv_in, 16 * 2)
            v = wkv_sb[:, :, 0:D].rearrange("p k (h d) -> p k h d", d=HD)
            link(dve.tensor_reduce(hmean[:, :, 0, :], v, AX, ALU.add))
            link(dve.tensor_scalar(hmean[:, :, 0, :], hmean[:, :, 0, :], 1.0 / HD, None, ALU.mult))
            for k in range(KC):
                last = dve.tensor_tensor(v[:, k], v[:, k], hmean[:, k, 0, :].unsqueeze(2).to_broadcast([P, H, HD]), ALU.subtract)
            last.then_inc(w_h, 1)
            dve.wait_ge(wq_c, 1)
            v = bankQ[:, :].rearrange("p (k h d) -> p k h d", k=KC, d=HD)
            link(dve.tensor_reduce(hmean[:, :, 1, :], v, AX, ALU.add))
            link(dve.tensor_scalar(hmean[:, :, 1, :], hmean[:, :, 1, :], 1.0 / HD, None, ALU.mult))
            for k in range(KC):
                last = dve.tensor_tensor(wq_sb[:, k, :].rearrange("p (h d) -> p h d", d=HD), v[:, k],
                                         hmean[:, k, 1, :].unsqueeze(2).to_broadcast([P, H, HD]), ALU.subtract)
            last.then_inc(w_h, 1)

            def values(i):
                b, c = v_pairs[i]
                dve.wait_ge(v_rd, i + 1)
                dve.tensor_tensor(VB[:, b * G:(b + 2) * G, c, :].rearrange("p s (j d) -> p s j d", d=VC)[:, :, :, 0:HD],
                                  value_bank[i % 3][:, :].rearrange("p (s j d) -> p s j d", s=2 * G, j=GH),
                                  msk[:, c, :].unsqueeze(1).unsqueeze(3).to_broadcast([P, 2 * G, GH, HD]), ALU.mult).then_inc(v_used, 1)

            def spread(i):
                hl, g = halves[i]
                dve.wait_ge(kt_rd, i + 1)
                for j in range(GH):
                    last = dve.tensor_scalar(KB[:, :, hl, j * M:(j + 1) * M].rearrange("p (b g) m -> p b g m", g=G)[:, :, g, :],
                                             turn_bank[i % 3].bitcast(F16)[:, 0:B * M].rearrange("p (b m) -> p b m", b=B),
                                             own_sb[:, j:j + 1], None, ALU.mult)
                last.then_inc(kb_dve, 1)

            def spreads(n):
                dve.wait_ge(sq_ready, n + 1)
                link(dve.tensor_reduce(e_ss[:, n % 2], e_sq[:, n % 2].rearrange("p (h d) -> p h d", d=HD), AX, ALU.add))
                for t in range(TT):
                    last = dve.tensor_scalar(e_ss[:, n % 2, t * H:(t + 1) * H], e_ss[:, n % 2, t * H:(t + 1) * H], 1.0 / HD,
                                             e_eps[:, TT * n + t:TT * n + t + 1], ALU.mult, ALU.add)
                last.then_inc(qv_ready, 1)

            nq_h = nq[:, :, :, :].rearrange("p t g (j d) -> p (t g j) d", d=HD)
            nq_g = nq[:, :, :, :].rearrange("p t g k -> p (t g) k")
            each = lambda a, r: a.unsqueeze(1).to_broadcast([P, r, HD])

            def halved(n):
                if not isinstance(n, int) or n >= 1:
                    dve.wait_ge(qt_ready, n)
                hi, lo = (qs[:, :, :, l, :].rearrange("p t g k -> p (t g) k") for l in range(2))
                dve.tensor_copy(hi, nq_g).then_inc(q_hi, 1)
                dve.wait_ge(q_hi, n + 1)
                dve.tensor_tensor(lo, nq_g, hi, ALU.subtract).then_inc(qs_ready, 1)

            def queries(n):
                dve.wait_ge(qr_ready, n + 1)
                if n >= 1:
                    dve.wait_ge(qs_ready, n)
                link(dve.tensor_tensor(nq_h, early_bank[n % 2].rearrange("p (h d) -> p h d", d=HD),
                                       e_r[:, n % 2].unsqueeze(2).to_broadcast([P, TT * H, HD]), ALU.mult))
                link(dve.tensor_tensor(nq_h, nq_h, each(gb[:, 0, :], TT * H), ALU.mult))
                link(dve.tensor_tensor(nq_h, nq_h, each(gb[:, 1, :], TT * H), ALU.add))
                halved(n)

            dve.wait_ge(g_in, 16 * 5)
            dve.wait_ge(k_sq, 2)
            link(dve.tensor_reduce(kss, ktmp, AX, ALU.add))
            dve.tensor_scalar(kss, kss, 1.0 / HD, EPS, ALU.mult, ALU.add).then_inc(k_ss, 1)
            dve.tensor_scalar(gcoef[:, :, :], gb[:, :, :], SCALE, None, ALU.mult)
            dve.wait_ge(k_r, 1)
            dve.tensor_tensor(khat[:, 0:4 * H], key_bank[0].rearrange("p (r d) -> p r d", d=HD),
                              kr[:, 0:4 * H].unsqueeze(2).to_broadcast([P, 4 * H, HD]), ALU.mult)
            dve.tensor_tensor(khat[:, 4 * H:], key_bank[1].rearrange("p (r d) -> p r d", d=HD),
                              kr[:, 4 * H:].unsqueeze(2).to_broadcast([P, H, HD]), ALU.mult).then_inc(k_norm, 1)
            dve.wait_ge(k_norm, 1)
            link(dve.tensor_tensor(khat, khat, each(gcoef[:, 0, :], KT * H), ALU.mult))
            dve.tensor_tensor(khat, khat, each(gcoef[:, 1, :], KT * H), ALU.add).then_inc(k_fin, 1)
            for b in range(-(-EARLY * TT // 8)):
                dve.wait_ge(x_rows[b], 16)
            for t in range(EARLY * TT):
                last = dve.bn_stats(e_stat[:, t, :], X1[:, t, :])
            link(last)
            for t in range(EARLY * TT):
                last = dve.bn_aggr(e_mv[:, t, :], e_stat[:, t, :])
            link(last)
            link(dve.tensor_scalar(e_eps, e_mv[:, :, 1], EPS, EPS, ALU.add, ALU.mult))
            spreads(0)
            spreads(1)
            values(0)
            values(1)
            spread(0)
            values(2)
            spread(2)
            queries(0)
            queries(1)
            dve.wait_ge(k_sq, 3)
            link(dve.tensor_reduce(kss, ktmp, AX, ALU.add))
            link(dve.tensor_tensor(ktmp[:, 0:2, :], gb[:, :, :], gb[:, :, :], ALU.mult))
            dve.tensor_reduce(guard[:, 0:1], ktmp[:, 0, :], AX, ALU.max)
            dve.tensor_reduce(guard[:, 1:2], ktmp[:, 1, :], AX, ALU.add)
            link(dve.tensor_reduce(guard[:, 2:3], kss, AX, ALU.max))
            dve.tensor_scalar(guard[:, 0:3], guard[:, 0:3], 1e-30, None, ALU.add).then_inc(gu_in, 1)
            values(3)
            values(4)
            spreads(2)
            values(5)
            queries(2)
            spread(4)
            dve.wait_ge(gu_rt, 1)
            link(dve.scalar_tensor_tensor(out=guard[:, 0:1], in0=guard[:, 6:7], scalar=float(HD) ** 0.5, in1=guard[:, 7:8],
                                          op0=ALU.mult, op1=ALU.add))
            dve.tensor_tensor(guard[:, 1:2], guard[:, 0:1], guard[:, 8:9], ALU.mult).then_inc(k_u, 1)
            spread(6)
            spreads(3)
            values(6)
            queries(3)
            values(7)
            values(8)
            dve.wait_ge(u_all, 1)
            link(dve.tensor_scalar(guard[:, 2:3], guard[:, 3:4], -1.0, GUARD, ALU.mult, ALU.add))
            dve.tensor_scalar(shift, guard[:, 2:3], 0.0, None, ALU.min).then_inc(guarded, 1)
            spreads(4)
            values(9)
            queries(4)
            dve.tensor_copy(VB[:, :, :, :].rearrange("p s c (j d) -> p s c j d", d=VC)[:, :, :, :, HD],
                            msk[:, :, :].unsqueeze(1).to_broadcast([P, STEPS, W, GH])).then_inc(v_ones, 1)
            for b in range(B):
                dve.wait_ge(x_rows[b], 16)
            dve.wait_ge(c_in, 16 * 4)

            def body(s, p, kinds):
                n, v, m = s + U_LEAD, s - PV_LAG, s - O_LAG
                QL, OL = 7, 4

                def q(k, ins):
                    ins.then_inc(dve_q, 1)
                    dve.wait_ge(dve_q, QL * (n - EARLY) + k)

                def o(k, ins):
                    ins.then_inc(dve_o, 1)
                    dve.wait_ge(dve_o, OL * m + k)

                def norm(bank):
                    if "o" in kinds and bank == 0:
                        dve.wait_ge(os_ld[p], 8 * (m - p) + 16)
                    dve.wait_ge(pv_ready, 2 * v + (bank + 1))
                    src = bankO[bank][:, 0:4 * GH * VC].rearrange("p (t j d) -> p t j d", t=4, d=VC)
                    r = rec[:, bank, :].rearrange("p (t j) -> p t j", t=4)
                    dve.reciprocal(r, src[:, :, :, HD]).then_inc(dve_p, 1)
                    dve.wait_ge(dve_p, 2 * v + (bank + 1))
                    aside(dve)
                    dst = Oat[:, ds(8 * ((v // 4) % 2) + 4 * bank, 4), ds(GW * (v % 4), GW)].rearrange("p t (j d) -> p t j d", d=HD)
                    dve.tensor_tensor(dst, src[:, :, :, 0:HD], r.unsqueeze(3).to_broadcast([P, 4, GH, HD]), ALU.mult).then_inc(pv_norm, 1)

                if "u" in kinds:
                    aside(dve)
                    for t in range(TT):
                        last = dve.bn_stats(xstat[:, t, :], X1[:, ds(2 * n + t, 1), :].rearrange("p o d -> p (o d)"))
                    q(1, last)
                    aside(dve)
                    for t in range(TT):
                        last = dve.bn_aggr(xmv[:, t, :], xstat[:, t, :])
                    q(2, last)
                    q(3, dve.tensor_scalar(qeps[:, :], xmv[:, :, 1], EPS, EPS, ALU.add, ALU.mult))
                if "o" in kinds:
                    dve.wait_ge(y_ready, m + 1)
                    aside(dve)
                    xr = X1[:, ds(2 * m, TT), :]
                    o(1, dve.tensor_tensor(xr, xr, bankR[:, :].rearrange("p (t d) -> p t d", t=TT), ALU.add))
                    o(2, dve.tensor_tensor(xr, xr, bp_sb[:, :].unsqueeze(1).to_broadcast([P, TT, D]), ALU.add))
                    aside(dve)
                    for t in range(TT):
                        last = dve.bn_stats(ostat[:, t, :], X1[:, ds(2 * m + t, 1), :].rearrange("p o d -> p (o d)"))
                    o(3, last)
                    aside(dve)
                    for t in range(TT):
                        last = dve.bn_aggr(omv[:, t, :], ostat[:, t, :])
                    o(4, last)
                    dve.tensor_scalar(omv[:, :, 1], omv[:, :, 1], EPS, None, ALU.add).then_inc(ov_ready, 1)
                    dve.wait_ge(or_ready, m + 1)
                    for t in range(TT):
                        last = dve.tensor_scalar(X2[:, p, t, :], X1[:, ds(2 * m + t, 1), :].rearrange("p o d -> p (o d)"),
                                                 omv[:, t, 0:1], orr[:, t:t + 1], ALU.subtract, ALU.mult)
                    last.then_inc(x2_ready, 1)
                if "u" in kinds:
                    dve.wait_ge(sq_ready, n + 1)
                    q(4, dve.tensor_reduce(qss[:, :], sq[:, :].rearrange("p (h d) -> p h d", d=HD), AX, ALU.add))
                    for t in range(TT):
                        last = dve.tensor_scalar(qss[:, t * H:(t + 1) * H], qss[:, t * H:(t + 1) * H], 1.0 / HD,
                                                 qeps[:, t:t + 1], ALU.mult, ALU.add)
                    last.then_inc(qv_ready, 1)
                if "p" in kinds:
                    norm(0)
                if "u" in kinds:
                    dve.wait_ge(qr_ready, n + 1)
                    q(5, dve.tensor_tensor(nq_h, bankQ[:, :].rearrange("p (h d) -> p h d", d=HD),
                                           qr[:, :].unsqueeze(2).to_broadcast([P, TT * H, HD]), ALU.mult))
                    q(6, dve.tensor_tensor(nq_h, nq_h, each(gb[:, 0, :], TT * H), ALU.mult))
                    q(7, dve.tensor_tensor(nq_h, nq_h, each(gb[:, 1, :], TT * H), ALU.add))
                    halved(n)
                if "o" in kinds:
                    dve.wait_ge(lg_ready, m + 1)
                    dve.tensor_copy(LG[:, ds(2 * m, TT), :], bankR[:, 0:TT * E].rearrange("p (t e) -> p t e", e=E)).then_inc(o_done, 1)
                if "p" in kinds:
                    norm(1)
            segments(dve, body)

            def moments(k, m):
                dve.wait_ge(l_y, k + 1)
                dve.wait_ge(l_bias, 1)
                xr = X1[:, 2 * m:2 * m + TT]
                link(dve.tensor_tensor(xr, xr, late_bank[k].rearrange("p (t d) -> p t d", t=TT), ALU.add))
                for t in range(TT):
                    last = dve.bn_stats(ostat[:, t, :], X1[:, 2 * m + t])
                link(last)
                for t in range(TT):
                    last = dve.bn_aggr(late_mv[:, k, t, :], ostat[:, t, :])
                link(last)
                dve.tensor_scalar(late_mv[:, k, :, 1], late_mv[:, k, :, 1], EPS, None, ALU.add).then_inc(l_ov, 1)

            def rows_of(k, m):
                dve.wait_ge(l_or, k + 1)
                for t in range(TT):
                    last = dve.tensor_scalar(XR[:, 2 * m + t, 0:D], X1[:, 2 * m + t], late_mv[:, k, t, 0:1], late_r[:, k, t:t + 1],
                                             ALU.subtract, ALU.mult)
                last.then_inc(l_x2, 1)
            for k, m in enumerate(late):
                moments(k, m)
                if k >= 1:
                    rows_of(k - 1, m - 1)
            rows_of(len(late) - 1, STEPS - 1)
            for k, m in enumerate(late):
                dve.wait_ge(l_lg, k + 1)
                dve.tensor_copy(LG[:, 2 * m:2 * m + TT, :], late_bank[k][:, 0:TT * E].rearrange("p (t e) -> p t e", e=E)).then_inc(l_done, 1)

            dve.wait_ge(r_exp, 1)
            tile_of = lambda a: a.unsqueeze(2).to_broadcast([P, TILES, E])
            of_e = lambda a: a.unsqueeze(1).to_broadcast([P, TILES, E])
            link(dve.tensor_scalar(ex, ex, 1.0, None, ALU.add))
            link(dve.reciprocal(sc, ex))
            link(dve.tensor_tensor(sbias, sc, of_e(ebias), ALU.add))
            for k, oh in enumerate((oh1, oh2)):
                link(dve.tensor_reduce(small[:, 1], sbias, AX, ALU.max))
                link(dve.tensor_tensor(cand, sbias, tile_of(small[:, 1]), ALU.is_equal))
                link(dve.tensor_tensor(cand, cand, of_e(rev), ALU.mult))
                link(dve.tensor_reduce(small[:, 2 + k], cand, AX, ALU.max))
                link(dve.tensor_tensor(oh, cand, tile_of(small[:, 2 + k]), ALU.is_equal))
                link(dve.tensor_tensor(cand, oh, sc, ALU.mult))
                link(dve.tensor_reduce(small[:, 4 + k], cand, AX, ALU.add))
                if k == 0:
                    link(dve.scalar_tensor_tensor(out=sbias, in0=oh, scalar=-BIG, in1=sbias, op0=ALU.mult, op1=ALU.add))
            link(dve.tensor_tensor(cum_a, oh1, oh2, ALU.add))
            a_, b_ = cum_a, cum_b
            step_ = 1
            while step_ < TILES:
                dve.tensor_copy(b_[:, 0:step_], a_[:, 0:step_])
                link(dve.tensor_tensor(b_[:, step_:], a_[:, step_:], a_[:, 0:TILES - step_], ALU.add))
                a_, b_ = b_, a_
                step_ *= 2
            dve.tensor_copy(small[:, 0, 0:E], a_[:, TILES - 1, :]).then_inc(r_tot, 1)
            link(dve.tensor_tensor(slot, a_, oh1, ALU.subtract))
            link(dve.tensor_tensor(slot, slot, oh2, ALU.subtract))
            link(dve.tensor_tensor(small[:, 6], small[:, 4], small[:, 5], ALU.add))
            link(dve.tensor_scalar(small[:, 6], small[:, 6], 1e-20, None, ALU.add))
            link(dve.reciprocal(small[:, 7], small[:, 6]))
            for k in range(2):
                last = dve.tensor_tensor(wts[:, k], small[:, 4 + k], small[:, 7], ALU.mult)
            link(last)
            dve.wait_ge(r_sum, 1)
            n_i = small[:, 9, 0:E].bitcast(I32)
            link(dve.tensor_scalar(n_i, bankQ[:, E:2 * E], float(P - 1), None, ALU.add))
            link(dve.tensor_scalar(n_i, n_i, 7, 7, ALU.arith_shift_right, ALU.logical_shift_left))
            link(dve.tensor_copy(small[:, 10, 0:E], n_i))
            a_, b_ = small[:, 10, 0:E], small[:, 11, 0:E]
            link(dve.tensor_copy(small[:, 12, 0:E], a_))
            for step_ in (1, 2, 4):
                dve.tensor_copy(b_[:, 0:step_], a_[:, 0:step_])
                link(dve.tensor_tensor(b_[:, step_:], a_[:, step_:], a_[:, 0:E - step_], ALU.add))
                a_, b_ = b_, a_
            ends = a_
            link(dve.tensor_tensor(small[:, 12, 0:E], ends, small[:, 12, 0:E], ALU.subtract))
            link(dve.tensor_tensor(small[:, 12, 0:E], small[:, 12, 0:E], bankQ[:, 0:E], ALU.add))
            link(dve.tensor_tensor(slot, slot, of_e(small[:, 12, 0:E]), ALU.add))
            for k, oh in enumerate((oh1, oh2)):
                link(dve.tensor_tensor(cand, slot, oh, ALU.mult))
                link(dve.tensor_reduce(pos_f[:, k], cand, AX, ALU.add))
            link(dve.tensor_copy(pos, pos_f))
            link(dve.tensor_tensor(wide, tstart.unsqueeze(2).to_broadcast([P, SLOTS, E]), ends.unsqueeze(1).to_broadcast([P, SLOTS, E]), ALU.is_ge))
            link(dve.tensor_reduce(etf, wide, AX, ALU.add))
            link(dve.tensor_scalar(etf, etf, float(E - 1), None, ALU.min))
            link(dve.tensor_copy(etile, etf))
            link(dve.tensor_copy(XR[:, :, D], tokens))
            dve.tensor_scalar(XR[:, :, D + 1], small[:, 2], -1.0, float(E), ALU.mult, ALU.add).then_inc(routed, 1)

            def places(a):
                for h in range(2):
                    dve.wait_ge(f_ld["e"][h], 16 * a + 16)
                    aside(dve)
                    dve.tensor_tensor(dest_f[:, h], x_row[:, 2 * h:2 * h + 2, D + 1], etf[:, ds(4 * a + 2 * h, 2)], ALU.not_equal).then_inc(e_chain, 1)
                    dve.wait_ge(e_chain, 2 * a + (h + 1))
                    aside(dve)
                    dve.scalar_tensor_tensor(out=dest[:, ds(4 * a + 2 * h, 2)], in0=dest_f[:, h], scalar=float(B * N),
                                             in1=x_row[:, 2 * h:2 * h + 2, D], op0=ALU.mult, op1=ALU.add).then_inc(e_dst, 1)

            def ffn(kind, tiles):
                def four(a):
                    def inner(k):
                        dve.wait_ge(f_si[kind], 4 * a + (k + 1))
                        if k >= 2 or not isinstance(a, int) or a >= 1:
                            dve.wait_ge(f_ht[kind], 4 * a + (k - 1))
                        dve.tensor_tensor(h_in[:, k % 2], act_g[:, k], gate_bank(k)[:, F:2 * F], ALU.mult).then_inc(f_h[kind], 1)

                    def columns(k):
                        dve.wait_ge(f_ht[kind], 4 * a + (k + 1))
                        aside(dve)
                        dve.tensor_copy(h_col[0:FP, k], (bankQ, bankR)[k % 2][0:FP, 0:D]).then_inc(f_hc[kind], 1)

                    def result(k):
                        dve.wait_ge(f_y[kind], 4 * a + (k + 1))
                        if kind == "s":
                            aside(dve)
                            xt = X1[:, ds(4 * a + k, 1), :].rearrange("p o d -> p (o d)")
                            dve.tensor_tensor(xt, xt, down_bank(k), ALU.add).then_inc(f_yd["s"], 1)
                        else:
                            if not isinstance(a, int) or a >= 1:
                                dve.wait_ge(y_st[k], 16 * a)
                            aside(dve)
                            dve.tensor_copy(y_out[:, k], down_bank(k)).then_inc(f_yd["e"], 1)

                    inner(0)
                    inner(1)
                    columns(0)
                    inner(2)
                    columns(1)
                    result(0)
                    inner(3)
                    columns(2)
                    result(1)
                    columns(3)
                    result(2)
                    if kind == "e" and more(a, tiles):
                        places(a + 1)
                    result(3)
                if kind == "e":
                    places(0)
                quads(dve, tiles, four)
            ffn("s", TILES)
            ffn("e", SLOTS)

            for c in range(TILES // CT):
                dve.wait_ge(c_ld[c % CS], 32 * (c // CS + 1))
                for k in range(2):
                    for t in range(CT):
                        tile = c * CT + t
                        last = dve.scalar_tensor_tensor(out=X1[:, tile, :], in0=ya[:, c % CS, k * CT + t], scalar=wts[:, k, tile:tile + 1],
                                                        in1=X1[:, tile, :], op0=ALU.mult, op1=ALU.add)
                    if k == 0:
                        last.then_inc(c_half, 1)
                        dve.wait_ge(c_half, c + 1)
                last.then_inc(c_sum, 1)


_OUT = (B, N, D)


def kernel(**inputs):
    import concourse.bacc as _bacc
    from concourse.bass_utils import run_bass_kernel_spmd as _run

    g = {k: np.asarray(v) for k, v in inputs.items()}
    a = {}
    a["x"] = g["x"].reshape(B * N, D)
    a["xT"] = np.ascontiguousarray(a["x"].T)
    c = g["ctx_1024"].transpose(2, 0, 1)
    a["ctx2T"] = np.ascontiguousarray(np.concatenate([c, c], axis=2))
    c = c.reshape(D, B * M)
    a["keysT"] = np.ascontiguousarray(np.concatenate([c, c[:, :KT * P - B * M]], axis=1))
    a["wq"] = np.ascontiguousarray(g["L0_xattn_Wq"].T)
    a["wkv"] = np.ascontiguousarray(np.concatenate([g["L0_xattn_Wk"].T, g["L0_xattn_Wv"].T], axis=1))
    a["wp"] = np.ascontiguousarray(g["L0_xattn_Wp"].T)
    a["bp"] = g["L0_xattn_bp"]
    a["wr"] = g["L0_ffn_W_gate_router"]
    a["ln_g"] = g["L0_xattn_ln_g"]
    a["ln_b"] = g["L0_xattn_ln_b"]
    a["centre"] = (np.eye(D) - 1.0 / D).astype(np.float32)
    a["ident"] = np.eye(P, dtype=np.float32)
    a["ident16"] = np.eye(P, dtype=np.float16)
    head = (np.arange(W)[None, :] * P + np.arange(P)[:, None]) // M
    a["mask"] = (head[:, :, None] == np.arange(GH)).astype(np.float32)
    own = (np.arange(P) // HD) % GH
    a["own"] = (own[:, None] == np.arange(GH)).astype(np.float32)
    cat = np.concatenate([g["L0_ffn_Wg"], g["L0_ffn_Wu"]], axis=2)
    a["wgu"] = np.ascontiguousarray(cat.transpose(1, 0, 2))
    a["wd"] = np.ascontiguousarray(g["L0_ffn_Wd"].transpose(1, 0, 2))
    a["wgu_s"] = np.concatenate([g["L0_ffn_Wg_s"], g["L0_ffn_Wu_s"]], axis=1)
    a["wd_s"] = g["L0_ffn_Wd_s"]
    a["e_bias"] = g["L0_ffn_expert_bias"]
    row = np.arange(P)
    a["tri_c"] = np.stack([row[:, None] < row[None, :], np.ones((P, P), bool)]).astype(np.float32)
    a["rev_c"] = np.tile(np.arange(E, 0, -1, dtype=np.float32), (P, 1))
    a["tok_c"] = (np.arange(TILES)[None, :] * P + row[:, None]).astype(np.float32)
    a["tst_c"] = np.tile(np.arange(SLOTS, dtype=np.float32) * P, (P, 1))
    a["fill_c"] = np.zeros((P, ROW), np.float32)
    a["fill_c"][:, D] = NOWHERE
    nc = _bacc.Bacc("TRN2", target_bir_lowering=False, num_devices=1)
    args = {n: nc.dram_tensor(f"in_{n}", v.shape, mybir.dt.from_np(v.dtype), kind="ExternalInput").ap() for n, v in a.items()}
    out = nc.dram_tensor("out", (B * N, D), F32, kind="ExternalOutput").ap()
    scratch = {n: nc.dram_tensor(n, shape, F32, kind="Internal").ap() for n, shape in (
        ("x2_rows", (B * N, D)), ("x2_cols", (STEPS, P, TT * D)), ("sorted_rows", (SLOTS, P, ROW)), ("y_rows", (2 * B * N, D)))}
    build(nc, **args, **scratch, out=out)
    r = _run(nc, [{f"in_{n}": v for n, v in a.items()}], core_ids=[0])
    return r.results[0]["out"].reshape(_OUT)
```
